# Optimizing a Trainium2 kernel written in Bass

```python
import numpy as np
import jax
import jax.numpy as jnp

def _softmax(x, axis=-1):
    return jax.nn.softmax(x, axis=axis)

def _gelu(x):
    return jax.nn.gelu(x, approximate=True)

def _silu(x):
    return jax.nn.silu(x)

def _sigmoid(x):
    return jax.nn.sigmoid(x)

def _layernorm(x, axis=-1, eps=1e-05):
    m = jnp.mean(x, axis=axis, keepdims=True)
    v = jnp.var(x, axis=axis, keepdims=True)
    return (x - m) / jnp.sqrt(v + eps)

def _scatter_add(tgt, idx, src, axis=0):
    return tgt.at[idx].add(src)

def _segment_sum(src, seg, n):
    return jax.ops.segment_sum(src, seg, n)
kernel_name = 'mk_xattn_ffn_d2_seqx_r8_4cc5ed'

def setup_inputs(seed: int=0):
    np.random.seed(seed)
    _w = jnp.asarray

    def _rec_inputs():
        import jax
        import jax.numpy as jnp
        _rk = jax.random.key(seed)
        x = -0.0002928 + 1 * jax.random.normal(jax.random.fold_in(_rk, 1), (32, 128, 128), jnp.float32)
        _lenS = 128 - jax.random.randint(jax.random.fold_in(_rk, 7), (32,), 0, max(1, 128 // 4) + 1, jnp.int32)
        _lenS2 = 128 - jax.random.randint(jax.random.fold_in(_rk, 8), (32,), 0, max(1, 128 // 4) + 1, jnp.int32)
        _ctx_1024P = jax.random.normal(jax.random.fold_in(_rk, 11), (32, 16, 128), jnp.float32)
        _ctx_1024c = jax.random.dirichlet(jax.random.fold_in(_rk, 511), 0.3 * jnp.ones((16,), jnp.float32), (32, 128))
        _ctx_1024t = jnp.einsum('bsk,bkd->bsd', _ctx_1024c, _ctx_1024P)
        _ctx_1024t = _ctx_1024t * jax.lax.rsqrt(jnp.mean(jnp.square(_ctx_1024t)) + 1e-12) * 0.953939
        ctx_1024 = -1.39393e-06 + 0.999914 * (_ctx_1024t + 0.3 * jax.random.normal(jax.random.fold_in(_rk, 611), (32, 128, 128), jnp.float32))
        _validS = jnp.arange(128)[None, :] < _lenS[:, None]
        _validS2 = jnp.arange(128)[None, :] < _lenS2[:, None]
        _causal = jnp.tril(jnp.ones((128, 128), dtype=bool))
        mask_BxSxS2_ik1 = jnp.where(jnp.broadcast_to(_validS2[:, None, :], (32, 128, 128)), 1, 0).astype(jnp.int32)
        return (x, ctx_1024, mask_BxSxS2_ik1)
    x, ctx_1024, mask_BxSxS2_ik1 = _rec_inputs()

    def _L0_xattn_setup():
        import jax, jax.numpy as jnp
        import numpy as np
        import math
        D_MODEL = 128
        N_HEADS = 16
        D_K = D_MODEL // N_HEADS
        ROPE_BASE = 10000.0

        def rope_cos_sin(seq_len, d_k, base=ROPE_BASE, dtype=jnp.float32):
            inv_freq = 1.0 / base ** (jnp.arange(0, d_k, 2, dtype=dtype) / d_k)
            pos = jnp.arange(seq_len, dtype=dtype)
            freqs = jnp.outer(pos, inv_freq)
            return (jnp.cos(freqs), jnp.sin(freqs))

        def apply_rope(x, cos, sin):
            x1 = x[..., 0::2]
            x2 = x[..., 1::2]
            c = cos[None, None]
            s = sin[None, None]
            r1 = x1 * c - x2 * s
            r2 = x1 * s + x2 * c
            return jnp.stack([r1, r2], axis=-1).reshape(x.shape)
        key = jax.random.key(seed)
        ks = jax.random.split(key, 7)
        B, T = (2, 256)
        scale = 1.0 / math.sqrt(D_MODEL)
        return {'query': jax.random.normal(ks[0], (B, T, D_MODEL), jnp.float32), 'key': jax.random.normal(ks[1], (B, T, D_MODEL), jnp.float32), 'value': jax.random.normal(ks[2], (B, T, D_MODEL), jnp.float32), 'Wq': jax.random.normal(ks[3], (D_MODEL, D_MODEL), jnp.float32) * scale, 'Wk': jax.random.normal(ks[4], (D_MODEL, D_MODEL), jnp.float32) * scale, 'Wv': jax.random.normal(ks[5], (D_MODEL, D_MODEL), jnp.float32) * scale, 'Wo': jax.random.normal(ks[6], (D_MODEL, D_MODEL), jnp.float32) * scale}
    _L0_xattn_all = _L0_xattn_setup()
    _L0_xattn_in = {k: v for k, v in _L0_xattn_all.items() if k in ('Wq', 'Wk', 'Wv', 'Wo')}
    del _L0_xattn_all

    def _L0_ffn_setup():
        import jax, jax.numpy as jnp
        import numpy as np
        EPS = 1e-05

        def _quantize(W):
            gamma = jnp.mean(jnp.abs(W))
            return jnp.clip(jnp.round(W / (gamma + EPS)), -1.0, 1.0)
        key = jax.random.key(seed)
        k_x, k_w1, k_b1, k_w2, k_b2 = jax.random.split(key, 5)
        n_embd = 128
        d_ff = 4 * n_embd
        B, S = (4, 512)
        bound1 = 1.0 / np.sqrt(n_embd)
        bound2 = 1.0 / np.sqrt(d_ff)
        x = jax.random.normal(k_x, (B, S, n_embd), dtype=jnp.float32)
        W1 = jax.random.uniform(k_w1, (d_ff, n_embd), jnp.float32, -bound1, bound1)
        b1 = jax.random.uniform(k_b1, (d_ff,), jnp.float32, -bound1, bound1)
        W2 = jax.random.uniform(k_w2, (n_embd, d_ff), jnp.float32, -bound2, bound2)
        b2 = jax.random.uniform(k_b2, (n_embd,), jnp.float32, -bound2, bound2)
        return {'x': x, 'W1': W1, 'b1': b1, 'W2': W2, 'b2': b2}
    _L0_ffn_all = _L0_ffn_setup()
    _L0_ffn_in = {k: v for k, v in _L0_ffn_all.items() if k in ('W1', 'b1', 'W2', 'b2')}
    del _L0_ffn_all

    def _L1_xattn_setup():
        import jax, jax.numpy as jnp
        import numpy as np
        E = 128
        HQ = 16
        HK = 4
        D = E // HQ
        G = HQ // HK
        KVE = D * HK
        B = 2
        N = 256
        LN_EPS = 1e-05

        def _xavier(k, fan_out, fan_in):
            std = np.sqrt(2.0 / (fan_in + fan_out)).astype(np.float32)
            return jax.random.normal(k, (fan_out, fan_in), jnp.float32) * std
        key = jax.random.key(seed)
        ks = jax.random.split(key, 8)
        return {'query': jax.random.normal(ks[0], (B, N, E), jnp.float32), 'key': jax.random.normal(ks[1], (B, N, E), jnp.float32), 'value': jax.random.normal(ks[2], (B, N, E), jnp.float32), 'adj': jax.random.randint(ks[3], (B, N, N), 0, 2, jnp.int32), 'Wq': _xavier(ks[4], E, E), 'bq': jnp.zeros((E,), jnp.float32), 'Wk': _xavier(ks[5], KVE, E), 'bk': jnp.zeros((KVE,), jnp.float32), 'Wv': _xavier(ks[6], KVE, E), 'bv': jnp.zeros((KVE,), jnp.float32), 'Wo': _xavier(ks[7], E, E), 'bo': jnp.zeros((E,), jnp.float32), 'ln_g': jnp.ones((E,), jnp.float32), 'ln_b': jnp.zeros((E,), jnp.float32)}
    _L1_xattn_all = _L1_xattn_setup()
    _L1_xattn_in = {k: v for k, v in _L1_xattn_all.items() if k in ('Wq', 'bq', 'Wk', 'bk', 'Wv', 'bv', 'Wo', 'bo', 'ln_g', 'ln_b')}
    del _L1_xattn_all

    def _L1_ffn_setup():
        import jax, jax.numpy as jnp
        import numpy as np
        NUM_EXPERTS = 8
        IN_FEATURES = 128
        HIDDEN_FEATURES = 512
        GATE_DIM = 16
        EPS = 0.0001
        key = jax.random.key(seed)
        ks = jax.random.split(key, 7)
        hidden_states = jax.random.normal(ks[0], (1, 256, IN_FEATURES), dtype=jnp.float32)
        wg_red = jax.random.normal(ks[1], (GATE_DIM, IN_FEATURES), dtype=jnp.float32) * 0.02
        wg = jax.random.normal(ks[2], (NUM_EXPERTS, GATE_DIM), dtype=jnp.float32)
        w1 = jax.random.uniform(ks[3], (NUM_EXPERTS, IN_FEATURES, HIDDEN_FEATURES), dtype=jnp.float32)
        b1 = jax.random.uniform(ks[4], (NUM_EXPERTS, HIDDEN_FEATURES), dtype=jnp.float32)
        w2 = jax.random.uniform(ks[5], (NUM_EXPERTS, HIDDEN_FEATURES, IN_FEATURES), dtype=jnp.float32)
        b2 = jax.random.uniform(ks[6], (NUM_EXPERTS, IN_FEATURES), dtype=jnp.float32)
        return {'hidden_states': hidden_states, 'wg_red': wg_red, 'wg': wg, 'w1': w1, 'b1': b1, 'w2': w2, 'b2': b2}
    _L1_ffn_all = _L1_ffn_setup()
    _L1_ffn_in = {k: v for k, v in _L1_ffn_all.items() if k in ('wg_red', 'wg', 'w1', 'b1', 'w2', 'b2')}
    del _L1_ffn_all
    return {'x': x, 'ctx_1024': ctx_1024, 'mask_BxSxS2_ik1': mask_BxSxS2_ik1, 'L0_xattn_Wq': _L0_xattn_in['Wq'], 'L0_xattn_Wk': _L0_xattn_in['Wk'], 'L0_xattn_Wv': _L0_xattn_in['Wv'], 'L0_xattn_Wo': _L0_xattn_in['Wo'], 'L0_ffn_W1': _L0_ffn_in['W1'], 'L0_ffn_b1': _L0_ffn_in['b1'], 'L0_ffn_W2': _L0_ffn_in['W2'], 'L0_ffn_b2': _L0_ffn_in['b2'], 'L1_xattn_Wq': _L1_xattn_in['Wq'], 'L1_xattn_bq': _L1_xattn_in['bq'], 'L1_xattn_Wk': _L1_xattn_in['Wk'], 'L1_xattn_bk': _L1_xattn_in['bk'], 'L1_xattn_Wv': _L1_xattn_in['Wv'], 'L1_xattn_bv': _L1_xattn_in['bv'], 'L1_xattn_Wo': _L1_xattn_in['Wo'], 'L1_xattn_bo': _L1_xattn_in['bo'], 'L1_xattn_ln_g': _L1_xattn_in['ln_g'], 'L1_xattn_ln_b': _L1_xattn_in['ln_b'], 'L1_ffn_wg_red': _L1_ffn_in['wg_red'], 'L1_ffn_wg': _L1_ffn_in['wg'], 'L1_ffn_w1': _L1_ffn_in['w1'], 'L1_ffn_b1': _L1_ffn_in['b1'], 'L1_ffn_w2': _L1_ffn_in['w2'], 'L1_ffn_b2': _L1_ffn_in['b2']}

def reference(x, ctx_1024, mask_BxSxS2_ik1, L0_xattn_Wq, L0_xattn_Wk, L0_xattn_Wv, L0_xattn_Wo, L0_ffn_W1, L0_ffn_b1, L0_ffn_W2, L0_ffn_b2, L1_xattn_Wq, L1_xattn_bq, L1_xattn_Wk, L1_xattn_bk, L1_xattn_Wv, L1_xattn_bv, L1_xattn_Wo, L1_xattn_bo, L1_xattn_ln_g, L1_xattn_ln_b, L1_ffn_wg_red, L1_ffn_wg, L1_ffn_w1, L1_ffn_b1, L1_ffn_w2, L1_ffn_b2):
    import jax
    import jax.numpy as jnp

    def _L0_xattn_ref(query, key, value, Wq, Wk, Wv, Wo):
        import jax, jax.numpy as jnp
        import numpy as np
        import math
        D_MODEL = 128
        N_HEADS = 16
        D_K = D_MODEL // N_HEADS
        ROPE_BASE = 10000.0

        def rope_cos_sin(seq_len, d_k, base=ROPE_BASE, dtype=jnp.float32):
            inv_freq = 1.0 / base ** (jnp.arange(0, d_k, 2, dtype=dtype) / d_k)
            pos = jnp.arange(seq_len, dtype=dtype)
            freqs = jnp.outer(pos, inv_freq)
            return (jnp.cos(freqs), jnp.sin(freqs))

        def apply_rope(x, cos, sin):
            x1 = x[..., 0::2]
            x2 = x[..., 1::2]
            c = cos[None, None]
            s = sin[None, None]
            r1 = x1 * c - x2 * s
            r2 = x1 * s + x2 * c
            return jnp.stack([r1, r2], axis=-1).reshape(x.shape)
        B, Tq, _ = query.shape
        Tk = key.shape[1]
        Q = (query @ Wq.T).reshape(B, Tq, N_HEADS, D_K).transpose(0, 2, 1, 3)
        K = (key @ Wk.T).reshape(B, Tk, N_HEADS, D_K).transpose(0, 2, 1, 3)
        V = (value @ Wv.T).reshape(B, Tk, N_HEADS, D_K).transpose(0, 2, 1, 3)
        cos_q, sin_q = rope_cos_sin(Tq, D_K)
        cos_k, sin_k = rope_cos_sin(Tk, D_K)
        Q = apply_rope(Q, cos_q, sin_q)
        K = apply_rope(K, cos_k, sin_k)
        scores = jnp.einsum('bhqd,bhkd->bhqk', Q, K) / math.sqrt(D_K)
        attn = jax.nn.softmax(scores, axis=-1)
        out = jnp.einsum('bhqk,bhkd->bhqd', attn, V)
        out = out.transpose(0, 2, 1, 3).reshape(B, Tq, D_MODEL)
        return out @ Wo.T

    def _L0_ffn_ref(x, W1, b1, W2, b2):
        import jax, jax.numpy as jnp
        import numpy as np
        EPS = 1e-05

        def _quantize(W):
            gamma = jnp.mean(jnp.abs(W))
            return jnp.clip(jnp.round(W / (gamma + EPS)), -1.0, 1.0)
        Wq1 = _quantize(W1)
        Wq2 = _quantize(W2)
        h = jax.nn.relu(jnp.einsum('bsd,fd->bsf', x, Wq1) + b1)
        out = jnp.einsum('bsf,df->bsd', h, Wq2) + b2
        return out

    def _L1_xattn_ref(query, key, value, adj, Wq, bq, Wk, bk, Wv, bv, Wo, bo, ln_g, ln_b):
        import jax, jax.numpy as jnp
        import numpy as np
        E = 128
        HQ = 16
        HK = 4
        D = E // HQ
        G = HQ // HK
        KVE = D * HK
        B = 2
        N = 256
        LN_EPS = 1e-05

        def _xavier(k, fan_out, fan_in):
            std = np.sqrt(2.0 / (fan_in + fan_out)).astype(np.float32)
            return jax.random.normal(k, (fan_out, fan_in), jnp.float32) * std
        b, n, _ = query.shape
        q = query @ Wq.T + bq
        k = key @ Wk.T + bk
        v = value @ Wv.T + bv
        q = q.reshape(b, n, HQ, D).transpose(0, 2, 1, 3) / np.float32(np.sqrt(D))
        q = q.reshape(b, HK, G, n, D).transpose(0, 2, 1, 3, 4)
        k = k.reshape(b, n, HK, D).transpose(0, 2, 1, 3)
        v = v.reshape(b, n, HK, D).transpose(0, 2, 1, 3)
        sim = jnp.einsum('bghnd,bhsd->bghns', q, k)
        causal = jnp.tril(jnp.ones((n, n), bool))
        mask = causal[None, None, None, :, :] & (adj != 0)[:, None, None, :, :]
        neg = jnp.finfo(sim.dtype).min
        sim = jnp.where(mask, sim, neg)
        attn = jax.nn.softmax(sim, axis=-1)
        out = jnp.einsum('bghns,bhsd->bghnd', attn, v)
        out = out.transpose(0, 3, 2, 1, 4).reshape(b, n, E)
        mu = out.mean(-1, keepdims=True)
        var = jnp.mean(jnp.square(out - mu), -1, keepdims=True)
        out = (out - mu) / jnp.sqrt(var + LN_EPS) * ln_g + ln_b
        return out @ Wo.T + bo

    def _L1_ffn_ref(hidden_states, wg_red, wg, w1, b1, w2, b2):
        import jax, jax.numpy as jnp
        import numpy as np
        NUM_EXPERTS = 8
        IN_FEATURES = 128
        HIDDEN_FEATURES = 512
        GATE_DIM = 16
        EPS = 0.0001
        b, t, c = hidden_states.shape
        x = hidden_states.reshape(-1, c)
        xr = x @ wg_red.T
        wg_unit = wg / jnp.maximum(jnp.linalg.norm(wg, axis=1, keepdims=True), EPS)
        logits = xr @ wg_unit.T
        gates = jax.nn.softmax(logits, axis=1)
        indices_s = jnp.argmax(gates, axis=1)
        scores = jnp.max(gates, axis=1)
        E = wg.shape[0]
        out = jnp.zeros_like(x)
        for e in range(E):
            mask = (indices_s == e).astype(x.dtype)[:, None]
            h = jax.nn.gelu(x @ w1[e] + b1[e], approximate=False)
            out = out + mask * (h @ w2[e] + b2[e])
        out = out * scores[:, None]
        return out.reshape(b, t, c)
    x = x + _L0_xattn_ref(_layernorm(x, axis=-1), ctx_1024, ctx_1024, L0_xattn_Wq, L0_xattn_Wk, L0_xattn_Wv, L0_xattn_Wo)
    x = x + _L0_ffn_ref(_layernorm(x, axis=-1), L0_ffn_W1, L0_ffn_b1, L0_ffn_W2, L0_ffn_b2)
    x = x + _L1_xattn_ref(_layernorm(x, axis=-1), ctx_1024, ctx_1024, mask_BxSxS2_ik1, L1_xattn_Wq, L1_xattn_bq, L1_xattn_Wk, L1_xattn_bk, L1_xattn_Wv, L1_xattn_bv, L1_xattn_Wo, L1_xattn_bo, L1_xattn_ln_g, L1_xattn_ln_b)
    x = x + _L1_ffn_ref(_layernorm(x, axis=-1), L1_ffn_wg_red, L1_ffn_wg, L1_ffn_w1, L1_ffn_b1, L1_ffn_w2, L1_ffn_b2)
    return x

_drawn_inputs = setup_inputs


def setup_inputs(seed=0):
    import zlib

    import numpy as np

    out = dict(_drawn_inputs(seed))
    spreads = {'L1_xattn_bq': (0.0, 0.8),
     'L1_xattn_bk': (0.0, 0.8),
     'L1_xattn_bv': (0.0, 0.8),
     'L1_xattn_bo': (0.0, 0.8),
     'L1_xattn_ln_g': (1.0, 0.6),
     'L1_xattn_ln_b': (0.0, 0.8)}
    factors = {'L0_ffn_b1': 7.748,
     'L0_ffn_b2': 8.0,
     'L1_xattn_Wq': 8.0,
     'L1_xattn_Wk': 8.0,
     'L1_xattn_Wv': 5.888,
     'L1_xattn_Wo': 5.828,
     'L1_ffn_b1': 8.0,
     'L1_ffn_w2': 2.752,
     'L1_ffn_b2': 8.0}
    for name, (base, spread) in spreads.items():
        noise = np.random.default_rng([zlib.crc32(name.encode()), seed]).standard_normal(out[name].shape)
        drawn = base * np.exp(spread * noise) if base else spread * noise
        out[name] = jnp.asarray(drawn.astype(out[name].dtype))
    for name, factor in factors.items():
        out[name] = (out[name] * factor).astype(out[name].dtype)
    return out
```

```python
from contextlib import ExitStack

import numpy as np

import concourse.bass as bass
from concourse import mybir

ALU = mybir.AluOpType
ACT = mybir.ActivationFunctionType
AX = mybir.AxisListType
F32 = mybir.dt.float32
BF16 = mybir.dt.bfloat16
F16 = mybir.dt.float16
I32 = mybir.dt.int32

B, S, D = 32, 128, 128
HEADS, DK = 16, 8
KV1 = 4
FF = 512
FC = FF // 128
EXPERTS, GATE = 8, 16
QUARTERS = 4
HQ = HEADS // QUARTERS
PAIR = 2 * S
PAIRS = B // 2
BODY = 4
NB = B // BODY
QSLOT = (0, 0, 1, 0, 1, 2)
KSLOT = (0, 1, 0, 2, 1, 0)
SLOTS = len(QSLOT)
TERMS = 96
ROWS = TERMS + 3
VW = DK + 1
VP = 3 * VW
SCALE = float(1.0 / np.sqrt(np.float32(DK)))
MASKED = -float(2.0 ** 100)
LN_EPS = 1e-5
BIG_ROUND = 12582912.0


def build(nc, a, out):
    ctx = ExitStack()
    with ctx:
        def sb(name, shape, dt=F32):
            return ctx.enter_context(nc.sbuf_tensor(name, shape, dt))

        sems = {}

        def sem(name):
            if name not in sems:
                sems[name] = ctx.enter_context(nc.semaphore(name))
            return sems[name]

        def count(value):
            return max(value, 0) if isinstance(value, int) else value

        bank = [ctx.enter_context(nc.psum_tensor(f"bank{i}", [128, 512], F32)) for i in range(8)]
        SCORE = bank[0:2]
        SCORET = bank[2:4]
        PVOUT = bank[4]
        MISC = bank[5:8]

        X = sb("X", [128, B, D])
        eye = sb("eye", [128, 128])
        eyeb = sb("eyeb", [128, 128], BF16)
        ones = sb("ones", [128, 128])
        negI = sb("negI", [128, 128], BF16)
        upper = sb("upper", [128, 128], BF16)
        cosT = sb("cosT", [128, 128])
        sinT = sb("sinT", [128, 128])
        W0 = sb("W0", [128, 6, 128])
        W1Q = sb("W1Q", [128, 128])
        W1K = sb("W1K", [128, 32])
        W1V = sb("W1V", [128, 32])
        W1O = sb("W1O", [128, 128])
        cols = sb("cols", [128, 8])
        rowsb = sb("rowsb", [128, 3, 128])
        F1 = sb("F1", [128, FF])
        F1b = sb("F1b", [128, FC])
        F2 = sb("F2", [128, FC, 128])
        WG = sb("WG", [128, GATE])
        wgr = sb("wgr", [EXPERTS, GATE])
        M1 = sb("M1", [128, EXPERTS, FF])
        M1b = sb("M1b", [128, EXPERTS, FC])
        M2 = sb("M2", [128, EXPERTS, FC, 128])
        M2b = sb("M2b", [128, EXPERTS, 128])
        rank = sb("rank", [128, EXPERTS])

        ctxT = [sb(f"ctxT{i}", [128, PAIR]) for i in range(2)]
        adj = [sb(f"adj{i}", [128, 2, 128], I32) for i in range(2)]
        mask = sb("mask", [128, BODY, 128], BF16)
        stats = sb("stats", [128, 2, 6])
        mv = sb("mv", [128, 2, 2])
        rstd = sb("rstd", [128, 2])
        powers = sb("powers", [128, 9])
        xn = sb("xn", [128, 2, 128])
        xnT = sb("xnT", [128, 512])
        rotA = [sb(f"rotA{i}", [128, PAIR]) for i in range(2)]
        rotB = [sb(f"rotB{i}", [128, PAIR]) for i in range(2)]
        full = [sb(f"full{i}", [128, PAIR]) for i in range(2)]
        rest = [sb(f"rest{i}", [128, PAIR]) for i in range(2)]
        piece = [sb(f"piece{i}", [128, 3, PAIR], BF16) for i in range(2)]
        Qs = [sb(f"Qs{i}", [ROWS, HEADS, PAIR], BF16) for i in range(2)]
        Ks = [sb(f"Ks{i}", [ROWS, HEADS, PAIR], BF16) for i in range(2)]
        vfull = sb("vfull", [128, 2, 128])
        vrest = sb("vrest", [128, 2, 128])
        Vp = sb("Vp", [128, BODY, HEADS, 3, VW], BF16)
        negmax = sb("negmax", [128, 2, HEADS])
        negrest = sb("negrest", [128, HEADS])
        negp = sb("negp", [128, 8, HEADS], BF16)
        negpT = [sb(f"negpT{i}", [3 * HEADS, 128], BF16) for i in range(2)]
        P32 = sb("P32", [128, QUARTERS, 512])
        Ph = sb("Ph", [128, QUARTERS, 512], F16)
        Pl = sb("Pl", [128, QUARTERS, 512], F16)
        osum = sb("osum", [128, HEADS, VW])
        rden = sb("rden", [128, HEADS])
        onorm = sb("onorm", [128, 128])
        ostat = sb("ostat", [128, 6])
        omv = sb("omv", [128, 2])
        orstd = sb("orstd", [128, 1])
        oln = sb("oln", [128, 128])
        oT = sb("oT", [128, 128])
        proj = sb("proj", [128, 128])

        fxn = sb("fxn", [128, 2, 128])
        fxnT = sb("fxnT", [128, 2, PAIR])
        hT = sb("hT", [128, 2, FC, PAIR])
        tmp = sb("tmp", [128, 2, 128])
        qred = sb("qred", [128, 2])
        qgam = sb("qgam", [128, 2])
        mxn = sb("mxn", [128, 4, 128])
        mhT = sb("mhT", [128, 2, FC, 512])
        my = sb("my", [128, 2, 128])
        macc = sb("macc", [128, 4, 128])
        xrT = sb("xrT", [GATE, 512])
        wgT = sb("wgT", [GATE, EXPERTS])
        wgn = sb("wgn", [EXPERTS, 3])
        wgs = sb("wgs", [EXPERTS, 2, GATE])
        lg = sb("lg", [128, 4, EXPERTS])
        gtmp = sb("gtmp", [128, 4, EXPERTS])
        gs = sb("gs", [128, 4, 4])
        wt = sb("wt", [128, 4, EXPERTS])
        mst = sb("mst", [128, 4, 6])
        mmv = sb("mmv", [128, 4, 2])
        mrs = sb("mrs", [128, 4])

        xd = a["x"].rearrange("b s d -> s b d")
        od = out.rearrange("b s d -> s b d")
        maskd = a["mask"].rearrange("b q k -> q b k")
        ctxd = a["ctxT"]

        loads = [
            (eye[:], a["eye"]), (W0[:], a["W0"].rearrange("n e m -> e n m")),
            (cosT[:], a["cosT"]), (sinT[:], a["sinT"]),
            (eyeb[:], a["eyeb"]), (negI[:], a["negI"]), (upper[:], a["upper"]),
            (W1Q[:], a["W1Q"]), (W1K[:], a["W1K"]), (W1V[:], a["W1V"]), (W1O[:], a["W1O"]),
            (cols[:, 0:4], a["cols"]),
            (rowsb[:, 0, 0:32], a["bv"].partition_broadcast(128)),
            (rowsb[:, 1, :], a["bo"].partition_broadcast(128)),
            (rowsb[:, 2, :], a["b2"].partition_broadcast(128)),
            (F1[:], a["F1"]), (F1b[:], a["F1b"]), (F2[:], a["F2"].rearrange("(c p) n -> p c n", p=128)),
            (WG[:], a["WG"]), (wgr[:], a["wg"]),
            (rank[:], a["rank"].partition_broadcast(128)),
            (M1b[:], a["M1b"]),
            (M2b[:], a["M2b"].rearrange("e n -> (e n)").partition_broadcast(128)),
            (M1[:], a["M1"].rearrange("e p n -> p e n")),
            (M2[:], a["M2"].rearrange("e (c p) n -> p e c n", p=128)),
        ]
        X_CHUNKS = 4
        LOADED = 16 * len(loads)

        body = {}

        def body_loop(eng, step):
            def run(i):
                body["i"] = i
                for j in range(BODY):
                    step(i * BODY + j, j)

            run(0)
            with eng.Fori(1, NB - 1) as i:
                run(i)
            run(NB - 1)
            body["i"] = 0

        def pair(k):
            return body["i"] * (BODY // 2) + k // 2

        def parity(k):
            return k // 2 % 2

        def turns(k):
            return body["i"] + k // 4 + 1

        body["i"] = 0
        block = ctx.enter_context(nc.Block())

        @block.sync
        def _(sp):
            for c in range(X_CHUNKS):
                w = B // X_CHUNKS
                sp.dma_start(X[:, c * w:(c + 1) * w, :], xd[:, c * w:(c + 1) * w, :]).then_inc(sem("x_loaded"), 16)
                if c == 0:
                    for dst, src in loads:
                        sp.dma_start(dst, src).then_inc(sem("weights_loaded"), 16)

            def attention(L):
                n_kv = (HEADS, KV1)[L]

                def known(value):
                    return value if isinstance(value, int) else sp.snap(value)

                def load_ctx(k):
                    p, b = pair(k), parity(k)
                    before, column, row = known(p - 1), known(p * PAIR), known(p * 2)
                    sp.wait_ge(sem(f"v_projected{L}"), count(before))
                    sp.dma_start(ctxT[b][:], ctxd[:, bass.ds(column, PAIR)]).then_inc(sem(f"ctx_loaded{L}{b}"), 16)
                    if L:
                        sp.wait_ge(sem("mask_made"), count(before))
                        sp.dma_start(adj[b][:], maskd[:, bass.ds(row, 2), :]).then_inc(sem(f"adj_loaded{b}"), 16)

                def stack(k):
                    p, b = pair(k), parity(k)
                    read, cut = known(8 * (p - 1)), known(5 * p + 5)
                    sp.wait_ge(sem(f"scoresT_ready{L}"), count(read))
                    sp.wait_ge(sem(f"q_pieces{L}"), count(cut))
                    for s in range(SLOTS):
                        sp.dma_start(Qs[b][s * DK:(s + 1) * DK, :, :],
                                     piece[0][:, QSLOT[s], :]).then_inc(sem(f"q_stacked{L}{b}"), 16)
                    sp.wait_ge(sem(f"k_pieces{L}"), count(cut))
                    for s in range(SLOTS):
                        sp.dma_start(Ks[b][s * DK:(s + 1) * DK, 0:n_kv, :],
                                     piece[1][0:n_kv * DK, KSLOT[s], :]).then_inc(sem(f"k_stacked{L}{b}"), 16)

                def max_rows(t, b, tb):
                    sp.wait_ge(sem(f"negmaxT_ready{L}"), count(t + 1))
                    sp.dma_start(Qs[b][TERMS:ROWS, :, tb * S:(tb + 1) * S],
                                 negpT[tb][:]).then_inc(sem(f"max_rows{L}"), 16)

                load_ctx(0)
                load_ctx(2)
                if L == 0:
                    sp.wait_ge(sem("stacks_cleared"), count(4))
                stack(0)
                stack(2)
                max_rows(0, 0, 0)

                def step(t, j):
                    if j % 2 == 0 and not (isinstance(t, int) and t + 4 >= B):
                        load_ctx(j + 4)
                    if j % 2 == 0 and not (isinstance(t, int) and (t == 0 or t + 2 >= B)):
                        stack(j + 2)
                    if not (isinstance(t, int) and t + 1 >= B):
                        max_rows(t + 1, ((j + 1) // 2) % 2, (j + 1) % 2)

                body_loop(sp, step)

            attention(0)
            attention(1)
            for g in range(B // 4):
                sp.wait_ge(sem("out_ready"), count(g + 1))
                sp.dma_start(od[:, 4 * g:4 * g + 4, :], X[:, 4 * g:4 * g + 4, :]).then_inc(sem("stored"), 16)
            sp.wait_ge(sem("stored"), 16 * (B // 4))

        @block.tensor
        def _(pe):
            pe.wait_ge(sem("weights_loaded"), LOADED)

            def quantize_sums():
                for i in range(2):
                    pe.wait_ge(sem("abs_summed"), count(i + 1))
                    nc.tensor.matmul(MISC[i][:, 0:1], ones[:], qred[:, i:i + 1], start=True, stop=True).then_inc(sem("abs_total"), 1)
                pe.wait_ge(sem("gate_unit"), count(5))
                nc.tensor.transpose(MISC[2][0:GATE, 0:EXPERTS], wgs[:, 1, :], eye[0:EXPERTS, 0:EXPERTS]).then_inc(sem("gate_T"), 1)
                pe.wait_ge(sem("quantized"), count(2))
                pe.wait_ge(sem("gate_unitT"), count(1))

            quantize_sums()

            def attention(L):
                n_kv = (HEADS, KV1)[L]
                WQ, WK, WV, WO = ((W0[:, 0, :], W0[:, 2, :], W0[:, 4, :], W0[:, 5, :]) if L == 0 else
                                  (W1Q[:], W1K[:], W1V[:], W1O[:]))
                def xn_transposes(p, first=False):
                    pe.wait_ge(sem(f"xn_ready{L}"), count(2 * (p + 1)))
                    pe.wait_ge(sem(f"k_bank_read{L}" if first else f"v_split{L}"), count(p if first else 3 * (p - 1)))
                    for b in range(2):
                        mm = nc.tensor.transpose(MISC[0][:, b * S:(b + 1) * S], xn[:, b, :], eye[:])
                    mm.then_inc(sem(f"xn_transposed{L}"), 1)

                def project_q(p):
                    pe.wait_ge(sem(f"xnT_ready{L}"), count(p + 1))
                    nc_ = MISC[1]
                    mm = nc.tensor.matmul(nc_[:, 0:PAIR], WQ, xnT[:, 0:PAIR], start=True, stop=True)
                    if L == 0:
                        mm = nc.tensor.matmul(nc_[:, PAIR:2 * PAIR], W0[:, 1, :], xnT[:, 0:PAIR], start=True, stop=True)
                    mm.then_inc(sem(f"q_projected{L}"), 1)

                def project_k(k):
                    p, b = pair(k), parity(k)
                    pe.wait_ge(sem(f"ctx_loaded{L}{b}"), count(16 * turns(k)))
                    m = n_kv * DK
                    mm = nc.tensor.matmul(MISC[2][0:m, 0:PAIR], WK, ctxT[b][:], start=True, stop=True)
                    if L == 0:
                        mm = nc.tensor.matmul(MISC[2][:, PAIR:2 * PAIR], W0[:, 3, :], ctxT[b][:], start=True, stop=True)
                    mm.then_inc(sem(f"k_projected{L}"), 1)

                def project_v(p, b):
                    m = n_kv * DK
                    for h in range(2):
                        mm = nc.tensor.matmul(MISC[0][:, h * 128:h * 128 + m], ctxT[b][:, h * S:(h + 1) * S], WV,
                                              start=True, stop=True)
                    mm.then_inc(sem(f"v_projected{L}"), 1)

                def scores(t, c, pb, tb, mj, k):
                    if c == 0:
                        pe.wait_ge(sem(f"q_stacked{L}{pb}"), count(16 * SLOTS * turns(k)))
                        pe.wait_ge(sem(f"k_stacked{L}{pb}"), count(16 * SLOTS * turns(k)))
                        if L:
                            pe.wait_ge(sem("mask_made"), count(pair(k) + 1))
                    pe.wait_ge(sem(f"maxima{L}"), count(4 * t + c - 1))
                    o = SCORE[c % 2]
                    if L:
                        nc.tensor.matmul(o[:].rearrange("p (h k) -> p h k", h=HQ), negI[:],
                                         mask[:, mj, :].unsqueeze(1).broadcast_to([128, HQ, 128]),
                                         start=True, stop=False, skip_group_check=True)
                    for i in range(HQ):
                        h = c * HQ + i
                        kv = h if L == 0 else c
                        mm = nc.tensor.matmul(o[:, i * 128:(i + 1) * 128], Qs[pb][0:TERMS, h, tb * S:(tb + 1) * S],
                                              Ks[pb][0:TERMS, kv, tb * S:(tb + 1) * S],
                                              start=(L == 0), stop=True, skip_group_check=bool(L))
                    mm.then_inc(sem(f"scores_ready{L}"), 1)

                def scoresT(t, c, pb, tb, mj):
                    if c == 0:
                        pe.wait_ge(sem(f"max_rows{L}"), count(16 * (t + 1)))
                    pe.wait_ge(sem(f"exp_done{L}"), count(2 * (4 * t + c - 1)))
                    o = SCORET[c % 2]
                    if L:
                        nc.tensor.matmul(o[:].rearrange("p (h q) -> p h q", h=HQ), mask[:, mj, :],
                                         negI[:].unsqueeze(1).broadcast_to([128, HQ, 128]),
                                         start=True, stop=False, skip_group_check=True)
                        mm = nc.tensor.matmul(o[:].rearrange("p (h q) -> p h q", h=HQ), Ks[pb][0:ROWS, c, tb * S:(tb + 1) * S],
                                              Qs[pb][0:ROWS, c * HQ:(c + 1) * HQ, tb * S:(tb + 1) * S],
                                              start=False, stop=True, skip_group_check=True)
                    else:
                        for i in range(HQ):
                            h = c * HQ + i
                            mm = nc.tensor.matmul(o[:, i * 128:(i + 1) * 128], Ks[pb][0:ROWS, h, tb * S:(tb + 1) * S],
                                                  Qs[pb][0:ROWS, h, tb * S:(tb + 1) * S], start=True, stop=True)
                    mm.then_inc(sem(f"scoresT_ready{L}"), 1)

                def pv(t, c, j):
                    if c == 0:
                        pe.wait_ge(sem(f"pv_read{L}"), count(t))
                        if j % 2 == 0:
                            pe.wait_ge(sem(f"v_split{L}"), count(3 * (pair(j) + 1)))
                    pe.wait_ge(sem(f"low_even{L}" if c % 2 == 0 else f"low_odd{L}"), count(2 * t + c // 2 + 1))
                    pe.wait_ge(sem(f"exp_done{L}"), count(2 * (4 * t + c + 1)))
                    for i in range(HQ):
                        h = c * HQ + i
                        for n, p in enumerate((Ph, Pl)):
                            mm = nc.tensor.matmul(PVOUT[:, h * VP:(h + 1) * VP], p[:, c, i * 128:(i + 1) * 128],
                                                  Vp[:, j, h if L == 0 else c, :, :].rearrange("p c e -> p (c e)"),
                                                  start=(n == 0), stop=(n == 1))
                    mm.then_inc(sem(f"pv_done{L}"), 1)

                def max_transpose(t, tb, even_step):
                    pe.wait_ge(sem(f"negmax_split{L}"), count(4 * (t + 1)))
                    m = MISC[2 if even_step else 1]
                    nc.tensor.transpose(m[:, 0:64].bitcast(BF16), negp[:].rearrange("p c h -> p (c h)"),
                                        eyeb[:]).then_inc(sem(f"negmax_transposed{L}"), 1)

                NORM = (2, 4)[L]

                def out_transpose(t, j):
                    m = MISC[1 if j % 2 == 0 else 0]
                    if L == 0:
                        pe.wait_ge(sem("out_norm0"), count(2 * t))
                    else:
                        pe.wait_ge(sem("out_centred"), count(t))
                    nc.tensor.transpose(m[:, 0:128], (onorm if L == 0 else oln)[:], eye[:]).then_inc(sem(f"out_transposed{L}"), 1)

                def out_project(t, j):
                    m = MISC[1 if j % 2 == 0 else 2]
                    pe.wait_ge(sem(f"outT_ready{L}"), count(t))
                    nc.tensor.matmul(m[:, 0:128], oT[:], WO, start=True, stop=True).then_inc(sem(f"out_projected{L}"), 1)

                for p in range(2):
                    xn_transposes(p, first=True)
                    if p:
                        pe.wait_ge(sem(f"q_bank_read{L}"), count(p))
                    project_q(p)
                    if p:
                        pe.wait_ge(sem(f"k_bank_read{L}"), count(p))
                    project_k(2 * p)
                pe.wait_ge(sem(f"xnT_ready{L}"), count(2))
                project_v(0, 0)
                for c in range(QUARTERS):
                    scores(0, c, 0, 0, 0, 0)
                pe.wait_ge(sem(f"k_bank_read{L}"), count(2))
                max_transpose(0, 0, True)

                def step(t, j):
                    first = isinstance(t, int) and t == 0
                    ahead = not (isinstance(t, int) and t + 1 >= B)
                    pb, tb = (j // 2) % 2, j % 2
                    nj = (j + 1) % BODY
                    npb, ntb = nj // 2, nj % 2

                    def s(c):
                        if ahead:
                            scores(t + 1, c, npb, ntb, nj, j + 1)

                    for c in range(2):
                        scoresT(t, c, pb, tb, j)
                        s(c)
                    pv(t, 0, j)
                    scoresT(t, 2, pb, tb, j)
                    s(2)
                    pv(t, 1, j)
                    scoresT(t, 3, pb, tb, j)
                    s(3)
                    if not first:
                        if j % 2 == 0:
                            pe.wait_ge(sem(f"negmaxT_ready{L}"), count(t + 1))
                        else:
                            pe.wait_ge(sem(f"xnT_ready{L}"), count(pair(j) + 3 if not (isinstance(t, int) and t + 3 >= B) else PAIRS))
                        out_transpose(t, j)
                    if j % 2 == 1:
                        if not (isinstance(t, int) and t + 3 >= B):
                            pe.wait_ge(sem(f"attn_added{L}"), count(2 * (t - 1)))
                            project_q(pair(j) + 2)
                            pe.wait_ge(sem(f"negmaxT_ready{L}"), count(t + 1))
                            project_k(j + 3)
                        if not (isinstance(t, int) and t + 1 >= B):
                            pe.wait_ge(sem(f"outT_ready{L}"), count(t if not first else 0))
                            project_v(pair(j) + 1, (j // 2 + 1) % 2)
                    pv(t, 2, j)
                    if ahead:
                        if j % 2 == 0:
                            pe.wait_ge(sem(f"attn_added{L}"), count(2 * (t - 1)))
                        elif not (isinstance(t, int) and t + 3 >= B):
                            pe.wait_ge(sem(f"q_bank_read{L}"), count(pair(j) + 3))
                        else:
                            pe.wait_ge(sem(f"attn_added{L}"), count(2 * (t - 1)))
                        max_transpose(t + 1, ntb, j % 2 == 0)
                    if not first:
                        if j % 2 == 1 and not (isinstance(t, int) and t + 3 >= B):
                            pe.wait_ge(sem(f"k_bank_read{L}"), count(pair(j) + 3))
                        elif j % 2 == 1:
                            pe.wait_ge(sem(f"negmaxT_ready{L}"), count(t + 1))
                        out_project(t, j)
                    pv(t, 3, j)
                    if j % 2 == 0 and not (isinstance(t, int) and t + 4 >= B):
                        xn_transposes(pair(j) + 2)

                body_loop(pe, step)
                pe.wait_ge(sem(f"attn_added{L}"), count(2 * (B - 1)))
                out_transpose(B, 0)
                out_project(B, 0)
                pe.wait_ge(sem(f"attn_added{L}"), count(2 * B))

            def ffn():
                def transposes(p, b):
                    pe.wait_ge(sem("f_xn_ready"), count(2 * (p + 1)))
                    pe.wait_ge(sem("f_xnT_ready"), count(p - 1))
                    for h in range(2):
                        mm = nc.tensor.transpose(bank[b][:, h * S:(h + 1) * S], fxn[:, h, :], eye[:])
                    mm.then_inc(sem("f_transposed"), 1)

                def up(p, b):
                    pe.wait_ge(sem("f_xnT_ready"), count(p + 1))
                    for c in range(FC):
                        pe.wait_ge(sem("f_relu"), count(FC * p + c - FC + 1))
                        nc.tensor.matmul(bank[2 + c][:, 0:PAIR], F1[:, c * 128:(c + 1) * 128], fxnT[:, b, :],
                                         start=True, stop=True).then_inc(sem("f_up"), 1)

                def down(p, b):
                    pe.wait_ge(sem("f_relu"), count(FC * (p + 1)))
                    for h in range(2):
                        pe.wait_ge(sem("f_bank_read"), count(2 * p + h - 1))
                        for c in range(FC):
                            mm = nc.tensor.matmul(bank[6 + h][:, 0:128], hT[:, b, c, h * S:(h + 1) * S], F2[:, c, :],
                                                  start=(c == 0), stop=(c == FC - 1))
                        mm.then_inc(sem("f_down"), 1)

                def step(p, b, last):
                    if last < 2:
                        transposes(p + 2, b)
                    if last < 1 or last == 2:
                        pass
                    if not last == 3:
                        up(p + 1, 1 - b)
                    down(p, b)

                transposes(0, 0)
                transposes(1, 1)
                up(0, 0)
                step(0, 0, 0)
                step(1, 1, 0)
                with pe.Fori(1, PAIRS // 2 - 1) as i:
                    for b in range(2):
                        step(i * 2 + b, b, 0)
                step(PAIRS - 2, 0, 2)
                step(PAIRS - 1, 1, 3)
                pe.wait_ge(sem("f_bank_read"), count(2 * PAIRS))

            def moe():
                for g in range(B // 4):
                    pe.wait_ge(sem("m_xn_ready"), count(4 * (g + 1)))
                    pe.wait_ge(sem("m_gated"), count(0))
                    if g:
                        pe.wait_ge(sem("m_acc"), count(64 * g))
                    for h in range(4):
                        mm = nc.tensor.transpose(bank[0][:, h * S:(h + 1) * S], mxn[:, h, :], eye[:])
                    mm.then_inc(sem("m_transposed"), 1)
                    pe.wait_ge(sem("m_xnT"), count(g + 1))
                    nc.tensor.matmul(bank[1][0:GATE, :], WG[:], xnT[:], start=True, stop=True).then_inc(sem("m_red"), 1)
                    pe.wait_ge(sem("m_redT"), count(g + 1))
                    for h in range(4):
                        mm = nc.tensor.matmul(bank[0][:, h * EXPERTS:(h + 1) * EXPERTS], xrT[:, h * S:(h + 1) * S], wgT[:],
                                              start=True, stop=True)
                    mm.then_inc(sem("m_logits"), 1)
                    def up(e):
                        n = g * EXPERTS + e
                        for c in range(FC):
                            pe.wait_ge(sem("m_gelu"), count(FC * n + c - 3))
                            nc.tensor.matmul(bank[2 + c][:], M1[:, e, c * 128:(c + 1) * 128], xnT[:],
                                             start=True, stop=True).then_inc(sem("m_up"), 1)
                    def down(e):
                        n = g * EXPERTS + e
                        pe.wait_ge(sem("m_gelu"), count(FC * (n + 1)))
                        for h in range(4):
                            pe.wait_ge(sem("m_bank_read"), count(4 * n + h - 1))
                            for c in range(FC):
                                mm = nc.tensor.matmul(bank[6 + h % 2][:, 0:128], mhT[:, e % 2, c, h * S:(h + 1) * S],
                                                      M2[:, e, c, :], start=(c == 0), stop=(c == FC - 1))
                            mm.then_inc(sem("m_down"), 1)
                    up(0)
                    for e in range(EXPERTS):
                        if e + 1 < EXPERTS:
                            up(e + 1)
                        down(e)

            attention(0)
            ffn()
            attention(1)
            moe()

        @block.scalar
        def _(act):
            act.wait_ge(sem("weights_loaded"), LOADED)

            def attention(L):
                def evac_xnT(p):
                    act.wait_ge(sem(f"xn_transposed{L}"), count(p + 1))
                    act.wait_ge(sem(f"q_projected{L}"), count(p))
                    nc.scalar.copy(xnT[:, 0:PAIR], MISC[0][:, 0:PAIR]).then_inc(sem(f"xnT_ready{L}"), 1)

                def biased(k, which):
                    p = pair(k)
                    m = (128, KV1 * DK)[which]
                    nm = "qk"[which]
                    act.wait_ge(sem(f"{nm}_projected{L}"), count(p + 1))
                    act.wait_ge(sem(f"{nm}_pieces{L}"), count(5 * p))
                    act.wait_ge(sem(f"{nm}_stacked{L}{parity(k - 2)}"), count(16 * SLOTS * turns(k - 2)))
                    src = MISC[1 + which][0:m, 0:PAIR]
                    nc.scalar.activation(full[which][0:m, :], src, ACT.Identity, bias=cols[0:m, which:which + 1]
                                         ).then_inc(sem(f"{nm}_pieces{L}"), 1)
                    nc.scalar.activation(piece[which][0:m, 0, :], src, ACT.Identity, bias=cols[0:m, which:which + 1]
                                         ).then_inc(sem(f"{nm}_pieces{L}"), 1)
                    act.wait_ge(sem(f"{nm}_pieces{L}"), count(5 * p + 2))
                    act.sem_inc(sem(f"{nm}_bank_read{L}"), 1)

                def exps(t, c):
                    act.wait_ge(sem(f"scoresT_ready{L}"), count(4 * t + c + 1))
                    act.wait_ge(sem(f"pv_done{L}"), count(4 * t + c - 3))
                    nc.scalar.activation(P32[:, c, :], SCORET[c % 2][:], ACT.Exp, scale=SCALE).then_inc(sem(f"exp_done{L}"), 1)
                    nc.scalar.activation(Ph[:, c, :], SCORET[c % 2][:], ACT.Exp, scale=SCALE).then_inc(sem(f"exp_done{L}"), 1)

                def evac_max(t, tb, even_step):
                    act.wait_ge(sem(f"negmax_transposed{L}"), count(t + 1))
                    act.wait_ge(sem(f"max_rows{L}"), count(16 * (t - 1)))
                    m = MISC[2 if even_step else 1]
                    nc.scalar.copy(negpT[tb][:], m[0:48, 0:64].bitcast(BF16)).then_inc(sem(f"negmaxT_ready{L}"), 1)

                def evac_out(t, j):
                    m = MISC[1 if j % 2 == 0 else 0]
                    act.wait_ge(sem(f"out_transposed{L}"), count(t))
                    act.wait_ge(sem(f"out_projected{L}"), count(t - 1))
                    if L == 0:
                        nc.scalar.copy(oT[:], m[:, 0:128]).then_inc(sem(f"outT_ready{L}"), 1)
                    else:
                        nc.scalar.activation(oT[:], m[:, 0:128], ACT.Identity, bias=cols[:, 3:4], scale=cols[:, 2:3]
                                             ).then_inc(sem(f"outT_ready{L}"), 1)

                for p in range(2):
                    evac_xnT(p)
                    if L:
                        biased(2 * p, 0)
                        biased(2 * p, 1)
                evac_max(0, 0, True)

                def step(t, j):
                    first = isinstance(t, int) and t == 0
                    for c in range(QUARTERS):
                        exps(t, c)
                    if not first:
                        evac_out(t, j)
                    if j % 2 == 1 and L and not (isinstance(t, int) and t + 3 >= B):
                        biased(j + 3, 0)
                        biased(j + 3, 1)
                    if not (isinstance(t, int) and t + 1 >= B):
                        evac_max(t + 1, (j + 1) % 2, j % 2 == 0)
                    if j % 2 == 0 and not (isinstance(t, int) and t + 4 >= B):
                        evac_xnT(pair(j) + 2)

                body_loop(act, step)
                evac_out(B, 0)

            def ffn():
                def step(p, b):
                    act.wait_ge(sem("f_transposed"), count(p + 1))
                    act.wait_ge(sem("f_up"), count(FC * (p - 1)))
                    nc.scalar.copy(fxnT[:, b, :], bank[b][:, 0:PAIR]).then_inc(sem("f_xnT_ready"), 1)

                def relus(p, b):
                    for c in range(FC):
                        act.wait_ge(sem("f_up"), count(FC * p + c + 1))
                        act.wait_ge(sem("f_down"), count(2 * (p - 1)))
                        nc.scalar.activation(hT[:, b, c, :], bank[2 + c][:, 0:PAIR], ACT.Relu, bias=F1b[:, c:c + 1]
                                             ).then_inc(sem("f_relu"), 1)

                step(0, 0)
                step(1, 1)
                relus(0, 0)
                for b in range(2):
                    step(b + 2, b)
                    relus(b + 1, 1 - b)
                with act.Fori(1, PAIRS // 2 - 1) as i:
                    for b in range(2):
                        step(i * 2 + b + 2, b)
                        relus(i * 2 + b + 1, 1 - b)
                relus(PAIRS - 1, 1)

            def moe():
                for g in range(B // 4):
                    act.wait_ge(sem("m_transposed"), count(g + 1))
                    act.wait_ge(sem("m_up"), count(FC * EXPERTS * g))
                    nc.scalar.copy(xnT[:], bank[0][:]).then_inc(sem("m_xnT"), 1)
                    act.wait_ge(sem("m_red"), count(g + 1))
                    nc.scalar.copy(xrT[:], bank[1][0:GATE, :]).then_inc(sem("m_redT"), 1)
                    act.wait_ge(sem("m_maxed"), count(g + 1))
                    for h in range(4):
                        nc.scalar.activation(gtmp[:, h, :], lg[:, h, :], ACT.Exp, bias=gs[:, h, 0:1],
                                             accum_out=gs[:, h, 1:2]).then_inc(sem("m_exp"), 1)
                    for e in range(EXPERTS):
                        n = g * EXPERTS + e
                        for c in range(FC):
                            act.wait_ge(sem("m_up"), count(FC * n + c + 1))
                            act.wait_ge(sem("m_down"), count(4 * (n - 1)))
                            nc.scalar.activation(mhT[:, e % 2, c, :], bank[2 + c][:], ACT.Gelu, bias=M1b[:, e, c:c + 1]
                                                 ).then_inc(sem("m_gelu"), 1)

            attention(0)
            ffn()
            attention(1)
            moe()

        @block.gpsimd
        def _(pool):
            nc.gpsimd.memset(powers[:, 0:4], -0.5).then_inc(sem("powers_set"), 1)
            nc.gpsimd.memset(powers[:, 4:5], 0.5).then_inc(sem("powers_set"), 1)
            nc.gpsimd.memset(powers[:, 5:9], LN_EPS).then_inc(sem("powers_set"), 1)
            pool.wait_ge(sem("powers_set"), 3)

            def rstd_of(name, index, n, mv_, rs_):
                pool.wait_ge(sem(name + "_stats"), count(2 * n * (index + 1)))
                pool.wait_ge(sem(name), count(n * index))
                nc.gpsimd.tensor_tensor(rs_[:], mv_[:, :, 1:2].rearrange("p n o -> p (n o)"), powers[:, 5:5 + n], ALU.add).then_inc(sem(name + "_rstd"), 1)
                pool.wait_ge(sem(name + "_rstd"), 2 * index + 1)
                nc.gpsimd.tensor_tensor(rs_[:], rs_[:], powers[:, 0:n], ALU.pow).then_inc(sem(name + "_rstd"), 1)

            def attention(L):
                def cut(k, which):
                    p = pair(k)
                    nm = "qk"[which]
                    m = 128 if L == 0 or which == 0 else KV1 * DK
                    h, f, r, pc = (piece[which][0:m, 0, :], full[which][0:m, :], rest[which][0:m, :], piece[which])
                    if L == 0:
                        pool.wait_ge(sem(f"{nm}_rotated"), count(2 * (p + 1)))
                        pool.wait_ge(sem(f"{nm}_stacked{L}{parity(k - 2)}"), count(16 * SLOTS * turns(k - 2)))
                        A, Bt = rotA[which][:], rotB[which][:]
                        nc.gpsimd.tensor_tensor(h, A, Bt, ALU.add).then_inc(sem(f"{nm}_pieces{L}"), 1)
                        pool.wait_ge(sem(f"{nm}_pieces{L}"), 5 * p + 1)
                        nc.gpsimd.tensor_tensor(f, A, Bt, ALU.add).then_inc(sem(f"{nm}_pieces{L}"), 1)
                        pool.wait_ge(sem(f"{nm}_pieces{L}"), 5 * p + 2)
                    else:
                        pool.wait_ge(sem(f"{nm}_pieces{L}"), count(5 * p + 2))
                    nc.gpsimd.tensor_tensor(pc[0:m, 1, :], f, h, ALU.subtract).then_inc(sem(f"{nm}_pieces{L}"), 1)
                    pool.wait_ge(sem(f"{nm}_pieces{L}"), 5 * p + 3)
                    nc.gpsimd.tensor_tensor(r, f, h, ALU.subtract).then_inc(sem(f"{nm}_pieces{L}"), 1)
                    pool.wait_ge(sem(f"{nm}_pieces{L}"), 5 * p + 4)
                    nc.gpsimd.tensor_tensor(pc[0:m, 2, :], r, pc[0:m, 1, :], ALU.subtract).then_inc(sem(f"{nm}_pieces{L}"), 1)

                def low(t, c):
                    pool.wait_ge(sem(f"exp_done{L}"), count(2 * (4 * t + c + 1)))
                    pool.wait_ge(sem(f"pv_done{L}"), count(4 * t + c - 3))
                    nc.gpsimd.tensor_tensor(Pl[:, c, :], P32[:, c, :], Ph[:, c, :], ALU.subtract).then_inc(sem(f"low_even{L}"), 1)

                if L == 0:
                    pool.wait_ge(sem("gate_unit"), count(2))
                    nc.gpsimd.tensor_tensor(wgn[:, 1:2], wgn[:, 0:1], powers[0:EXPERTS, 4:5], ALU.pow).then_inc(sem("gate_norm"), 1)
                    for i in range(2):
                        nc.gpsimd.memset(Qs[i][:], 0.0).then_inc(sem("stacks_cleared"), 1)
                for p in range(2):
                    rstd_of(f"xn_ready{L}", p, 2, mv, rstd)
                    cut(2 * p, 0)
                    cut(2 * p, 1)

                def step(t, j):
                    low(t, 0)
                    if L and not (isinstance(t, int) and t == 0):
                        out_rstd(t)
                    if j % 2 == 0 and not (isinstance(t, int) and t + 4 >= B):
                        rstd_of(f"xn_ready{L}", pair(j) + 2, 2, mv, rstd)
                    if j % 2 == 0 and not (isinstance(t, int) and (t == 0 or t + 2 >= B)):
                        cut(j + 2, 1)
                    low(t, 2)
                    if j % 2 == 1 and not (isinstance(t, int) and t + 3 >= B):
                        cut(j + 3, 0)

                def out_rstd(t):
                    pool.wait_ge(sem("out_norm1"), count(4 * t))
                    pool.wait_ge(sem("out_centred"), count(t - 1))
                    nc.gpsimd.tensor_tensor(orstd[:], omv[:, 1:2], powers[:, 5:6], ALU.add).then_inc(sem("out_rstd"), 1)
                    pool.wait_ge(sem("out_rstd"), 2 * (t - 1) + 1)
                    nc.gpsimd.tensor_tensor(orstd[:], orstd[:], powers[:, 0:1], ALU.pow).then_inc(sem("out_rstd"), 1)

                body_loop(pool, step)
                if L:
                    out_rstd(B)

            attention(0)
            rstd_of("f_xn_ready", 0, 2, mv, rstd)
            with pool.Fori(1, PAIRS) as p:
                rstd_of("f_xn_ready", p, 2, mv, rstd)
            attention(1)
            for g in range(B // 4):
                rstd_of("m_xn_ready", g, 4, mmv, mrs)

        @block.vector
        def _(dve):
            def norm_stats(name, index, n, src, st_, mv_):
                for i in range(n):
                    nc.vector.bn_stats(st_[:, i, :], src(i)).then_inc(sem(name + "_stats"), 1)
                dve.wait_ge(sem(name + "_stats"), index * 2 * n + n)
                dve.sem_inc(sem("stats_seen"), 1)
                for i in range(n):
                    nc.vector.bn_aggr(mv_[:, i, :], st_[:, i, :]).then_inc(sem(name + "_stats"), 1)

            def norm_apply(name, index, n, src, mv_, rs_, dst):
                dve.wait_ge(sem(name + "_rstd"), count(2 * (index + 1)))
                for i in range(n):
                    nc.vector.tensor_scalar(dst(i), src(i), mv_[:, i, 0:1], rs_[:, i:i + 1], ALU.subtract, ALU.mult
                                            ).then_inc(sem(name), 1)

            for i in range(2):
                nc.vector.memset(Ks[i][:], 0.0).then_inc(sem("k_cleared"), 1)
            nc.vector.memset(ones[:], 1.0).then_inc(sem("ones_set"), 1)
            nc.vector.memset(Vp[:], 0.0).then_inc(sem("v_cleared"), 1)
            nc.vector.memset(negp[:], 0.0).then_inc(sem("ones_set"), 1)
            dve.wait_ge(sem("k_cleared"), 2)
            for i in range(2):
                nc.vector.memset(Ks[i][TERMS:ROWS, :, :], 1.0).then_inc(sem("stacks_cleared"), 1)
            dve.wait_ge(sem("v_cleared"), 1)
            nc.vector.memset(Vp[:, :, :, 0, DK:VW], 1.0).then_inc(sem("v_cleared"), 1)
            dve.wait_ge(sem("weights_loaded"), LOADED)
            dve.wait_ge(sem("ones_set"), 2)

            FW = (F1[:], F2[:].rearrange("p c n -> p (c n)"))
            for i, w in enumerate(FW):
                nc.vector.tensor_reduce(qred[:, i:i + 1], w, AX.X, ALU.add, apply_absolute_value=True).then_inc(sem("abs_summed"), 1)
            for i, w in enumerate(FW):
                dve.wait_ge(sem("abs_total"), count(i + 1))
                nc.vector.tensor_scalar(qgam[:, i:i + 1], MISC[i][:, 0:1], 1.0 / (FF * D), 1e-5, ALU.mult, ALU.add).then_inc(sem(f"quant{i}"), 1)
                dve.wait_ge(sem(f"quant{i}"), 1)
                nc.vector.reciprocal(qred[:, i:i + 1], qgam[:, i:i + 1]).then_inc(sem(f"quant{i}"), 1)
                dve.wait_ge(sem(f"quant{i}"), 2)
                nc.vector.tensor_scalar(w, w, qred[:, i:i + 1], 1.0, ALU.mult, ALU.min).then_inc(sem(f"quant{i}"), 1)
                dve.wait_ge(sem(f"quant{i}"), 3)
                nc.vector.tensor_scalar(w, w, -1.0, BIG_ROUND, ALU.max, ALU.add).then_inc(sem(f"quant{i}"), 1)
                dve.wait_ge(sem(f"quant{i}"), 4)
                nc.vector.tensor_scalar(w, w, BIG_ROUND, None, ALU.subtract).then_inc(sem("quantized"), 1)
            nc.vector.tensor_tensor(wgs[:, 0, :], wgr[:], wgr[:], ALU.mult).then_inc(sem("gate_unit"), 1)
            dve.wait_ge(sem("gate_unit"), 1)
            nc.vector.tensor_reduce(wgn[:, 0:1], wgs[:, 0, :], AX.X, ALU.add).then_inc(sem("gate_unit"), 1)
            dve.wait_ge(sem("gate_unit"), 2)
            dve.wait_ge(sem("gate_norm"), 1)
            nc.vector.tensor_scalar(wgn[:, 2:3], wgn[:, 1:2], 1e-4, None, ALU.max).then_inc(sem("gate_unit"), 1)
            dve.wait_ge(sem("gate_unit"), 3)
            nc.vector.reciprocal(wgn[:, 0:1], wgn[:, 2:3]).then_inc(sem("gate_unit"), 1)
            dve.wait_ge(sem("gate_unit"), 4)
            nc.vector.tensor_scalar(wgs[:, 1, :], wgr[:], wgn[:, 0:1], None, ALU.mult).then_inc(sem("gate_unit"), 1)
            dve.wait_ge(sem("gate_T"), count(1))
            nc.vector.tensor_copy(wgT[:], MISC[2][0:GATE, 0:EXPERTS]).then_inc(sem("gate_unitT"), 1)
            dve.wait_ge(sem("x_loaded"), 16 * X_CHUNKS)

            def attention(L):
                n_kv = (HEADS, KV1)[L]
                NORM = (2, 4)[L]

                def x_of(p):
                    if isinstance(p, int):
                        return lambda i: X[:, 2 * p + i, :]
                    return lambda i: X[:, bass.ds(p * 2 + i, 1), :].rearrange("p o d -> p (o d)")

                def x_stats(p):
                    norm_stats(f"xn_ready{L}", p, 2, x_of(p), stats, mv)

                def x_apply(p):
                    dve.wait_ge(sem(f"xn_transposed{L}"), count(p))
                    norm_apply(f"xn_ready{L}", p, 2, x_of(p), mv, rstd, lambda i: xn[:, i, :])

                def rotate(p, which):
                    nm = "qk"[which]
                    dve.wait_ge(sem(f"{nm}_projected{L}"), count(p + 1))
                    dve.wait_ge(sem(f"{nm}_pieces{L}"), count(5 * p))
                    for tab, dst, off in ((cosT, rotA, 0), (sinT, rotB, PAIR)):
                        ins = nc.vector.tensor_tensor(
                            dst[which][:].rearrange("p (b s) -> p b s", b=2),
                            MISC[1 + which][:, off:off + PAIR].rearrange("p (b s) -> p b s", b=2),
                            tab[:].unsqueeze(1).broadcast_to([128, 2, 128]), ALU.mult)
                        ins.then_inc(sem(f"{nm}_rotated"), 1)
                    dve.wait_ge(sem(f"{nm}_rotated"), 2 * (p + 1))
                    dve.sem_inc(sem(f"{nm}_bank_read{L}"), 1)

                def split_v(p, j):
                    dve.wait_ge(sem(f"v_projected{L}"), count(p + 1))
                    m = n_kv * DK
                    ps = MISC[0][:, 0:256].rearrange("p (b n) -> p b n", b=2)[:, :, 0:m]
                    f, r = vfull[:, :, 0:m], vrest[:, :, 0:m]

                    def pieces(c):
                        return Vp[:, j:j + 2, 0:n_kv, c, 0:DK]

                    def heads(ap):
                        return ap.rearrange("p b (h d) -> p b h d", d=DK)

                    if L == 0:
                        nc.vector.tensor_copy(f, ps).then_inc(sem(f"v_split{L}"), 1)
                    else:
                        nc.vector.tensor_tensor(f, ps, rowsb[:, 0:1, 0:m].broadcast_to([128, 2, m]), ALU.add).then_inc(sem(f"v_split{L}"), 1)
                    dve.wait_ge(sem(f"v_split{L}"), 3 * p + 1)
                    nc.vector.tensor_copy(pieces(0), heads(f)).then_inc(sem(f"v_split{L}"), 1)
                    dve.wait_ge(sem(f"v_split{L}"), 3 * p + 2)
                    nc.vector.tensor_tensor(heads(r), heads(f), pieces(0), ALU.subtract).then_inc(sem(f"v_rest{L}"), 1)
                    nc.vector.tensor_tensor(pieces(1), heads(f), pieces(0), ALU.subtract).then_inc(sem(f"v_rest{L}"), 1)
                    dve.wait_ge(sem(f"v_rest{L}"), 2 * (p + 1))
                    nc.vector.tensor_tensor(pieces(2), heads(r), pieces(1), ALU.subtract).then_inc(sem(f"v_split{L}"), 1)

                def make_mask(k):
                    b, j = parity(k), k % BODY
                    dve.wait_ge(sem(f"adj_loaded{b}"), count(16 * turns(k)))
                    for i in range(2):
                        jj = (j + i) % BODY
                        ins = nc.vector.scalar_tensor_tensor(mask[:, jj, :], adj[b][:, i, :], 0.0, upper[:], ALU.is_equal, ALU.max)
                    ins.then_inc(sem("mask_made"), 1)

                def maxima(t, c, tb):
                    dve.wait_ge(sem(f"scores_ready{L}"), count(4 * t + c + 1))
                    nc.vector.tensor_reduce(negmax[:, tb, c * HQ:(c + 1) * HQ], SCORE[c % 2][:].rearrange("p (h k) -> p h k", h=HQ),
                                            AX.X, ALU.max, negate=True).then_inc(sem(f"maxima{L}"), 1)

                def split_max(t, tb):
                    dve.wait_ge(sem(f"maxima{L}"), 4 * t + 4)
                    dve.wait_ge(sem(f"negmax_transposed{L}"), count(t))
                    nm = negmax[:, tb, :]
                    nc.vector.tensor_copy(negp[:, 0, :], nm).then_inc(sem(f"negmax_split{L}"), 1)
                    dve.wait_ge(sem(f"negmax_split{L}"), 4 * t + 1)
                    nc.vector.tensor_tensor(negrest[:], nm, negp[:, 0, :], ALU.subtract).then_inc(sem(f"negmax_split{L}"), 1)
                    dve.wait_ge(sem(f"negmax_split{L}"), 4 * t + 2)
                    nc.vector.tensor_copy(negp[:, 1, :], negrest[:]).then_inc(sem(f"negmax_split{L}"), 1)
                    dve.wait_ge(sem(f"negmax_split{L}"), 4 * t + 3)
                    nc.vector.tensor_tensor(negp[:, 2, :], negrest[:], negp[:, 1, :], ALU.subtract).then_inc(sem(f"negmax_split{L}"), 1)

                def sum_pieces(t):
                    dve.wait_ge(sem(f"pv_done{L}"), count(4 * t))
                    nc.vector.tensor_reduce(osum[:], PVOUT[:, 0:HEADS * VP].rearrange("p (h c e) -> p h e c", c=3, e=VW),
                                            AX.X, ALU.add).then_inc(sem(f"pv_read{L}"), 1)

                def norm_out(t):
                    dve.wait_ge(sem(f"pv_read{L}"), t)
                    if L == 0:
                        dve.wait_ge(sem(f"out_transposed{L}"), count(t - 1))
                    nc.vector.reciprocal(rden[:], osum[:, :, DK:VW].rearrange("p h o -> p (h o)")).then_inc(sem(f"out_norm{L}"), 1)
                    dve.wait_ge(sem(f"out_norm{L}"), NORM * (t - 1) + 1)
                    nc.vector.tensor_tensor(onorm[:].rearrange("p (h d) -> p h d", d=DK), osum[:, :, 0:DK],
                                                   rden[:].unsqueeze(2).broadcast_to([128, HEADS, DK]), ALU.mult).then_inc(sem(f"out_norm{L}"), 1)
                    dve.wait_ge(sem(f"out_norm{L}"), NORM * (t - 1) + 2)
                    if L:
                        nc.vector.bn_stats(ostat[:], onorm[:]).then_inc(sem(f"out_norm{L}"), 1)
                        dve.wait_ge(sem(f"out_norm{L}"), NORM * (t - 1) + 3)
                        dve.sem_inc(sem("stats_seen"), 1)
                        nc.vector.bn_aggr(omv[:], ostat[:]).then_inc(sem(f"out_norm{L}"), 1)
                        dve.wait_ge(sem(f"out_norm{L}"), NORM * (t - 1) + 4)

                def centre_out(t):
                    dve.wait_ge(sem("out_rstd"), count(2 * t))
                    dve.wait_ge(sem(f"out_transposed{L}"), count(t - 1))
                    nc.vector.tensor_scalar(oln[:], onorm[:], omv[:, 0:1], orstd[:], ALU.subtract, ALU.mult
                                            ).then_inc(sem("out_centred"), 1)

                def low(t, c):
                    dve.wait_ge(sem(f"exp_done{L}"), count(2 * (4 * t + c + 1)))
                    dve.wait_ge(sem(f"pv_done{L}"), count(4 * t + c - 3))
                    nc.vector.tensor_tensor(Pl[:, c, :], P32[:, c, :], Ph[:, c, :], ALU.subtract).then_inc(sem(f"low_odd{L}"), 1)

                def add_out(t, j):
                    m = MISC[1 if j % 2 == 0 else 2]
                    dve.wait_ge(sem(f"out_projected{L}"), count(t))
                    x = X[:, t - 1, :] if isinstance(t, int) else X[:, bass.ds(t - 1, 1), :].rearrange("p o d -> p (o d)")
                    if L == 0:
                        nc.vector.tensor_copy(proj[:], m[:, 0:128]).then_inc(sem(f"attn_added{L}"), 1)
                    else:
                        nc.vector.tensor_tensor(proj[:], m[:, 0:128], rowsb[:, 1, :], ALU.add).then_inc(sem(f"attn_added{L}"), 1)
                    dve.wait_ge(sem(f"attn_added{L}"), 2 * (t - 1) + 1)
                    nc.vector.tensor_tensor(x, x, proj[:], ALU.add).then_inc(sem(f"attn_added{L}"), 1)

                for p in range(2):
                    x_stats(p)
                    x_apply(p)
                    if L == 0:
                        rotate(p, 0)
                        rotate(p, 1)
                    else:
                        make_mask(2 * p)
                split_v(0, 0)
                for c in range(QUARTERS):
                    maxima(0, c, 0)
                split_max(0, 0)

                def step(t, j):
                    first = isinstance(t, int) and t == 0
                    ahead = not (isinstance(t, int) and t + 1 >= B)
                    ntb = (j + 1) % 2
                    if not first:
                        sum_pieces(t)
                    if ahead:
                        maxima(t + 1, 0, ntb)
                    if not first:
                        norm_out(t)
                    if j % 2 == 0 and not (isinstance(t, int) and t + 4 >= B):
                        x_stats(pair(j) + 2)
                    if ahead:
                        maxima(t + 1, 1, ntb)
                    low(t, 1)
                    if L and not first:
                        centre_out(t)
                    if ahead:
                        maxima(t + 1, 2, ntb)
                        maxima(t + 1, 3, ntb)
                        split_max(t + 1, ntb)
                    low(t, 3)
                    if j % 2 == 0:
                        if not (isinstance(t, int) and t + 4 >= B):
                            x_apply(pair(j) + 2)
                    else:
                        if not (isinstance(t, int) and t + 3 >= B):
                            if L == 0:
                                rotate(pair(j) + 2, 0)
                                rotate(pair(j) + 2, 1)
                            else:
                                dve.wait_ge(sem(f"scoresT_ready{L}"), count(4 * t + 4))
                                make_mask(j + 3)
                        if ahead:
                            split_v(pair(j) + 1, (j + 1) % BODY)
                    if not first:
                        add_out(t, j)

                body_loop(dve, step)
                sum_pieces(B)
                norm_out(B)
                if L:
                    centre_out(B)
                add_out(B, 0)

            def ffn():
                def norm(p):
                    src = ((lambda i: X[:, 2 * p + i, :]) if isinstance(p, int) else
                           (lambda i: X[:, bass.ds(p * 2 + i, 1), :].rearrange("p o d -> p (o d)")))
                    norm_stats("f_xn_ready", p, 2, src, stats, mv)
                    dve.wait_ge(sem("f_transposed"), count(p))
                    norm_apply("f_xn_ready", p, 2, src, mv, rstd, lambda i: fxn[:, i, :])

                def add(p):
                    for h in range(2):
                        dve.wait_ge(sem("f_down"), count(2 * p + h + 1))
                        x = X[:, p * 2 + h, :] if isinstance(p, int) else X[:, bass.ds(p * 2 + h, 1), :].rearrange("p o d -> p (o d)")
                        nc.vector.tensor_tensor(tmp[:, h, :], bank[6 + h][:, 0:128], rowsb[:, 2, :], ALU.add).then_inc(sem("f_bank_read"), 1)
                        dve.wait_ge(sem("f_bank_read"), 2 * p + h + 1)
                        nc.vector.tensor_tensor(x, x, tmp[:, h, :], ALU.add).then_inc(sem("f_added"), 1)

                dve.wait_ge(sem("attn_added0"), 2 * B)
                norm(0)
                norm(1)
                norm(2)
                with dve.Fori(0, PAIRS - 3) as p:
                    norm(p + 3)
                    add(p)
                for p in range(PAIRS - 3, PAIRS):
                    add(p)
                dve.wait_ge(sem("f_added"), 2 * PAIRS)

            def moe():
                dve.wait_ge(sem("attn_added1"), 2 * B)
                for g in range(B // 4):
                    dve.wait_ge(sem("m_transposed"), count(g))
                    norm_stats("m_xn_ready", g, 4, lambda i: X[:, 4 * g + i, :], mst, mmv)
                    norm_apply("m_xn_ready", g, 4, lambda i: X[:, 4 * g + i, :], mmv, mrs, lambda i: mxn[:, i, :])
                    dve.wait_ge(sem("m_logits"), count(g + 1))
                    nc.vector.tensor_copy(lg[:], bank[0][:, 0:4 * EXPERTS].rearrange("p (h e) -> p h e", h=4)).then_inc(sem("m_gate"), 1)
                    dve.wait_ge(sem("m_gate"), 8 * g + 1)
                    nc.vector.tensor_reduce(gs[:, :, 0:1], lg[:], AX.X, ALU.max, negate=True).then_inc(sem("m_maxed"), 1)
                    dve.wait_ge(sem("m_maxed"), count(g + 1))
                    dve.wait_ge(sem("m_exp"), count(4 * (g + 1)))
                    nc.vector.reciprocal(gs[:, :, 2:3], gs[:, :, 1:2]).then_inc(sem("m_gate"), 1)
                    dve.wait_ge(sem("m_gate"), 8 * g + 2)
                    nc.vector.tensor_scalar(gs[:, :, 3:4], gs[:, :, 0:1], -1.0, None, ALU.mult).then_inc(sem("m_gate"), 1)
                    dve.wait_ge(sem("m_gate"), 8 * g + 3)
                    nc.vector.tensor_tensor(wt[:], lg[:], gs[:, :, 3:4].broadcast_to([128, 4, EXPERTS]), ALU.is_ge).then_inc(sem("m_gate"), 1)
                    dve.wait_ge(sem("m_gate"), 8 * g + 4)
                    nc.vector.tensor_tensor(wt[:], wt[:], rank[:].unsqueeze(1).broadcast_to([128, 4, EXPERTS]), ALU.mult).then_inc(sem("m_gate"), 1)
                    dve.wait_ge(sem("m_gate"), 8 * g + 5)
                    nc.vector.tensor_reduce(gs[:, :, 3:4], wt[:], AX.X, ALU.max).then_inc(sem("m_gate"), 1)
                    dve.wait_ge(sem("m_gate"), 8 * g + 6)
                    nc.vector.tensor_tensor(wt[:], rank[:].unsqueeze(1).broadcast_to([128, 4, EXPERTS]),
                                                   gs[:, :, 3:4].broadcast_to([128, 4, EXPERTS]), ALU.is_equal).then_inc(sem("m_gate"), 1)
                    dve.wait_ge(sem("m_gate"), 8 * g + 7)
                    nc.vector.tensor_tensor(wt[:], wt[:], gs[:, :, 2:3].broadcast_to([128, 4, EXPERTS]), ALU.mult).then_inc(sem("m_gate"), 1)
                    dve.wait_ge(sem("m_gate"), 8 * (g + 1))
                    for e in range(EXPERTS):
                        for h in range(4):
                            n = (g * EXPERTS + e) * 4 + h
                            dve.wait_ge(sem("m_down"), count(n + 1))
                            nc.vector.tensor_tensor(my[:, h % 2, :], bank[6 + h % 2][:, 0:128], M2b[:, e, :], ALU.add).then_inc(sem("m_bank_read"), 1)
                            dve.wait_ge(sem("m_bank_read"), n + 1)
                            dve.wait_ge(sem("m_acc"), count(2 * (n - 3) - 64 * 0 if n >= 4 else 0))
                            if e == 0:
                                nc.vector.tensor_scalar(macc[:, h, :], my[:, h % 2, :], wt[:, h, e:e + 1], None, ALU.mult).then_inc(sem("m_acc"), 2)
                            else:
                                nc.vector.scalar_tensor_tensor(macc[:, h, :], my[:, h % 2, :], wt[:, h, e:e + 1], macc[:, h, :],
                                                               ALU.mult, ALU.add).then_inc(sem("m_acc"), 2)
                    dve.wait_ge(sem("m_acc"), 64 * (g + 1))
                    nc.vector.tensor_tensor(X[:, 4 * g:4 * g + 4, :], X[:, 4 * g:4 * g + 4, :], macc[:], ALU.add).then_inc(sem("out_ready"), 1)

            attention(0)
            ffn()
            attention(1)
            moe()


def rope_tables():
    inv = (1.0 / np.power(np.float32(10000.0), np.arange(0, DK, 2, dtype=np.float32) / np.float32(DK))).astype(np.float32)
    f = np.outer(np.arange(S, dtype=np.float32), inv).astype(np.float32)
    c, s = np.cos(f).astype(np.float32), np.sin(f).astype(np.float32)
    cosT = np.zeros((DK, HEADS, S), np.float32)
    sinT = np.zeros((DK, HEADS, S), np.float32)
    for i in range(DK // 2):
        cosT[2 * i] = cosT[2 * i + 1] = c[:, i]
        sinT[2 * i] = -s[:, i]
        sinT[2 * i + 1] = s[:, i]
    return cosT.reshape(128, S), sinT.reshape(128, S)


def by_component(heads):
    return np.arange(heads * DK).reshape(heads, DK).T.reshape(-1)


def kernel(**inputs):
    import ml_dtypes
    import concourse.bacc as bacc
    from concourse.bass_utils import run_bass_kernel_spmd

    g = {k: np.asarray(v) for k, v in inputs.items()}
    order = by_component(HEADS)
    order1 = by_component(KV1)
    swap = order ^ 1
    wq, wk = g["L0_xattn_Wq"], g["L0_xattn_Wk"]
    cosT, sinT = rope_tables()
    cols = np.zeros((128, 4), np.float32)
    cols[:, 0] = g["L1_xattn_bq"][order]
    cols[0:32, 1] = g["L1_xattn_bk"][order1]
    cols[:, 2] = g["L1_xattn_ln_g"]
    cols[:, 3] = g["L1_xattn_ln_b"]
    arrays = {
        "x": g["x"], "ctxT": g["ctx_1024"].reshape(B * S, D).T, "mask": g["mask_BxSxS2_ik1"],
        "W0": np.stack([wq[order].T, wq[swap].T, wk[order].T, wk[swap].T, g["L0_xattn_Wv"].T, g["L0_xattn_Wo"].T]),
        "cosT": cosT, "sinT": sinT, "eye": np.eye(128, dtype=np.float32),
        "eyeb": np.eye(128).astype(ml_dtypes.bfloat16),
        "negI": (np.eye(128) * MASKED).astype(ml_dtypes.bfloat16),
        "upper": np.triu(np.ones((128, 128)), 1).astype(ml_dtypes.bfloat16),
        "W1Q": g["L1_xattn_Wq"][order].T, "W1K": g["L1_xattn_Wk"][order1].T, "W1V": g["L1_xattn_Wv"].T, "W1O": g["L1_xattn_Wo"].T,
        "cols": cols, "bv": g["L1_xattn_bv"], "bo": g["L1_xattn_bo"], "b2": g["L0_ffn_b2"],
        "F1": g["L0_ffn_W1"].T, "F1b": g["L0_ffn_b1"].reshape(FC, 128).T, "F2": g["L0_ffn_W2"].T,
        "WG": g["L1_ffn_wg_red"].T, "wg": g["L1_ffn_wg"],
        "rank": (EXPERTS - np.arange(EXPERTS)).astype(np.float32),
        "M1": g["L1_ffn_w1"], "M1b": g["L1_ffn_b1"].reshape(EXPERTS, FC, 128).transpose(2, 0, 1), "M2": g["L1_ffn_w2"], "M2b": g["L1_ffn_b2"],
    }
    nc = bacc.Bacc("TRN2", target_bir_lowering=False, num_devices=1)
    feeds, aps = {}, {}
    for name, v in arrays.items():
        v = np.ascontiguousarray(v)
        feeds[f"in_{name}"] = v
        aps[name] = nc.dram_tensor(f"in_{name}", v.shape, mybir.dt.from_np(v.dtype), kind="ExternalInput").ap()
    out = nc.dram_tensor("out_0", (B, S, D), F32, kind="ExternalOutput").ap()
    build(nc, aps, out)
    r = run_bass_kernel_spmd(nc, [feeds], core_ids=[0])
    return r.results[0]["out_0"]
```

```python
from contextlib import ExitStack

import numpy as np

import concourse.bass as bass
from concourse import mybir

ALU = mybir.AluOpType
ACT = mybir.ActivationFunctionType
AX = mybir.AxisListType
F32 = mybir.dt.float32
BF16 = mybir.dt.bfloat16
F16 = mybir.dt.float16
I32 = mybir.dt.int32

B, S, D = 32, 128, 128
HEADS, DK = 16, 8
KV1 = 4
FF = 512
FC = FF // 128
EXPERTS, GATE = 8, 16
QUARTERS = 4
HQ = HEADS // QUARTERS
PAIR = 2 * S
PAIRS = B // 2
BODY = 6
AHEAD = 8
NB = (B - AHEAD) // BODY
QSLOT = (0, 0, 1, 0, 1, 2)
KSLOT = (0, 1, 0, 2, 1, 0)
SLOTS = len(QSLOT)
TERMS = 96
ROWS = TERMS + 3
VW = DK + 1
VP = 3 * VW
SCALE = float(1.0 / np.sqrt(np.float32(DK)))
MASKED = -float(2.0 ** 100)
LN_EPS = 1e-5
RW = 2 * D + 4
SCORE_AT, TOKEN_AT = 2 * D, 2 * D + 1
TOKENS = B * S
BLOCKS = B + EXPERTS - 1
TURNS = 3
BIG_ROUND = 12582912.0


def build(nc, a, out):
    ctx = ExitStack()
    with ctx:
        def sb(name, shape, dt=F32):
            return ctx.enter_context(nc.sbuf_tensor(name, shape, dt))

        sems = {}

        def sem(name):
            if name not in sems:
                sems[name] = ctx.enter_context(nc.semaphore(name))
            return sems[name]

        def count(value):
            return max(value, 0) if isinstance(value, int) else value

        bank = [ctx.enter_context(nc.psum_tensor(f"bank{i}", [128, 512], F32)) for i in range(8)]
        SCORE = bank[0:2]
        SCORET = bank[2:4]
        PVOUT = bank[4]
        MISC = bank[5:8]
        MAXT = bank[7][:, 256:320].bitcast(BF16)
        XNT, VAL = bank[5][:, 0:PAIR], bank[5][:, PAIR:2 * PAIR]
        QK = bank[6]
        OUTT, OUTP = bank[7][:, 0:128], bank[7][:, 128:256]

        XR = sb("XR", [128, B, RW])
        X = XR[:, :, D:2 * D]
        eye = sb("eye", [128, 128])
        eyeb = sb("eyeb", [128, 128], BF16)
        ones = sb("ones", [128, 128])
        negI = sb("negI", [128, 128], BF16)
        upper = sb("upper", [128, 128], BF16)
        cosT = sb("cosT", [128, 128])
        sinT = sb("sinT", [128, 128])
        W0 = sb("W0", [128, 6, 128])
        W1Q = sb("W1Q", [128, 128])
        W1K = sb("W1K", [128, 32])
        W1V = sb("W1V", [128, 32])
        W1O = sb("W1O", [128, 128])
        cols = sb("cols", [128, 8])
        rowsb = sb("rowsb", [128, 3, 128])
        F1 = sb("F1", [128, FF])
        F1b = sb("F1b", [128, FC])
        F2 = sb("F2", [128, FC, 128])
        WG = sb("WG", [128, GATE])
        wgr = sb("wgr", [EXPERTS, GATE])
        M1 = sb("M1", [128, EXPERTS, FF])
        M2 = sb("M2", [128, EXPERTS, FC, 128])
        M2b = sb("M2b", [128, EXPERTS, 128])
        rank = sb("rank", [128, EXPERTS])

        ctxT = [sb(f"ctxT{i}", [128, PAIR]) for i in range(3)]
        adj = [sb(f"adj{i}", [128, 2, 128], I32) for i in range(3)]
        mask = sb("mask", [128, BODY, 128], BF16)
        stats = sb("stats", [128, 2, 6])
        mv = sb("mv", [128, 2, 2])
        rstd = sb("rstd", [128, 2])
        powers = sb("powers", [128, 9])
        xn = sb("xn", [128, 2, 128])
        xnT = sb("xnT", [128, PAIR])
        shift = sb("shift", [128, 2])
        rotA = [sb(f"rotA{i}", [128, PAIR]) for i in range(2)]
        rotB = [sb(f"rotB{i}", [128, PAIR]) for i in range(2)]
        full = [sb(f"full{i}", [128, PAIR]) for i in range(2)]
        rest = [sb(f"rest{i}", [128, PAIR]) for i in range(2)]
        piece = [sb(f"piece{i}", [128, 3, PAIR], BF16) for i in range(2)]
        Qs = [sb(f"Qs{i}", [128, HEADS, PAIR], BF16) for i in range(2)]
        Ks = [sb(f"Ks{i}", [128, HEADS, PAIR], BF16) for i in range(2)]
        M1b = sb("M1b", [128, EXPERTS, FF])
        third = M1b[:].rearrange("p e n -> p (e n)").bitcast(BF16).rearrange("p (i h s) -> p i h s", i=2, h=HEADS)
        Qs = Qs + [third[:, 0]]
        Ks = Ks + [third[:, 1]]
        vfull = sb("vfull", [128, 2, 128])
        vrest = sb("vrest", [128, 2, 128])
        Vp = sb("Vp", [128, BODY, HEADS, 3, VW], BF16)
        negmax = sb("negmax", [128, 2, HEADS])
        negrest = sb("negrest", [128, HEADS])
        negp = sb("negp", [128, 8, HEADS], BF16)
        negpT = [sb(f"negpT{i}", [3 * HEADS, 128], BF16) for i in range(2)]
        P32 = sb("P32", [128, QUARTERS, 512])
        Ph = sb("Ph", [128, QUARTERS, 512], F16)
        Pl = sb("Pl", [128, QUARTERS, 512], F16)
        osum = sb("osum", [128, HEADS, VW])
        rden = sb("rden", [128, HEADS])
        onorm = sb("onorm", [128, 128])
        ostat = sb("ostat", [128, 6])
        omv = sb("omv", [128, 2])
        orstd = sb("orstd", [128, 1])
        oln = sb("oln", [128, 128])
        oT = sb("oT", [128, 128])

        fxn = sb("fxn", [128, 2, 128])
        fxnT = sb("fxnT", [128, 2, PAIR])
        hT = sb("hT", [128, 2, FC, PAIR])
        tmp = sb("tmp", [128, 2, 128])
        qred = sb("qred", [128, 2])
        qgam = sb("qgam", [128, 2])

        def carve(tile, *widths):
            flat = tile[:].rearrange("p h s -> p (h s)").bitcast(F32)
            ends_ = np.cumsum(widths)
            assert ends_[-1] <= flat.shape[1]
            return [flat[:, int(e - w):int(e)] for e, w in zip(ends_, widths)]

        *bh0, mxT0 = carve(Qs[0], FF, FF, FF, 512)
        *bh, mxT1 = carve(Qs[1], FF, FF, FF, 512)
        *bhT, by0 = carve(Ks[0], FF, FF, FF, D)
        views = carve(Ks[1], *[D] * TURNS, *[RW - D] * TURNS, *[128] * TURNS, *[D] * TURNS)
        XA, XB, bxT, by = (views[i * TURNS:(i + 1) * TURNS] for i in range(4))
        mxT = [mxT0, mxT1]
        xrT = [sb(f"xrT{i}", [GATE, 512]) for i in range(2)]
        wgT = sb("wgT", [GATE, EXPERTS])
        wgn = sb("wgn", [EXPERTS, 3])
        wgs = sb("wgs", [EXPERTS, 2, GATE])
        mst = [sb(f"mst{i}", [128, 4, 6]) for i in range(2)]
        mmv = [sb(f"mmv{i}", [128, 4, 2]) for i in range(2)]
        mrs = [sb(f"mrs{i}", [128, 4]) for i in range(2)]
        lg = sb("lg", [128, B, EXPERTS])
        ex = sb("ex", [128, B, EXPERTS])
        cand = sb("cand", [128, B, EXPERTS])
        chosen = sb("chosen", [128, B, EXPERTS], BF16)
        top = sb("top", [128, 3, B])
        cnt = sb("cnt", [128, EXPERTS, B])
        cum = sb("cum", [128, EXPERTS, B])
        place = sb("place", [128, 2, EXPERTS * B])
        zero = sb("zero", [128, EXPERTS * B])
        ends = sb("ends", [128, 4, EXPERTS + 1])
        slot = sb("slot", [128, B])
        sloti = sb("sloti", [128, B], I32)
        blk = sb("blk", [1, BLOCKS])
        blkge = sb("blkge", [1, BLOCKS, EXPERTS - 1])
        expf = sb("expf", [1, BLOCKS])
        expert = sb("expert", [1, BLOCKS], I32)
        before = sb("before", [128, 128], BF16)
        onesb = sb("onesb", [128, 128], BF16)
        rows_d = nc.dram_tensor("expert_rows", [BLOCKS * 128, RW], F32, kind="Internal").ap()

        xd = a["x"].rearrange("b s d -> s b d")
        maskd = a["mask"].rearrange("b q k -> q b k")
        ctxd = a["ctxT"]

        first_loads = [
            (eye[:], a["eye"]), (wgr[:], a["wg"]), (F1[:], a["F1"]), (F2[:], a["F2"].rearrange("(c p) n -> p c n", p=128)),
        ]
        attention_loads = [
            (W0[:], a["W0"].rearrange("n e m -> e n m")), (cosT[:], a["cosT"]), (sinT[:], a["sinT"]),
            (eyeb[:], a["eyeb"]), (negI[:], a["negI"]), (upper[:], a["upper"]),
            (W1Q[:], a["W1Q"]), (W1K[:], a["W1K"]), (W1V[:], a["W1V"]), (W1O[:], a["W1O"]),
            (cols[:, 0:4], a["cols"]),
            (rowsb[:, 0, 0:32], a["bv"].partition_broadcast(128)),
            (rowsb[:, 1, :], a["bo"].partition_broadcast(128)),
            (rowsb[:, 2, :], a["b2"].partition_broadcast(128)),
            (F1b[:], a["F1b"]), (WG[:], a["WG"]), (rank[:], a["rank"].partition_broadcast(128)),
            (before[:], a["before"]), (blk[:], a["blk"].rearrange("(o n) -> o n", o=1)),
        ]
        expert_loads = [
            (M2b[:].rearrange("p e n -> p (e n)"), a["M2b"].rearrange("e n -> (e n)").partition_broadcast(128)),
            (M1[:], a["M1"].rearrange("e p n -> p e n")),
            (M2[:], a["M2"].rearrange("e (c p) n -> p e c n", p=128)),
        ]
        X_CHUNKS = 4
        FIRST_LOADED, LOADED, EXPERTS_LOADED = 16 * len(first_loads), 16 * len(attention_loads), 16 * (len(expert_loads) + 1)

        body = {}

        def body_loop(eng, step):
            def run(t):
                body["i"] = t // BODY
                step(t, t % BODY)

            for t in range(-AHEAD, BODY):
                run(t)
            with eng.Fori(1, NB) as i:
                body["i"] = i
                for j in range(BODY):
                    step(i * BODY + j, j)
            for t in range(NB * BODY, B + 3):
                run(t)

        def is_batch(t):
            return not isinstance(t, int) or 0 <= t < B

        def is_pair(p):
            return not isinstance(p, int) or 0 <= p < PAIRS

        def pair(k):
            return body["i"] * (BODY // 2) + k // 2

        def turn(k):
            return k // 2 % 3

        def turns(k):
            return body["i"] + k // BODY + 1

        def block_loop(eng, step, first, end):
            for j in range(first, 2 * TURNS):
                step(j, j % TURNS, j // TURNS + 1)
            with eng.Fori(2, BLOCKS // TURNS - 1) as i:
                for r in range(TURNS):
                    step(i * TURNS + r, r, i + 1)
            for j in range(BLOCKS - TURNS, end):
                step(j, j % TURNS, j // TURNS + 1)

        block = ctx.enter_context(nc.Block())

        @block.sync
        def _(sp):
            for dst, src in first_loads:
                sp.dma_start(dst, src).then_inc(sem("first_loaded"), 16)
            for c in range(X_CHUNKS):
                w = B // X_CHUNKS
                sp.dma_start(X[:, c * w:(c + 1) * w, :], xd[:, c * w:(c + 1) * w, :]).then_inc(sem(f"x_loaded{c}"), 16)
                if c == 0:
                    for dst, src in attention_loads:
                        sp.dma_start(dst, src).then_inc(sem("weights_loaded"), 16)

            def attention(L):
                T0, P0 = L * B, L * PAIRS
                n_kv = (HEADS, KV1)[L]

                def known(value):
                    return value if isinstance(value, int) else sp.snap(value)

                def load_ctx(k):
                    p, b = pair(k), turn(k)
                    if is_pair(p):
                        read, column = known(p + P0 - 2), known(p * PAIR)
                        sp.wait_ge(sem("v_projected"), count(read))
                        sp.dma_start(ctxT[b][:], ctxd[:, bass.ds(column, PAIR)]).then_inc(sem(f"ctx_loaded{L}{b}"), 16)

                def load_adj(k):
                    p, b = pair(k), turn(k)
                    if is_pair(p):
                        made, row = known(p - 2), known(p * 2)
                        sp.wait_ge(sem("mask_made"), count(made))
                        sp.dma_start(adj[b][:], maskd[:, bass.ds(row, 2), :]).then_inc(sem(f"adj_loaded{b}"), 16)

                def stack_q(k):
                    p, b = pair(k), turn(k)
                    if is_pair(p):
                        read, cut = known(8 * (p + P0 - 2)), known(3 * (p + P0) + 3)
                        sp.wait_ge(sem("scoresT_ready"), count(read))
                        sp.wait_ge(sem("q_pieces"), cut)
                        for s in range(SLOTS):
                            sp.dma_start(Qs[b][s * DK:(s + 1) * DK, :, :],
                                         piece[0][:, QSLOT[s], :]).then_inc(sem(f"q_stacked{L}{b}"), 16)

                def stack_k(k):
                    p, b = pair(k), turn(k)
                    if is_pair(p):
                        cut = known(3 * (p + P0) + 3)
                        sp.wait_ge(sem("k_pieces"), cut)
                        for s in range(SLOTS):
                            sp.dma_start(Ks[b][s * DK:(s + 1) * DK, 0:n_kv, :],
                                         piece[1][0:n_kv * DK, KSLOT[s], :]).then_inc(sem(f"k_stacked{L}{b}"), 16)

                def max_rows(t, k):
                    if is_batch(t):
                        sp.wait_ge(sem("negmaxT_ready"), t + T0 + 1)
                        sp.dma_start(Qs[turn(k)][TERMS:ROWS, :, k % 2 * S:(k % 2 + 1) * S],
                                     negpT[k % 2][:]).then_inc(sem(f"max_rows{L}{k % 2}"), 16)

                def step(t, j):
                    if j % 2 == 0:
                        stack_q(j + 4)
                    else:
                        stack_k(j + 3)
                        load_ctx(j + 7)
                        if L:
                            load_adj(j + 5)
                    max_rows(t + 1, j + 1)

                body_loop(sp, step)

            sp.wait_ge(sem("stacks_cleared"), 6)
            attention(0)
            for dst, src in expert_loads:
                sp.dma_start(dst, src).then_inc(sem("experts_loaded"), 16)
            sp.wait_ge(sem("zeros_set"), 1)
            sp.dma_start(rows_d.rearrange("(n p) w -> p n w", p=128)[:, :, 0:2 * D],
                         zero[:].unsqueeze(1).broadcast_to([128, BLOCKS, 2 * D])).then_inc(sem("rows_blank"), 16)
            sp.dma_start(rows_d[:, 2 * D:RW], a["tails"]).then_inc(sem("rows_blank"), 16)
            attention(1)
            sp.wait_ge(sem("scoresT_ready"), 8 * B)
            sp.dma_start(M1b[:].rearrange("p e n -> p (e n)"), a["M1b"].rearrange("e n -> (e n)").partition_broadcast(128)
                         ).then_inc(sem("experts_loaded"), 16)

            def load_xn(j, r):
                ahead = j - TURNS + 1
                sp.wait_ge(sem("b_transposed"), count(ahead))
                sp.dma_start(XA[r], rows_d[bass.ds(j * 128, 128), 0:D]).then_inc(sem(f"xa_loaded{r}"), 16)

            def load_x(j, r, turn):
                sp.wait_ge(sem(f"gone_out{r}"), count(16 * (turn - 1)))
                sp.dma_start(XB[r], rows_d[bass.ds(j * 128, 128), D:RW]).then_inc(sem(f"xb_loaded{r}"), 16)

            sp.wait_ge(sem("scattered"), 16 * B)
            for j in range(TURNS):
                load_xn(j, j)

            def step(j, r, turn):
                if not isinstance(j, int) or j + TURNS < BLOCKS:
                    load_xn(j + TURNS, r)
                load_x(j, r, turn)

            block_loop(sp, step, 0, BLOCKS)

        @block.tensor
        def _(pe):
            pe.wait_ge(sem("first_loaded"), FIRST_LOADED)

            def quantize_sums():
                for i in range(2):
                    pe.wait_ge(sem("abs_summed"), count(i + 1))
                    nc.tensor.matmul(MISC[i][:, 0:1], ones[:], qred[:, i:i + 1], start=True, stop=True).then_inc(sem("abs_total"), 1)
                pe.wait_ge(sem("gate_unit"), count(5))
                nc.tensor.transpose(MISC[2][0:GATE, 0:EXPERTS], wgs[:, 1, :], eye[0:EXPERTS, 0:EXPERTS]).then_inc(sem("gate_T"), 1)
                pe.wait_ge(sem("quantized"), 2)
                pe.wait_ge(sem("gate_unitT"), 1)

            quantize_sums()
            pe.wait_ge(sem("weights_loaded"), LOADED)

            def attention(L):
                T0, P0 = L * B, L * PAIRS
                n_kv = (HEADS, KV1)[L]
                m = n_kv * DK
                WQ, WK, WV, WO = ((W0[:, 0, :], W0[:, 2, :], W0[:, 4, :], W0[:, 5, :]) if L == 0 else
                                  (W1Q[:], W1K[:], W1V[:], W1O[:]))

                def xn_transposes(k):
                    p = pair(k)
                    if is_pair(p):
                        pe.wait_ge(sem("xn_ready"), 2 * (p + P0) + 2)
                        pe.wait_ge(sem("v_high"), count((p + P0) - 1))
                        for b in range(2):
                            mm = nc.tensor.transpose(XNT[:, b * S:(b + 1) * S], xn[:, b, :], eye[:])
                        mm.then_inc(sem("xn_transposed"), 1)

                def project_q(k):
                    p = pair(k)
                    if is_pair(p):
                        pe.wait_ge(sem("xnT_ready"), p + P0 + 1)
                        pe.wait_ge(sem("k_bank_read"), count(p + P0))
                        mm = nc.tensor.matmul(QK[:, 0:PAIR], WQ, xnT[:], start=True, stop=True)
                        if L == 0:
                            mm = nc.tensor.matmul(QK[:, PAIR:2 * PAIR], W0[:, 1, :], xnT[:], start=True, stop=True)
                        mm.then_inc(sem("q_projected"), 1)

                def project_k(k):
                    p, b = pair(k), turn(k)
                    if is_pair(p):
                        pe.wait_ge(sem(f"ctx_loaded{L}{b}"), 16 * turns(k))
                        pe.wait_ge(sem("q_bank_read"), p + P0 + 1)
                        mm = nc.tensor.matmul(QK[0:m, 0:PAIR], WK, ctxT[b][:], start=True, stop=True)
                        if L == 0:
                            mm = nc.tensor.matmul(QK[:, PAIR:2 * PAIR], W0[:, 3, :], ctxT[b][:], start=True, stop=True)
                        mm.then_inc(sem("k_projected"), 1)

                def project_v(k):
                    p, b = pair(k), turn(k)
                    if is_pair(p):
                        pe.wait_ge(sem("v_high"), count(p + P0))
                        for h in range(2):
                            o = VAL[:, h * 128:h * 128 + m]
                            mm = nc.tensor.matmul(o, ctxT[b][:, h * S:(h + 1) * S], WV, start=True, stop=(L == 0))
                            if L:
                                mm = nc.tensor.matmul(o, ones[0:1, :], rowsb[0:1, 0, 0:m], start=False, stop=True)
                        mm.then_inc(sem("v_projected"), 1)

                def scores(t, c, k):
                    if not is_batch(t):
                        return
                    pb, tb = turn(k), k % 2
                    if c == 0:
                        pe.wait_ge(sem(f"q_stacked{L}{pb}"), 16 * SLOTS * turns(k))
                        pe.wait_ge(sem(f"k_stacked{L}{pb}"), 16 * SLOTS * turns(k))
                        if L:
                            pe.wait_ge(sem("mask_made"), pair(k) + 1)
                    pe.wait_ge(sem("maxima"), count(4 * (t + T0) + c - 1))
                    o = SCORE[c % 2]
                    if L:
                        nc.tensor.matmul(o[:].rearrange("p (h k) -> p h k", h=HQ), negI[:],
                                         mask[:, k % BODY, :].unsqueeze(1).broadcast_to([128, HQ, 128]),
                                         start=True, stop=False, skip_group_check=True)
                    for i in range(HQ):
                        h = c * HQ + i
                        kv = h if L == 0 else c
                        mm = nc.tensor.matmul(o[:, i * 128:(i + 1) * 128], Qs[pb][0:TERMS, h, tb * S:(tb + 1) * S],
                                              Ks[pb][0:TERMS, kv, tb * S:(tb + 1) * S],
                                              start=(L == 0), stop=True, skip_group_check=bool(L))
                    mm.then_inc(sem("scores_ready"), 1)

                def scoresT(t, c, k):
                    if not is_batch(t):
                        return
                    pb, tb = turn(k), k % 2
                    if c == 0:
                        pe.wait_ge(sem(f"max_rows{L}{tb}"), 16 * (pair(k) + 1))
                    pe.wait_ge(sem("exp_done"), count(2 * (4 * (t + T0) + c - 1)))
                    o = SCORET[c % 2]
                    if L:
                        nc.tensor.matmul(o[:].rearrange("p (h q) -> p h q", h=HQ), mask[:, k % BODY, :],
                                         negI[:].unsqueeze(1).broadcast_to([128, HQ, 128]),
                                         start=True, stop=False, skip_group_check=True)
                        mm = nc.tensor.matmul(o[:].rearrange("p (h q) -> p h q", h=HQ), Ks[pb][0:ROWS, c, tb * S:(tb + 1) * S],
                                              Qs[pb][0:ROWS, c * HQ:(c + 1) * HQ, tb * S:(tb + 1) * S],
                                              start=False, stop=True, skip_group_check=True)
                    else:
                        for i in range(HQ):
                            h = c * HQ + i
                            mm = nc.tensor.matmul(o[:, i * 128:(i + 1) * 128], Ks[pb][0:ROWS, h, tb * S:(tb + 1) * S],
                                                  Qs[pb][0:ROWS, h, tb * S:(tb + 1) * S], start=True, stop=True)
                    mm.then_inc(sem("scoresT_ready"), 1)

                def pv(t, c, k):
                    if not is_batch(t):
                        return
                    if c == 0:
                        pe.wait_ge(sem("pv_read"), count(t + T0))
                        pe.wait_ge(sem("v_split"), (pair(k) + P0) + 1)
                    if c == 1:
                        pe.wait_ge(sem("lows_dve"), t + T0 + 1)
                    else:
                        pe.wait_ge(sem("lows_pool"), 3 * (t + T0) + (1, 1, 2, 3)[c])
                    pe.wait_ge(sem("exp_done"), 8 * (t + T0) + 2 * c + 2)
                    for i in range(HQ):
                        h = c * HQ + i
                        for n, p in enumerate((Ph, Pl)):
                            mm = nc.tensor.matmul(PVOUT[:, h * VP:(h + 1) * VP], p[:, c, i * 128:(i + 1) * 128],
                                                  Vp[:, k % BODY, h if L == 0 else c, :, :].rearrange("p c e -> p (c e)"),
                                                  start=(n == 0), stop=(n == 1))
                    mm.then_inc(sem("pv_done"), 1)

                def max_transpose(t):
                    pe.wait_ge(sem("attn_added"), count((t + T0) - 3))
                    if is_batch(t):
                        pe.wait_ge(sem("negmax_split"), 4 * (t + T0) + 4)
                        pe.wait_ge(sem("negmaxT_ready"), count(t + T0))
                        nc.tensor.transpose(MAXT, negp[:].rearrange("p c h -> p (c h)"),
                                            eyeb[:]).then_inc(sem("negmax_transposed"), 1)

                def out_transpose(t):
                    if is_batch(t):
                        if L == 0:
                            pe.wait_ge(sem("out_norm0"), 2 * t + 2)
                        else:
                            pe.wait_ge(sem("out_centred"), t + 1)
                        pe.wait_ge(sem("outT_ready"), count(t + T0))
                        nc.tensor.transpose(OUTT, (onorm if L == 0 else oln)[:], eye[:]).then_inc(sem("out_transposed"), 1)

                def out_project(t):
                    if is_batch(t):
                        if is_batch(t + 3):
                            pe.wait_ge(sem("negmaxT_ready"), t + T0 + 4)
                        pe.wait_ge(sem("outT_ready"), t + T0 + 1)
                        mm = nc.tensor.matmul(OUTP, oT[:], WO, start=True, stop=(L == 0))
                        if L:
                            mm = nc.tensor.matmul(OUTP, ones[0:1, :], rowsb[0:1, 1, :], start=False, stop=True)
                        mm.then_inc(sem("out_projected"), 1)

                def step(t, j):
                    scoresT(t, 0, j)
                    scores(t + 2, 0, j + 2)
                    pv(t - 1, 1, j - 1)
                    scoresT(t, 1, j)
                    scores(t + 2, 1, j + 2)
                    max_transpose(t + 1)
                    out_transpose(t - 2)
                    if j % 2 == 0:
                        xn_transposes(j + 6)
                    pv(t - 1, 2, j - 1)
                    scoresT(t, 2, j)
                    scores(t + 2, 2, j + 2)
                    pv(t - 1, 3, j - 1)
                    scoresT(t, 3, j)
                    scores(t + 2, 3, j + 2)
                    out_project(t - 2)
                    if j % 2 == 0:
                        project_q(j + 6)
                        project_v(j + 4)
                    else:
                        project_k(j + 5)
                    pv(t, 0, j)

                body_loop(pe, step)
                pe.wait_ge(sem("attn_added"), B + T0)

            def ffn():
                def transposes(p, b):
                    pe.wait_ge(sem("f_xn_ready"), count(2 * (p + 1)))
                    pe.wait_ge(sem("f_xnT_ready"), count(p - 1))
                    for h in range(2):
                        mm = nc.tensor.transpose(bank[b][:, h * S:(h + 1) * S], fxn[:, h, :], eye[:])
                    mm.then_inc(sem("f_transposed"), 1)

                def up(p, b):
                    pe.wait_ge(sem("f_xnT_ready"), count(p + 1))
                    for c in range(FC):
                        pe.wait_ge(sem("f_relu"), count(FC * p + c - FC + 1))
                        nc.tensor.matmul(bank[2 + c][:, 0:PAIR], F1[:, c * 128:(c + 1) * 128], fxnT[:, b, :],
                                         start=True, stop=True).then_inc(sem("f_up"), 1)

                def down(p, b):
                    pe.wait_ge(sem("f_relu"), count(FC * (p + 1)))
                    for h in range(2):
                        pe.wait_ge(sem("f_bank_read"), count(2 * p + h - 1))
                        for c in range(FC):
                            mm = nc.tensor.matmul(bank[6 + h][:, 0:128], hT[:, b, c, h * S:(h + 1) * S], F2[:, c, :],
                                                  start=(c == 0), stop=(c == FC - 1))
                        mm.then_inc(sem("f_down"), 1)

                def step(p, b, last):
                    if last < 2:
                        transposes(p + 2, b)
                    if last < 1 or last == 2:
                        pass
                    if not last == 3:
                        up(p + 1, 1 - b)
                    down(p, b)

                transposes(0, 0)
                transposes(1, 1)
                up(0, 0)
                step(0, 0, 0)
                step(1, 1, 0)
                with pe.Fori(1, PAIRS // 2 - 1) as i:
                    for b in range(2):
                        step(i * 2 + b, b, 0)
                step(PAIRS - 2, 0, 2)
                step(PAIRS - 1, 1, 3)
                pe.wait_ge(sem("f_bank_read"), count(2 * PAIRS))

            def gate():
                G = B // 4

                def transposes(g):
                    pe.wait_ge(sem("m_xn_ready"), 4 * (g + 1))
                    pe.wait_ge(sem("m_xT_ready"), count(g - 1))
                    for h in range(4):
                        mm = nc.tensor.transpose(bank[g % 2][:, h * S:(h + 1) * S], XR[:, 4 * g + h, 0:D], eye[:])
                    mm.then_inc(sem("m_transposed"), 1)

                def reduced(g):
                    pe.wait_ge(sem("m_xT_ready"), g + 1)
                    pe.wait_ge(sem("m_reduced_read"), count(g - 1))
                    nc.tensor.matmul(bank[2 + g % 2][0:GATE, :], WG[:], mxT[g % 2], start=True, stop=True
                                     ).then_inc(sem("m_reduced"), 1)

                def logits(g):
                    pe.wait_ge(sem("m_reduced_read"), g + 1)
                    pe.wait_ge(sem("m_logits_read"), count(g - 1))
                    for h in range(4):
                        mm = nc.tensor.matmul(bank[4 + g % 2][:, h * EXPERTS:(h + 1) * EXPERTS],
                                              xrT[g % 2][:, h * S:(h + 1) * S], wgT[:], start=True, stop=True)
                    mm.then_inc(sem("m_logits"), 1)

                for g in range(G + 2):
                    if g < G:
                        transposes(g)
                    if 1 <= g <= G:
                        reduced(g - 1)
                    if g >= 2:
                        logits(g - 2)
                pe.wait_ge(sem("chosen_ready"), 1)
                oh = chosen[:].rearrange("p t e -> p (t e)")
                nc.tensor.matmul(bank[6][:, 0:B * EXPERTS], before[:], oh, start=True, stop=True).then_inc(sem("ranked"), 1)
                nc.tensor.matmul(bank[7][:, 0:B * EXPERTS], onesb[:], oh, start=True, stop=True).then_inc(sem("ranked"), 1)

            def experts():
                def step(j, r, turn):
                    n1, n2, p1 = (r + 1) % TURNS, (r + 2) % TURNS, (r - 1) % TURNS
                    if not isinstance(j, int) or j + 2 < BLOCKS:
                        pe.wait_ge(sem(f"xa_loaded{n2}"), 16 * (turn + (r + 2) // TURNS))
                        pe.wait_ge(sem("b_xT_ready"), count(j + 2))
                        nc.tensor.transpose(bank[0][:, 0:128], XA[n2], eye[:]).then_inc(sem("b_transposed"), 1)
                    if not isinstance(j, int) or 0 <= j + 1 < BLOCKS:
                        e = pe.value_load(expert[0:1, bass.ds(j + 1, 1)], min_val=0, max_val=EXPERTS - 1)
                        pe.wait_ge(sem("b_xT_ready"), count(j + 2))
                        pe.wait_ge(sem("b_biased"), count(j - 1))
                        nc.tensor.matmul(bank[1 + n1][:], bxT[n1], M1[:, bass.ds(e, 1), :].rearrange("p o n -> p (o n)"),
                                         start=True, stop=True).then_inc(sem("b_up"), 1)
                    if not isinstance(j, int) or 0 <= j < BLOCKS:
                        pe.wait_ge(sem("b_gelu"), count(j + 1))
                        pe.wait_ge(sem("b_hT_ready"), count(j - 2))
                        for c in range(FC):
                            mm = nc.tensor.transpose(bank[4 + r][:, c * 128:(c + 1) * 128], bh[r][:, c * 128:(c + 1) * 128], eye[:])
                        mm.then_inc(sem("b_h_transposed"), 1)
                    if not isinstance(j, int) or 0 <= j - 1 < BLOCKS:
                        e = pe.value_load(expert[0:1, bass.ds(j - 1, 1)], min_val=0, max_val=EXPERTS - 1)
                        pe.wait_ge(sem("b_hT_ready"), count(j))
                        pe.wait_ge(sem("b_y_read"), count(j - 1))
                        for c in range(FC):
                            mm = nc.tensor.matmul(bank[7][:, 0:D], bhT[p1][:, c * 128:(c + 1) * 128],
                                                  M2[:, bass.ds(e, 1), c, :].rearrange("p o n -> p (o n)"),
                                                  start=(c == 0), stop=(c == FC - 1))
                        mm.then_inc(sem("b_down"), 1)

                pe.wait_ge(sem("expert_ready"), 1)
                pe.wait_ge(sem("experts_loaded"), EXPERTS_LOADED)
                block_loop(pe, step, -2, BLOCKS + 1)

            attention(0)
            ffn()
            attention(1)
            gate()
            experts()

        @block.scalar
        def _(act):
            act.wait_ge(sem("weights_loaded"), LOADED)

            def attention(L):
                T0, P0 = L * B, L * PAIRS
                def evac_xnT(k):
                    p = pair(k)
                    if is_pair(p):
                        act.wait_ge(sem("xn_transposed"), p + P0 + 1)
                        act.wait_ge(sem("q_projected"), count(p + P0))
                        nc.scalar.copy(xnT[:], XNT).then_inc(sem("xnT_ready"), 1)

                def high(k, which):
                    p = pair(k)
                    if not is_pair(p):
                        return
                    m = 128 if L == 0 or which == 0 else KV1 * DK
                    nm = "qk"[which]
                    stacked = sem(f"{nm}_stacked{L}{turn(k - 2)}")
                    if L == 0:
                        act.wait_ge(sem(f"{nm}_full"), p + P0 + 1)
                        act.wait_ge(stacked, count(16 * SLOTS * turns(k - 2)))
                        nc.scalar.copy(piece[which][:, 0, :], full[which][:]).then_inc(sem(f"{nm}_high"), 1)
                    else:
                        act.wait_ge(sem(f"{nm}_projected"), p + P0 + 1)
                        act.wait_ge(sem(f"{nm}_pieces"), count(3 * (p + P0)))
                        src, bias = QK[0:m, 0:PAIR], cols[0:m, which:which + 1]
                        nc.scalar.activation(full[which][0:m, :], src, ACT.Identity, bias=bias).then_inc(sem(f"{nm}_full"), 1)
                        act.wait_ge(stacked, count(16 * SLOTS * turns(k - 2)))
                        nc.scalar.activation(piece[which][0:m, 0, :], src, ACT.Identity, bias=bias).then_inc(sem(f"{nm}_high"), 1)
                        act.wait_ge(sem(f"{nm}_high"), p + P0 + 1)
                        act.sem_inc(sem(f"{nm}_bank_read"), 1)

                def values(k):
                    p = pair(k)
                    if is_pair(p):
                        n_kv = (HEADS, KV1)[L]
                        src = VAL.rearrange("p (b n) -> p b n", b=2)[:, :, 0:n_kv * DK]
                        j = k % BODY
                        act.wait_ge(sem("v_projected"), p + P0 + 1)
                        act.wait_ge(sem("v_split"), count(p + P0))
                        nc.scalar.copy(vfull[:, :, 0:n_kv * DK], src).then_inc(sem("v_full"), 1)
                        act.wait_ge(sem("pv_done"), count(8 * (p + P0) - 16))
                        nc.scalar.copy(Vp[:, j:j + 2, 0:n_kv, 0, 0:DK], src.rearrange("p b (h d) -> p b h d", d=DK)
                                       ).then_inc(sem("v_high"), 1)

                def exps(t, c):
                    if is_batch(t):
                        act.wait_ge(sem("scoresT_ready"), 4 * (t + T0) + c + 1)
                        act.wait_ge(sem("pv_done"), count(4 * (t + T0) + c - 3))
                        nc.scalar.activation(P32[:, c, :], SCORET[c % 2][:], ACT.Exp, scale=SCALE).then_inc(sem("exp_done"), 1)
                        nc.scalar.activation(Ph[:, c, :], SCORET[c % 2][:], ACT.Exp, scale=SCALE).then_inc(sem("exp_done"), 1)

                def evac_max(t, k):
                    if is_batch(t):
                        act.wait_ge(sem("negmax_transposed"), t + T0 + 1)
                        if is_batch(t - 3):
                            act.wait_ge(sem("out_transposed"), (t + T0) - 2)
                        act.wait_ge(sem(f"max_rows{L}{k % 2}"), count(16 * pair(k)))
                        nc.scalar.copy(negpT[k % 2][:], MAXT[0:3 * HEADS, :]).then_inc(sem("negmaxT_ready"), 1)

                def evac_out(t):
                    if is_batch(t):
                        act.wait_ge(sem("out_transposed"), t + T0 + 1)
                        act.wait_ge(sem("out_projected"), count(t + T0))
                        if L == 0:
                            nc.scalar.copy(oT[:], OUTT).then_inc(sem("outT_ready"), 1)
                        else:
                            nc.scalar.activation(oT[:], OUTT, ACT.Identity, bias=cols[:, 3:4], scale=cols[:, 2:3]
                                                 ).then_inc(sem("outT_ready"), 1)

                def normalise(k):
                    p = pair(k)
                    if is_pair(p):
                        act.wait_ge(sem("shifted"), 2 * (p + P0) + 2)
                        act.wait_ge(sem("xn_transposed"), count(p + P0))
                        for i in range(2):
                            x = X[:, 2 * p + i, :] if isinstance(p, int) else X[:, bass.ds(p * 2 + i, 1), :].rearrange("p o d -> p (o d)")
                            nc.scalar.activation(xn[:, i, :], x, ACT.Identity, bias=shift[:, i:i + 1], scale=rstd[:, i:i + 1]
                                                 ).then_inc(sem("xn_ready"), 1)

                def step(t, j):
                    if L:
                        if j % 2 == 0:
                            high(j + 4, 1)
                        else:
                            high(j + 5, 0)
                    exps(t, 0)
                    if j % 2 == 1:
                        values(j + 3)
                        normalise(j + 7)
                    exps(t, 1)
                    evac_max(t + 1, j + 1)
                    evac_out(t - 2)
                    if j % 2 == 0:
                        evac_xnT(j + 6)
                    if L == 0:
                        if j % 2 == 0:
                            high(j + 4, 1)
                        else:
                            high(j + 5, 0)
                    exps(t, 2)
                    exps(t, 3)

                body_loop(act, step)

            def ffn():
                def step(p, b):
                    act.wait_ge(sem("f_transposed"), count(p + 1))
                    act.wait_ge(sem("f_up"), count(FC * (p - 1)))
                    nc.scalar.copy(fxnT[:, b, :], bank[b][:, 0:PAIR]).then_inc(sem("f_xnT_ready"), 1)

                def relus(p, b):
                    for c in range(FC):
                        act.wait_ge(sem("f_up"), count(FC * p + c + 1))
                        act.wait_ge(sem("f_down"), count(2 * (p - 1)))
                        nc.scalar.activation(hT[:, b, c, :], bank[2 + c][:, 0:PAIR], ACT.Relu, bias=F1b[:, c:c + 1]
                                             ).then_inc(sem("f_relu"), 1)

                step(0, 0)
                step(1, 1)
                relus(0, 0)
                for b in range(2):
                    step(b + 2, b)
                    relus(b + 1, 1 - b)
                with act.Fori(1, PAIRS // 2 - 1) as i:
                    for b in range(2):
                        step(i * 2 + b + 2, b)
                        relus(i * 2 + b + 1, 1 - b)
                relus(PAIRS - 1, 1)

            def gate():
                G = B // 4
                for g in range(G + 1):
                    if g < G:
                        act.wait_ge(sem("m_transposed"), g + 1)
                        act.wait_ge(sem("m_reduced"), count(g - 1))
                        nc.scalar.copy(mxT[g % 2], bank[g % 2][:]).then_inc(sem("m_xT_ready"), 1)
                    if g >= 1:
                        act.wait_ge(sem("m_reduced"), g)
                        act.wait_ge(sem("m_logits"), count(g - 2))
                        nc.scalar.copy(xrT[(g - 1) % 2][:], bank[2 + (g - 1) % 2][0:GATE, :]).then_inc(sem("m_reduced_read"), 1)
                act.wait_ge(sem("logits_centred"), 1)
                nc.scalar.activation(ex[:], lg[:], ACT.Exp).then_inc(sem("gate_exp"), 1)

            def experts():
                def step(j, r, turn):
                    n1, n2 = (r + 1) % TURNS, (r + 2) % TURNS
                    if not isinstance(j, int) or j + 2 < BLOCKS:
                        act.wait_ge(sem("b_transposed"), count(j + 3))
                        act.wait_ge(sem("b_up"), count(j))
                        nc.scalar.copy(bxT[n2], bank[0][:, 0:128]).then_inc(sem("b_xT_ready"), 1)
                    if not isinstance(j, int) or 0 <= j + 1 < BLOCKS:
                        act.wait_ge(sem("b_biased"), count(j + 2))
                        act.wait_ge(sem("b_h_transposed"), count(j - 1))
                        nc.scalar.activation(bh[n1], bh0[n1], ACT.Gelu).then_inc(sem("b_gelu"), 1)
                    if not isinstance(j, int) or 0 <= j < BLOCKS:
                        act.wait_ge(sem("b_h_transposed"), count(j + 1))
                        act.wait_ge(sem("b_down"), count(j - 2))
                        nc.scalar.copy(bhT[r], bank[4 + r][:]).then_inc(sem("b_hT_ready"), 1)

                block_loop(act, step, -2, BLOCKS)

            attention(0)
            ffn()
            attention(1)
            gate()
            experts()

        @block.gpsimd
        def _(pool):
            nc.gpsimd.memset(powers[:, 0:4], -0.5).then_inc(sem("powers_set"), 1)
            nc.gpsimd.memset(powers[:, 4:5], 0.5).then_inc(sem("powers_set"), 1)
            nc.gpsimd.memset(powers[:, 5:9], LN_EPS).then_inc(sem("powers_set"), 1)
            for i in range(3):
                nc.gpsimd.memset(Qs[i][0:ROWS], 0.0).then_inc(sem("stacks_cleared"), 1)
            pool.wait_ge(sem("powers_set"), 3)
            pool.wait_ge(sem("zeros_set"), 1)
            pool.wait_ge(sem("tails_cleared"), 1)
            nc.gpsimd.iota(XR[:].bitcast(I32)[:, :, TOKEN_AT:TOKEN_AT + 1].rearrange("p t o -> p (t o)"), pattern=[[S, B]], base=0,
                           channel_multiplier=1).then_inc(sem("tokens_numbered"), 1)


            def rstd_of(name, index, n, mv_, rs_):
                pool.wait_ge(sem(name + "_stats"), count(2 * n * (index + 1)))
                pool.wait_ge(sem(name), count(n * (index if n == 2 else index - 1)))
                nc.gpsimd.tensor_tensor(rs_[:], mv_[:, :, 1:2].rearrange("p n o -> p (n o)"), powers[:, 5:5 + n], ALU.add).then_inc(sem(name + "_rstd"), 1)
                pool.wait_ge(sem(name + "_rstd"), 2 * index + 1)
                nc.gpsimd.tensor_tensor(rs_[:], rs_[:], powers[:, 0:n], ALU.pow).then_inc(sem(name + "_rstd"), 1)

            def attention(L):
                T0, P0 = L * B, L * PAIRS
                def whole(k, which):
                    p = pair(k)
                    if is_pair(p):
                        nm = "qk"[which]
                        pool.wait_ge(sem(f"{nm}_rotated"), 2 * p + 2)
                        pool.wait_ge(sem(f"{nm}_pieces"), count(3 * (p + P0)))
                        nc.gpsimd.tensor_tensor(full[which][:], rotA[which][:], rotB[which][:], ALU.add).then_inc(sem(f"{nm}_full"), 1)

                def cut(k, which):
                    p = pair(k)
                    if is_pair(p):
                        nm = "qk"[which]
                        m = 128 if L == 0 or which == 0 else KV1 * DK
                        h, f, r, pc = (piece[which][0:m, 0, :], full[which][0:m, :], rest[which][0:m, :], piece[which])
                        pool.wait_ge(sem(f"{nm}_high"), p + P0 + 1)
                        nc.gpsimd.tensor_tensor(pc[0:m, 1, :], f, h, ALU.subtract).then_inc(sem(f"{nm}_pieces"), 1)
                        nc.gpsimd.tensor_tensor(r, f, h, ALU.subtract).then_inc(sem(f"{nm}_pieces"), 1)
                        pool.wait_ge(sem(f"{nm}_pieces"), 3 * (p + P0) + 2)
                        nc.gpsimd.tensor_tensor(pc[0:m, 2, :], r, pc[0:m, 1, :], ALU.subtract).then_inc(sem(f"{nm}_pieces"), 1)

                def low(t, c):
                    if is_batch(t):
                        pool.wait_ge(sem("exp_done"), 8 * (t + T0) + 2 * c + 2)
                        pool.wait_ge(sem("pv_done"), count(4 * (t + T0) + c - 3))
                        nc.gpsimd.tensor_tensor(Pl[:, c, :], P32[:, c, :], Ph[:, c, :], ALU.subtract).then_inc(sem("lows_pool"), 1)

                def out_rstd(t):
                    if is_batch(t):
                        pool.wait_ge(sem("out_norm1"), 4 * t + 4)
                        pool.wait_ge(sem("out_centred"), count(t))
                        nc.gpsimd.tensor_tensor(orstd[:], omv[:, 1:2], powers[:, 5:6], ALU.add).then_inc(sem("out_rstd"), 1)
                        pool.wait_ge(sem("out_rstd"), 2 * t + 1)
                        nc.gpsimd.tensor_tensor(orstd[:], orstd[:], powers[:, 0:1], ALU.pow).then_inc(sem("out_rstd"), 1)

                if L == 0:
                    pool.wait_ge(sem("gate_unit"), count(2))
                    nc.gpsimd.tensor_tensor(wgn[:, 1:2], wgn[:, 0:1], powers[0:EXPERTS, 4:5], ALU.pow).then_inc(sem("gate_norm"), 1)

                def shift_of(p):
                    pool.wait_ge(sem("xn_ready_rstd"), 2 * (p + P0) + 2)
                    nc.gpsimd.tensor_tensor(shift[:], mv[:, :, 0], rstd[:], ALU.mult).then_inc(sem("shifted"), 1)
                    pool.wait_ge(sem("shifted"), 2 * (p + P0) + 1)
                    nc.gpsimd.tensor_tensor(shift[:], zero[:, 0:2], shift[:], ALU.subtract).then_inc(sem("shifted"), 1)

                def step(t, j):
                    k, which = (j + 4, 1) if j % 2 == 0 else (j + 5, 0)
                    if L == 0:
                        whole(k, which)
                    else:
                        out_rstd(t - 2)
                    low(t - 1, 3)
                    low(t, 0)
                    cut(k, which)
                    if j % 2 == 0 and is_pair(pair(j + 8)):
                        rstd_of("xn_ready", pair(j + 8) + P0, 2, mv, rstd)
                        shift_of(pair(j + 8))
                    low(t, 2)

                body_loop(pool, step)

            attention(0)
            rstd_of("f_xn_ready", 0, 2, mv, rstd)
            with pool.Fori(1, PAIRS) as p:
                rstd_of("f_xn_ready", p, 2, mv, rstd)
            attention(1)
            for g in range(B // 4):
                rstd_of("m_xn_ready", g, 4, mmv[g % 2], mrs[g % 2])
            pool.wait_ge(sem("rows_blank"), 32)
            pool.wait_ge(sem("slots_ready"), 1)
            pool.wait_ge(sem("tokens_numbered"), 1)
            for t in range(B):
                nc.gpsimd.indirect_dma_start(out=rows_d, out_offset=bass.IndirectOffsetOnAxis(ap=sloti[:, t:t + 1], axis=0),
                                             in_=XR[:, t, :], in_offset=None).then_inc(sem("scattered"), 16)

            def step(j, r, turn):
                pool.wait_ge(sem("b_y_ready"), count(j + 1))
                pool.sem_inc(sem("going_out"), 1)
                at_ = XB[r].bitcast(I32)[:, TOKEN_AT - D:TOKEN_AT - D + 1]
                nc.gpsimd.indirect_dma_start(out=out, out_offset=bass.IndirectOffsetOnAxis(ap=at_, axis=0),
                                             in_=by[r], in_offset=None).then_inc(sem(f"gone_out{r}"), 16)

            block_loop(pool, step, 0, BLOCKS)
            for r in range(TURNS):
                pool.wait_ge(sem(f"gone_out{r}"), 16 * (BLOCKS // TURNS))

        @block.vector
        def _(dve):
            def norm_stats(name, index, n, src, st_, mv_):
                for i in range(n):
                    nc.vector.bn_stats(st_[:, i, :], src(i)).then_inc(sem(name + "_stats"), 1)
                dve.wait_ge(sem(name + "_stats"), index * 2 * n + n)
                dve.sem_inc(sem("stats_seen"), 1)
                for i in range(n):
                    nc.vector.bn_aggr(mv_[:, i, :], st_[:, i, :]).then_inc(sem(name + "_stats"), 1)

            def norm_apply(name, index, n, src, mv_, rs_, dst):
                dve.wait_ge(sem(name + "_rstd"), count(2 * (index + 1)))
                for i in range(n):
                    nc.vector.tensor_scalar(dst(i), src(i), mv_[:, i, 0:1], rs_[:, i:i + 1], ALU.subtract, ALU.mult
                                            ).then_inc(sem(name), 1)

            for i in range(3):
                nc.vector.memset(Ks[i][0:ROWS], 0.0).then_inc(sem("k_cleared"), 1)
            nc.vector.memset(ones[:], 1.0).then_inc(sem("ones_set"), 1)
            nc.vector.memset(onesb[:], 1.0).then_inc(sem("ones_set"), 1)
            nc.vector.memset(zero[:], 0.0).then_inc(sem("zeros_set"), 1)
            nc.vector.memset(ends[:], 0.0).then_inc(sem("ones_set"), 1)
            nc.vector.memset(XR[:, :, SCORE_AT:RW], 0.0).then_inc(sem("tails_cleared"), 1)
            nc.vector.memset(Vp[:], 0.0).then_inc(sem("v_cleared"), 1)
            nc.vector.memset(negp[:], 0.0).then_inc(sem("ones_set"), 1)
            dve.wait_ge(sem("k_cleared"), 3)
            for i in range(3):
                nc.vector.memset(Ks[i][TERMS:ROWS, :, :], 1.0).then_inc(sem("stacks_cleared"), 1)
            dve.wait_ge(sem("v_cleared"), 1)
            nc.vector.memset(Vp[:, :, :, 0, DK:VW], 1.0).then_inc(sem("v_cleared"), 1)
            dve.wait_ge(sem("first_loaded"), FIRST_LOADED)
            dve.wait_ge(sem("ones_set"), 4)
            dve.wait_ge(sem("zeros_set"), 1)

            FW = (F1[:], F2[:].rearrange("p c n -> p (c n)"))
            for i, w in enumerate(FW):
                nc.vector.tensor_reduce(qred[:, i:i + 1], w, AX.X, ALU.add, apply_absolute_value=True).then_inc(sem("abs_summed"), 1)
            for i, w in enumerate(FW):
                dve.wait_ge(sem("abs_total"), count(i + 1))
                nc.vector.tensor_scalar(qgam[:, i:i + 1], MISC[i][:, 0:1], 1.0 / (FF * D), 1e-5, ALU.mult, ALU.add).then_inc(sem(f"quant{i}"), 1)
                dve.wait_ge(sem(f"quant{i}"), 1)
                nc.vector.reciprocal(qred[:, i:i + 1], qgam[:, i:i + 1]).then_inc(sem(f"quant{i}"), 1)
                dve.wait_ge(sem(f"quant{i}"), 2)
                nc.vector.tensor_scalar(w, w, qred[:, i:i + 1], 1.0, ALU.mult, ALU.min).then_inc(sem(f"quant{i}"), 1)
                dve.wait_ge(sem(f"quant{i}"), 3)
                nc.vector.tensor_scalar(w, w, -1.0, BIG_ROUND, ALU.max, ALU.add).then_inc(sem(f"quant{i}"), 1)
                dve.wait_ge(sem(f"quant{i}"), 4)
                nc.vector.tensor_scalar(w, w, BIG_ROUND, None, ALU.subtract).then_inc(sem("quantized"), 1)
            nc.vector.tensor_tensor(wgs[:, 0, :], wgr[:], wgr[:], ALU.mult).then_inc(sem("gate_unit"), 1)
            dve.wait_ge(sem("gate_unit"), 1)
            nc.vector.tensor_reduce(wgn[:, 0:1], wgs[:, 0, :], AX.X, ALU.add).then_inc(sem("gate_unit"), 1)
            dve.wait_ge(sem("gate_unit"), 2)
            dve.wait_ge(sem("gate_norm"), 1)
            nc.vector.tensor_scalar(wgn[:, 2:3], wgn[:, 1:2], 1e-4, None, ALU.max).then_inc(sem("gate_unit"), 1)
            dve.wait_ge(sem("gate_unit"), 3)
            nc.vector.reciprocal(wgn[:, 0:1], wgn[:, 2:3]).then_inc(sem("gate_unit"), 1)
            dve.wait_ge(sem("gate_unit"), 4)
            nc.vector.tensor_scalar(wgs[:, 1, :], wgr[:], wgn[:, 0:1], None, ALU.mult).then_inc(sem("gate_unit"), 1)
            dve.wait_ge(sem("gate_T"), count(1))
            nc.vector.tensor_copy(wgT[:], MISC[2][0:GATE, 0:EXPERTS]).then_inc(sem("gate_unitT"), 1)
            dve.wait_ge(sem("weights_loaded"), LOADED)
            for c in range(X_CHUNKS):
                dve.wait_ge(sem(f"x_loaded{c}"), 16)

            def attention(L):
                T0, P0 = L * B, L * PAIRS
                n_kv = (HEADS, KV1)[L]
                NORM = (2, 4)[L]

                def x_of(p):
                    if isinstance(p, int):
                        return lambda i: X[:, 2 * p + i, :]
                    return lambda i: X[:, bass.ds(p * 2 + i, 1), :].rearrange("p o d -> p (o d)")

                def x_stats(k):
                    p = pair(k)
                    if is_pair(p):
                        dve.wait_ge(sem("xn_ready"), count(2 * (p + P0)))
                        norm_stats("xn_ready", p + P0, 2, x_of(p), stats, mv)

                def rotate(k, which):
                    p = pair(k)
                    if not is_pair(p):
                        return
                    nm = "qk"[which]
                    dve.wait_ge(sem(f"{nm}_projected"), p + P0 + 1)
                    dve.wait_ge(sem(f"{nm}_full"), count(p + P0))
                    for tab, dst, off in ((cosT, rotA, 0), (sinT, rotB, PAIR)):
                        ins = nc.vector.tensor_tensor(
                            dst[which][:].rearrange("p (b s) -> p b s", b=2),
                            QK[:, off:off + PAIR].rearrange("p (b s) -> p b s", b=2),
                            tab[:].unsqueeze(1).broadcast_to([128, 2, 128]), ALU.mult)
                        ins.then_inc(sem(f"{nm}_rotated"), 1)
                    dve.wait_ge(sem(f"{nm}_rotated"), 2 * p + 2)
                    dve.sem_inc(sem(f"{nm}_bank_read"), 1)

                def split_v(k):
                    p, j = pair(k), k % BODY
                    if not is_pair(p):
                        return
                    m = n_kv * DK
                    f, r = vfull[:, :, 0:m], vrest[:, :, 0:m]

                    def pieces(c):
                        return Vp[:, j:j + 2, 0:n_kv, c, 0:DK]

                    def heads(ap):
                        return ap.rearrange("p b (h d) -> p b h d", d=DK)

                    dve.wait_ge(sem("v_high"), p + P0 + 1)
                    nc.vector.tensor_tensor(heads(r), heads(f), pieces(0), ALU.subtract).then_inc(sem("v_rest"), 1)
                    nc.vector.tensor_tensor(pieces(1), heads(f), pieces(0), ALU.subtract).then_inc(sem("v_rest"), 1)
                    dve.wait_ge(sem("v_rest"), 2 * (p + P0) + 2)
                    nc.vector.tensor_tensor(pieces(2), heads(r), pieces(1), ALU.subtract).then_inc(sem("v_split"), 1)

                def make_mask(k):
                    p = pair(k)
                    if not is_pair(p):
                        return
                    dve.wait_ge(sem(f"adj_loaded{turn(k)}"), 16 * turns(k))
                    dve.wait_ge(sem("scoresT_ready"), count(8 * (p + P0) - 16))
                    for i in range(2):
                        ins = nc.vector.scalar_tensor_tensor(mask[:, (k + i) % BODY, :], adj[turn(k)][:, i, :], 0.0, upper[:],
                                                             ALU.is_equal, ALU.max)
                    ins.then_inc(sem("mask_made"), 1)

                def maxima(t, c, k):
                    if is_batch(t):
                        dve.wait_ge(sem("scores_ready"), 4 * (t + T0) + c + 1)
                        nc.vector.tensor_reduce(negmax[:, k % 2, c * HQ:(c + 1) * HQ], SCORE[c % 2][:].rearrange("p (h k) -> p h k", h=HQ),
                                                AX.X, ALU.max, negate=True).then_inc(sem("maxima"), 1)

                def split_max_high(t, k):
                    if is_batch(t):
                        dve.wait_ge(sem("maxima"), 4 * (t + T0) + 4)
                        dve.wait_ge(sem("negmax_transposed"), count(t + T0))
                        nc.vector.tensor_copy(negp[:, 0, :], negmax[:, k % 2, :]).then_inc(sem("negmax_split"), 1)

                def split_max_rest(t, k):
                    if is_batch(t):
                        dve.wait_ge(sem("negmax_split"), 4 * (t + T0) + 1)
                        nm = negmax[:, k % 2, :]
                        nc.vector.tensor_tensor(negrest[:], nm, negp[:, 0, :], ALU.subtract).then_inc(sem("negmax_split"), 1)
                        nc.vector.tensor_tensor(negp[:, 1, :], nm, negp[:, 0, :], ALU.subtract).then_inc(sem("negmax_split"), 1)
                        dve.wait_ge(sem("negmax_split"), 4 * (t + T0) + 3)
                        nc.vector.tensor_tensor(negp[:, 2, :], negrest[:], negp[:, 1, :], ALU.subtract).then_inc(sem("negmax_split"), 1)

                def sum_pieces(t):
                    if is_batch(t):
                        dve.wait_ge(sem("pv_done"), 4 * (t + T0) + 4)
                        nc.vector.tensor_reduce(osum[:], PVOUT[:, 0:HEADS * VP].rearrange("p (h c e) -> p h e c", c=3, e=VW),
                                                AX.X, ALU.add).then_inc(sem("pv_read"), 1)

                def denominators(t):
                    if is_batch(t):
                        dve.wait_ge(sem("pv_read"), t + T0 + 1)
                        nc.vector.reciprocal(rden[:], osum[:, :, DK:VW].rearrange("p h o -> p (h o)")).then_inc(sem(f"out_norm{L}"), 1)

                def norm_out(t):
                    if is_batch(t):
                        if L == 0:
                            dve.wait_ge(sem("out_transposed"), count(t + T0))
                        dve.wait_ge(sem(f"out_norm{L}"), NORM * t + 1)
                        nc.vector.tensor_tensor(onorm[:].rearrange("p (h d) -> p h d", d=DK), osum[:, :, 0:DK],
                                                rden[:].unsqueeze(2).broadcast_to([128, HEADS, DK]), ALU.mult).then_inc(sem(f"out_norm{L}"), 1)

                def out_stats(t):
                    if is_batch(t):
                        dve.wait_ge(sem(f"out_norm{L}"), NORM * t + 2)
                        nc.vector.bn_stats(ostat[:], onorm[:]).then_inc(sem(f"out_norm{L}"), 1)
                        dve.wait_ge(sem(f"out_norm{L}"), NORM * t + 3)
                        dve.sem_inc(sem("stats_seen"), 1)
                        nc.vector.bn_aggr(omv[:], ostat[:]).then_inc(sem(f"out_norm{L}"), 1)

                def centre_out(t):
                    if is_batch(t):
                        dve.wait_ge(sem("out_rstd"), 2 * t + 2)
                        dve.wait_ge(sem("out_transposed"), count(t + T0))
                        nc.vector.tensor_scalar(oln[:], onorm[:], omv[:, 0:1], orstd[:], ALU.subtract, ALU.mult
                                                ).then_inc(sem("out_centred"), 1)

                def low(t, c):
                    if is_batch(t):
                        dve.wait_ge(sem("exp_done"), 8 * (t + T0) + 2 * c + 2)
                        dve.wait_ge(sem("pv_done"), count(4 * (t + T0) + c - 3))
                        nc.vector.tensor_tensor(Pl[:, c, :], P32[:, c, :], Ph[:, c, :], ALU.subtract).then_inc(sem("lows_dve"), 1)

                def add_out(t):
                    if is_batch(t):
                        dve.wait_ge(sem("out_projected"), t + T0 + 1)
                        x = X[:, t, :] if isinstance(t, int) else X[:, bass.ds(t, 1), :].rearrange("p o d -> p (o d)")
                        nc.vector.tensor_tensor(x, x, OUTP, ALU.add).then_inc(sem("attn_added"), 1)

                def step(t, j):
                    if L == 0:
                        if j % 2 == 0:
                            rotate(j + 4, 1)
                        else:
                            rotate(j + 5, 0)
                    add_out(t - 3)
                    split_max_high(t + 1, j + 1)
                    maxima(t + 2, 0, j + 2)
                    split_max_rest(t + 1, j + 1)
                    if L:
                        centre_out(t - 2)
                    maxima(t + 2, 1, j + 2)
                    if j % 2 == 0:
                        x_stats(j + 8)
                    else:
                        split_v(j + 3)
                        if L:
                            make_mask(j + 3)
                    low(t, 1)
                    maxima(t + 2, 2, j + 2)
                    sum_pieces(t - 1)
                    denominators(t - 1)
                    maxima(t + 2, 3, j + 2)
                    norm_out(t - 1)
                    if L:
                        out_stats(t - 1)

                body_loop(dve, step)

            def ffn():
                def norm(p):
                    src = ((lambda i: X[:, 2 * p + i, :]) if isinstance(p, int) else
                           (lambda i: X[:, bass.ds(p * 2 + i, 1), :].rearrange("p o d -> p (o d)")))
                    norm_stats("f_xn_ready", p, 2, src, stats, mv)
                    dve.wait_ge(sem("f_transposed"), count(p))
                    norm_apply("f_xn_ready", p, 2, src, mv, rstd, lambda i: fxn[:, i, :])

                def add(p):
                    for h in range(2):
                        dve.wait_ge(sem("f_down"), count(2 * p + h + 1))
                        x = X[:, p * 2 + h, :] if isinstance(p, int) else X[:, bass.ds(p * 2 + h, 1), :].rearrange("p o d -> p (o d)")
                        nc.vector.tensor_tensor(tmp[:, h, :], bank[6 + h][:, 0:128], rowsb[:, 2, :], ALU.add).then_inc(sem("f_bank_read"), 1)
                        dve.wait_ge(sem("f_bank_read"), 2 * p + h + 1)
                        nc.vector.tensor_tensor(x, x, tmp[:, h, :], ALU.add).then_inc(sem("f_added"), 1)

                dve.wait_ge(sem("attn_added"), B)
                norm(0)
                norm(1)
                norm(2)
                with dve.Fori(0, PAIRS - 3) as p:
                    norm(p + 3)
                    add(p)
                for p in range(PAIRS - 3, PAIRS):
                    add(p)
                dve.wait_ge(sem("f_added"), 2 * PAIRS)

            def gate():
                G = B // 4
                dve.wait_ge(sem("attn_added"), 2 * B)
                for g in range(G + 3):
                    if g < G:
                        norm_stats("m_xn_ready", g, 4, lambda i: X[:, 4 * g + i, :], mst[g % 2], mmv[g % 2])
                    if 1 <= g <= G:
                        norm_apply("m_xn_ready", g - 1, 4, lambda i: X[:, 4 * (g - 1) + i, :], mmv[(g - 1) % 2], mrs[(g - 1) % 2],
                                   lambda i: XR[:, 4 * (g - 1) + i, 0:D])
                    if g >= 3:
                        k = g - 3
                        dve.wait_ge(sem("m_logits"), k + 1)
                        nc.vector.tensor_copy(lg[:, 4 * k:4 * k + 4, :], bank[4 + k % 2][:, 0:4 * EXPERTS].rearrange("p (h e) -> p h e", h=4)
                                              ).then_inc(sem("m_logits_read"), 1)
                dve.wait_ge(sem("m_logits_read"), G)
                per = [128, B, EXPERTS]
                ranks = rank[:].unsqueeze(1).broadcast_to(per)

                def col(i):
                    return top[:, i, :].unsqueeze(2).broadcast_to(per)

                nc.vector.tensor_reduce(top[:, 0, :], lg[:], AX.X, ALU.max, negate=True).then_inc(sem("choosing"), 1)
                dve.wait_ge(sem("choosing"), 1)
                nc.vector.tensor_tensor(lg[:], lg[:], col(0), ALU.add).then_inc(sem("logits_centred"), 1)
                dve.wait_ge(sem("logits_centred"), 1)
                nc.vector.scalar_tensor_tensor(cand[:], lg[:], 0.0, ranks, ALU.is_ge, ALU.mult).then_inc(sem("choosing"), 1)
                dve.wait_ge(sem("choosing"), 2)
                nc.vector.tensor_reduce(top[:, 1, :], cand[:], AX.X, ALU.max).then_inc(sem("choosing"), 1)
                dve.wait_ge(sem("choosing"), 3)
                nc.vector.tensor_tensor(chosen[:], ranks, col(1), ALU.is_equal).then_inc(sem("chosen_ready"), 1)
                dve.wait_ge(sem("gate_exp"), 1)
                nc.vector.tensor_reduce(top[:, 2, :], ex[:], AX.X, ALU.add).then_inc(sem("choosing"), 1)
                dve.wait_ge(sem("choosing"), 4)
                dve.wait_ge(sem("tokens_numbered"), 1)
                nc.vector.reciprocal(XR[:, :, SCORE_AT], top[:, 2, :]).then_inc(sem("choosing"), 1)
                dve.wait_ge(sem("ranked"), 2)
                nc.vector.tensor_copy(cnt[:], bank[7][:, 0:B * EXPERTS].rearrange("p (t e) -> p e t", e=EXPERTS)).then_inc(sem("placing"), 1)
                dve.wait_ge(sem("placing"), 1)
                cumf, cntf = cum[:].rearrange("p e t -> p (e t)"), cnt[:].rearrange("p e t -> p (e t)")
                nc.vector.tensor_tensor_scan(cumf, cntf, zero[:], 0.0, ALU.add, ALU.add).then_inc(sem("placing"), 1)
                dve.wait_ge(sem("placing"), 2)
                nc.vector.tensor_copy(ends[:, 0, 1:EXPERTS + 1], cum[:, :, B - 1]).then_inc(sem("placing"), 1)
                nc.vector.tensor_tensor(place[:, 0, :], cumf, cntf, ALU.subtract).then_inc(sem("placing"), 1)
                dve.wait_ge(sem("placing"), 4)
                n = ends[:, 1, 0:EXPERTS]
                nc.vector.tensor_tensor(n, ends[:, 0, 1:EXPERTS + 1], ends[:, 0, 0:EXPERTS], ALU.subtract).then_inc(sem("placing"), 1)
                dve.wait_ge(sem("placing"), 5)
                nc.vector.tensor_scalar(n, n, 63.5, 1.0 / 128, ALU.add, ALU.mult).then_inc(sem("placing"), 1)
                dve.wait_ge(sem("placing"), 6)
                nc.vector.tensor_scalar(n, n, BIG_ROUND, None, ALU.add).then_inc(sem("placing"), 1)
                dve.wait_ge(sem("placing"), 7)
                nc.vector.tensor_scalar(n, n, BIG_ROUND, None, ALU.subtract).then_inc(sem("placing"), 1)
                dve.wait_ge(sem("placing"), 8)
                nc.vector.tensor_tensor_scan(ends[:, 2, 1:EXPERTS + 1], n, zero[:, 0:EXPERTS], 0.0, ALU.add, ALU.add).then_inc(sem("placing"), 1)
                dve.wait_ge(sem("placing"), 9)
                nc.vector.scalar_tensor_tensor(ends[:, 3, 0:EXPERTS], ends[:, 2, 0:EXPERTS], 128.0, ends[:, 0, 0:EXPERTS],
                                               ALU.mult, ALU.subtract).then_inc(sem("placing"), 1)
                nc.vector.tensor_tensor(blkge[:], blk[:].unsqueeze(2).broadcast_to([1, BLOCKS, EXPERTS - 1]),
                                        ends[0:1, 2, 1:EXPERTS].unsqueeze(1).broadcast_to([1, BLOCKS, EXPERTS - 1]),
                                        ALU.is_ge).then_inc(sem("placing"), 1)
                dve.wait_ge(sem("placing"), 11)
                nc.vector.tensor_reduce(expf[:], blkge[:], AX.X, ALU.add).then_inc(sem("placing"), 1)
                p0 = place[:, 0, :].rearrange("p (e t) -> p e t", t=B)
                p1 = place[:, 1, :].rearrange("p (e t) -> p e t", t=B)
                nc.vector.tensor_tensor(p1, p0, ends[:, 3, 0:EXPERTS].unsqueeze(2).broadcast_to([128, EXPERTS, B]), ALU.add
                                        ).then_inc(sem("placing"), 1)
                dve.wait_ge(sem("placing"), 13)
                nc.vector.tensor_copy(expert[:], expf[:]).then_inc(sem("expert_ready"), 1)
                nc.vector.tensor_tensor(cand[:], bank[6][:, 0:B * EXPERTS].rearrange("p (t e) -> p t e", e=EXPERTS),
                                        p1.rearrange("p e t -> p t e"), ALU.add).then_inc(sem("placing"), 1)
                dve.wait_ge(sem("placing"), 14)
                nc.vector.tensor_tensor(cand[:], cand[:], chosen[:], ALU.mult).then_inc(sem("placing"), 1)
                dve.wait_ge(sem("placing"), 15)
                nc.vector.tensor_reduce(slot[:], cand[:], AX.X, ALU.add).then_inc(sem("placing"), 1)
                dve.wait_ge(sem("placing"), 16)
                nc.vector.tensor_copy(sloti[:], slot[:]).then_inc(sem("slots_ready"), 1)

            def experts():
                def step(j, r, turn):
                    n1, p1 = (r + 1) % TURNS, (r - 1) % TURNS
                    if not isinstance(j, int) or 0 <= j + 1 < BLOCKS:
                        e = dve.value_load(expert[0:1, bass.ds(j + 1, 1)], min_val=0, max_val=EXPERTS - 1)
                        dve.wait_ge(sem("b_up"), count(j + 2))
                        dve.wait_ge(sem("b_gelu"), count(j - 1))
                        nc.vector.tensor_tensor(bh0[n1], bank[1 + n1][:], M1b[:, bass.ds(e, 1), :].rearrange("p o n -> p (o n)"), ALU.add
                                                ).then_inc(sem("b_biased"), 1)
                    if not isinstance(j, int) or 0 <= j - 1 < BLOCKS:
                        e = dve.value_load(expert[0:1, bass.ds(j - 1, 1)], min_val=0, max_val=EXPERTS - 1)
                        prior = turn - 1 if r == 0 else turn
                        dve.wait_ge(sem("b_down"), count(j))
                        dve.wait_ge(sem("b_y_ready"), count(j - 1))
                        nc.vector.tensor_tensor(by0, bank[7][:, 0:D], M2b[:, bass.ds(e, 1), :].rearrange("p o n -> p (o n)"), ALU.add
                                                ).then_inc(sem("b_y_read"), 1)
                        dve.wait_ge(sem("b_y_read"), count(j))
                        dve.wait_ge(sem(f"xb_loaded{p1}"), 16 * prior)
                        dve.wait_ge(sem(f"gone_out{p1}"), count(16 * (prior - 1)))
                        nc.vector.scalar_tensor_tensor(by[p1], by0, XB[p1][:, SCORE_AT - D:SCORE_AT - D + 1], XB[p1][:, 0:D],
                                                       ALU.mult, ALU.add).then_inc(sem("b_y_ready"), 1)

                dve.wait_ge(sem("expert_ready"), 1)
                dve.wait_ge(sem("experts_loaded"), EXPERTS_LOADED)
                block_loop(dve, step, -1, BLOCKS + 1)

            attention(0)
            ffn()
            attention(1)
            gate()
            experts()


def rope_tables():
    inv = (1.0 / np.power(np.float32(10000.0), np.arange(0, DK, 2, dtype=np.float32) / np.float32(DK))).astype(np.float32)
    f = np.outer(np.arange(S, dtype=np.float32), inv).astype(np.float32)
    c, s = np.cos(f).astype(np.float32), np.sin(f).astype(np.float32)
    cosT = np.zeros((DK, HEADS, S), np.float32)
    sinT = np.zeros((DK, HEADS, S), np.float32)
    for i in range(DK // 2):
        cosT[2 * i] = cosT[2 * i + 1] = c[:, i]
        sinT[2 * i] = -s[:, i]
        sinT[2 * i + 1] = s[:, i]
    return cosT.reshape(128, S), sinT.reshape(128, S)


def by_component(heads):
    return np.arange(heads * DK).reshape(heads, DK).T.reshape(-1)


def kernel(**inputs):
    import ml_dtypes
    import concourse.bacc as bacc
    from concourse.bass_utils import run_bass_kernel_spmd

    g = {k: np.asarray(v) for k, v in inputs.items()}
    order = by_component(HEADS)
    order1 = by_component(KV1)
    swap = order ^ 1
    wq, wk = g["L0_xattn_Wq"], g["L0_xattn_Wk"]
    cosT, sinT = rope_tables()
    cols = np.zeros((128, 4), np.float32)
    cols[:, 0] = g["L1_xattn_bq"][order]
    cols[0:32, 1] = g["L1_xattn_bk"][order1]
    cols[:, 2] = g["L1_xattn_ln_g"]
    cols[:, 3] = g["L1_xattn_ln_b"]
    arrays = {
        "x": g["x"], "ctxT": g["ctx_1024"].reshape(B * S, D).T, "mask": g["mask_BxSxS2_ik1"],
        "W0": np.stack([wq[order].T, wq[swap].T, wk[order].T, wk[swap].T, g["L0_xattn_Wv"].T, g["L0_xattn_Wo"].T]),
        "cosT": cosT, "sinT": sinT, "eye": np.eye(128, dtype=np.float32),
        "eyeb": np.eye(128).astype(ml_dtypes.bfloat16),
        "negI": (np.eye(128) * MASKED).astype(ml_dtypes.bfloat16),
        "upper": np.triu(np.ones((128, 128)), 1).astype(ml_dtypes.bfloat16),
        "W1Q": g["L1_xattn_Wq"][order].T, "W1K": g["L1_xattn_Wk"][order1].T, "W1V": g["L1_xattn_Wv"].T, "W1O": g["L1_xattn_Wo"].T,
        "cols": cols, "bv": g["L1_xattn_bv"], "bo": g["L1_xattn_bo"], "b2": g["L0_ffn_b2"],
        "F1": g["L0_ffn_W1"].T, "F1b": g["L0_ffn_b1"].reshape(FC, 128).T, "F2": g["L0_ffn_W2"].T,
        "WG": g["L1_ffn_wg_red"].T, "wg": g["L1_ffn_wg"],
        "rank": (EXPERTS - np.arange(EXPERTS)).astype(np.float32),
        "M1": g["L1_ffn_w1"], "M1b": g["L1_ffn_b1"], "M2": g["L1_ffn_w2"], "M2b": g["L1_ffn_b2"],
    }
    tails = np.zeros((BLOCKS * 128, RW - 2 * D), np.float32)
    tails[:, TOKEN_AT - 2 * D] = (TOKENS + np.arange(BLOCKS * 128, dtype=np.int32)).view(np.float32)
    arrays["tails"] = tails
    arrays["before"] = np.triu(np.ones((128, 128)), 1).astype(ml_dtypes.bfloat16)
    arrays["blk"] = np.arange(BLOCKS, dtype=np.float32)
    nc = bacc.Bacc("TRN2", target_bir_lowering=False, num_devices=1)
    feeds, aps = {}, {}
    for name, v in arrays.items():
        v = np.ascontiguousarray(v)
        feeds[f"in_{name}"] = v
        aps[name] = nc.dram_tensor(f"in_{name}", v.shape, mybir.dt.from_np(v.dtype), kind="ExternalInput").ap()
    out = nc.dram_tensor("out_0", (TOKENS + BLOCKS * 128, D), F32, kind="ExternalOutput").ap()
    build(nc, aps, out)
    r = run_bass_kernel_spmd(nc, [feeds], core_ids=[0])
    return r.results[0]["out_0"][0:TOKENS].reshape(B, S, D)
```

```python
from contextlib import ExitStack

import numpy as np

import concourse.bass as bass
from concourse import mybir

ALU = mybir.AluOpType
ACT = mybir.ActivationFunctionType
AX = mybir.AxisListType
F32 = mybir.dt.float32
BF16 = mybir.dt.bfloat16
F16 = mybir.dt.float16
I32 = mybir.dt.int32

B, S, D = 32, 128, 128
HEADS, DK = 16, 8
KV1 = 4
FF = 512
FC = FF // 128
EXPERTS, GATE = 8, 16
QUARTERS = 4
HQ = HEADS // QUARTERS
PAIR = 2 * S
PAIRS = B // 2
BODY = 6
AHEAD = 8
START = -4
EARLY = 6
NB = (B - AHEAD) // BODY
QSLOT = (0, 0, 1, 0, 1, 2)
KSLOT = (0, 1, 0, 2, 1, 0)
SLOTS = len(QSLOT)
TERMS = 96
ROWS = TERMS + 3
VW = DK + 1
VP = 3 * VW
SCALE = float(1.0 / np.sqrt(np.float32(DK)))
MASKED = -float(2.0 ** 100)
LN_EPS = 1e-5
RW = 2 * D + 4
SCORE_AT, TOKEN_AT = 2 * D, 2 * D + 1
TOKENS = B * S
BLOCKS = B + EXPERTS - 1
DUMMIES = BLOCKS - B
REGION = TOKENS + 128
TURNS = 3
BIG_ROUND = 12582912.0


def build(nc, a, out):
    ctx = ExitStack()
    with ctx:
        def sb(name, shape, dt=F32):
            return ctx.enter_context(nc.sbuf_tensor(name, shape, dt))

        sems = {}

        def sem(name):
            if name not in sems:
                sems[name] = ctx.enter_context(nc.semaphore(name))
            return sems[name]

        def count(value):
            return max(value, 0) if isinstance(value, int) else value

        bank = [ctx.enter_context(nc.psum_tensor(f"bank{i}", [128, 512], F32)) for i in range(8)]
        SCORE = bank[0:2]
        SCORET = bank[2:4]
        PVOUT = bank[4]
        MAXT = bank[7][:, 256:320].bitcast(BF16)
        XNT, VAL = bank[5][:, 0:PAIR], bank[5][:, PAIR:2 * PAIR]
        QK = bank[6]
        OUTT, OUTP = bank[7][:, 0:128], bank[7][:, 128:256]

        XR = sb("XR", [128, B, RW])
        X = XR[:, :, D:2 * D]
        eye = sb("eye", [128, 128])
        eyeb = sb("eyeb", [128, 128], BF16)
        ones = sb("ones", [128, 128])
        warm = sb("warm", [128, 1])
        negI = sb("negI", [128, 128], BF16)
        upper = sb("upper", [128, 128], BF16)
        cosT = sb("cosT", [128, 128])
        sinT = sb("sinT", [128, 128])
        W0 = sb("W0", [128, 6, 128])
        W1Q = sb("W1Q", [128, 128])
        W1K = sb("W1K", [128, 32])
        W1V = sb("W1V", [128, 32])
        W1O = sb("W1O", [128, 128])
        cols = sb("cols", [128, 8])
        rowsb = sb("rowsb", [128, 3, 128])
        F1 = sb("F1", [128, FF])
        F1b = sb("F1b", [128, FC])
        F2 = sb("F2", [128, FC, 128])
        M1b = sb("M1b", [128, EXPERTS, FC])
        WG = sb("WG", [128, GATE])
        wgr = sb("wgr", [EXPERTS, GATE])
        M1 = sb("M1", [128, EXPERTS, FF])
        M2 = sb("M2", [128, EXPERTS, FC, 128])
        M2b = sb("M2b", [96, EXPERTS, 128])
        rank = sb("rank", [128, EXPERTS])

        ctxT = [sb(f"ctxT{i}", [128, PAIR]) for i in range(3)]
        adj = [sb(f"adj{i}", [128, 2, 128], I32) for i in range(3)]
        mask = sb("mask", [128, BODY, 128], BF16)
        stats = sb("stats", [128, 2, 6])
        mv = sb("mv", [128, 2, 2])
        rstd = sb("rstd", [128, 2])
        powers = sb("powers", [128, 9])
        xn = sb("xn", [128, 2, 128])
        xnT = sb("xnT", [128, PAIR])
        shift = sb("shift", [128, 2])
        rotA = [sb(f"rotA{i}", [128, PAIR]) for i in range(2)]
        rotB = [sb(f"rotB{i}", [128, PAIR]) for i in range(2)]
        full = [sb(f"full{i}", [128, PAIR]) for i in range(2)]
        rest = [sb(f"rest{i}", [128, PAIR]) for i in range(2)]
        piece = [sb(f"piece{i}", [128, 3, PAIR], BF16) for i in range(2)]
        Qs = [sb(f"Qs{i}", [128, HEADS, PAIR], BF16) for i in range(3)]
        Ks = [sb(f"Ks{i}", [128, HEADS, PAIR], BF16) for i in range(3)]
        vfull = sb("vfull", [128, 2, 128])
        vrest = sb("vrest", [128, 2, 128])
        Vp = sb("Vp", [128, BODY, HEADS, 3, VW], BF16)
        negmax = sb("negmax", [128, 2, HEADS])
        negrest = sb("negrest", [128, HEADS])
        negp = sb("negp", [128, 8, HEADS], BF16)
        negpT = [sb(f"negpT{i}", [3 * HEADS, 128], BF16) for i in range(2)]
        P32 = sb("P32", [128, QUARTERS, 512])
        Ph = sb("Ph", [128, QUARTERS, 512], F16)
        Pl = sb("Pl", [128, QUARTERS, 512], F16)
        osum = sb("osum", [128, HEADS, VW])
        rden = sb("rden", [128, HEADS])
        onorm = sb("onorm", [128, 128])
        ostat = sb("ostat", [128, 6])
        omv = sb("omv", [128, 2])
        orstd = sb("orstd", [128, 1])
        oln = sb("oln", [128, 128])
        oT = sb("oT", [128, 128])

        fxn = sb("fxn", [128, 2, 2, 128])
        fstats = sb("fstats", [128, 2, 2, 6])
        fmv = sb("fmv", [128, 2, 2, 2])
        frstd = sb("frstd", [128, 2, 2])
        fxnT = sb("fxnT", [128, 2, PAIR])
        hT = sb("hT", [128, 2, FC, PAIR])
        qred = sb("qred", [128, 2])
        qgam = sb("qgam", [128, 2])

        def carve(tile, *widths):
            flat = tile[:].rearrange("p h s -> p (h s)").bitcast(F32)
            ends_ = np.cumsum(widths)
            assert ends_[-1] <= flat.shape[1]
            return [flat[:, int(e - w):int(e)] for e, w in zip(ends_, widths)]

        *W1e, mxT0 = carve(Qs[0], FF, FF, FF, 512)
        mxT1, brest, bpieces = carve(Qs[1], 512, EXPERTS * 128, EXPERTS * 64)
        brest = brest[0:96, :].rearrange("p (e n) -> p e n", e=EXPERTS)
        bpieces = bpieces[0:96, :].bitcast(BF16).rearrange("p (e n) -> p e n", e=EXPERTS)
        thrice = sb("thrice", [96, 128], BF16)
        bhT = carve(Ks[0], FF, FF, FF)
        views = carve(Ks[1], *[D] * TURNS, *[RW - D] * TURNS, *[128] * TURNS, *[D + 1] * TURNS)
        XA, XB, bxT, by = (views[i * TURNS:(i + 1) * TURNS] for i in range(4))
        b1e = carve(Ks[2], *[FC] * TURNS)
        mxT = [mxT0, mxT1]
        xrT = [sb(f"xrT{i}", [GATE, 512]) for i in range(2)]
        wgT = sb("wgT", [GATE, EXPERTS])
        wgn = sb("wgn", [EXPERTS, 3])
        wgs = sb("wgs", [EXPERTS, 2, GATE])
        mstats = sb("mstats", [128, B, 6])
        mmv = sb("mmv", [128, B, 2])
        mrstd = sb("mrstd", [128, B])
        mshift = sb("mshift", [128, B])
        spent = P32[:].rearrange("p c n -> p (c n)")
        lg, ex, cand, product = (spent[:, i * B * EXPERTS:(i + 1) * B * EXPERTS].rearrange("p (t e) -> p t e", e=EXPERTS)
                                 for i in range(4))
        past = spent[0:1, 4 * B * EXPERTS:4 * B * EXPERTS + 2 * BLOCKS * EXPERTS].rearrange("p (i n e) -> p i n e", i=2, e=EXPERTS)
        chosen = sb("chosen", [128, B, EXPERTS], BF16)
        top = sb("top", [128, 3, B])
        sums = sb("sums", [128, B // 4, EXPERTS], BF16)
        order = sb("order", [128, B])
        sloti = sb("sloti", [128, B], I32)
        first = sb("first", [128, 3, EXPERTS + 1])
        blank = sb("blank", [128, EXPERTS, RW])
        zero = blank[:, 0, 0:2 * D]
        blk = sb("blk", [1, BLOCKS])
        steps = sb("steps", [1, EXPERTS])
        place = sb("place", [1, 3, BLOCKS])
        base = sb("base", [1, BLOCKS], I32)
        ends = sb("ends", [1, EXPERTS], I32)
        expert = sb("expert", [1, BLOCKS], I32)
        before = sb("before", [128, 128], BF16)
        onesb = sb("onesb", [128, 128], BF16)
        rows_d = nc.dram_tensor("expert_rows", [(EXPERTS + 1) * REGION, RW], F32, kind="Internal").ap()

        xd = a["x"].rearrange("b s d -> s b d")
        maskd = a["mask"].rearrange("b q k -> q b k")
        ctxd = a["ctxT"]

        first_loads = [
            (eye[:], a["eye"]), (W0[:], a["W0"].rearrange("n e m -> e n m")), (cosT[:], a["cosT"]), (sinT[:], a["sinT"]),
        ]
        first_loads += [(Ks[i][TERMS:ROWS], a["ones"]) for i in range(3)]
        other_loads = [
            (F1[:], a["F1"]), (F2[:], a["F2"].rearrange("(c p) n -> p c n", p=128)), (wgr[:], a["wg"]),
            (eyeb[:], a["eyeb"]), (negI[:], a["negI"]), (upper[:], a["upper"]),
            (W1Q[:], a["W1Q"]), (W1K[:], a["W1K"]), (W1V[:], a["W1V"]), (W1O[:], a["W1O"]),
            (cols[:, 0:4], a["cols"]),
            (rowsb[:, 0, 0:32], a["bv"].partition_broadcast(128)),
            (rowsb[:, 1, :], a["bo"].partition_broadcast(128)),
            (rowsb[:, 2, :], a["b2"].partition_broadcast(128)),
            (F1b[:], a["F1b"]), (WG[:], a["WG"]), (rank[:], a["rank"].partition_broadcast(128)),
            (before[:], a["before"]), (blk[:], a["blk"].rearrange("(o n) -> o n", o=1)),
        ]
        expert_loads = [
            (M1b[:], a["M1b"]),
            (M2b[:].rearrange("p e n -> p (e n)"), a["M2b"].rearrange("e n -> (e n)").partition_broadcast(96)),
            (M1[:], a["M1"].rearrange("e p n -> p e n")),
            (M2[:], a["M2"].rearrange("e (c p) n -> p e c n", p=128)),
        ]
        X_CHUNKS = 4
        FIRST_LOADED, LOADED, EXPERTS_LOADED = 16 * len(first_loads), 16 * len(other_loads), 16 * len(expert_loads)

        body = {}

        def run(step, t):
            body["i"] = t // BODY
            step(t, t % BODY)

        def run_early(step, p):
            if isinstance(p, int) and p >= PAIRS - EARLY:
                run(step, p - (PAIRS - EARLY) - AHEAD)

        def body_loop(eng, step, first=-AHEAD):
            for t in range(first, BODY):
                run(step, t)
            with eng.Fori(1, NB) as i:
                body["i"] = i
                for j in range(BODY):
                    step(i * BODY + j, j)
            for t in range(NB * BODY, B + 3):
                run(step, t)

        def pair_loop(eng, step):
            for p in range(2):
                step(p, p)
            with eng.Fori(1, (PAIRS - EARLY) // 2) as i:
                for b in range(2):
                    step(i * 2 + b, b)
            for p in range(PAIRS - EARLY, PAIRS):
                step(p, p % 2)

        def is_batch(t):
            return not isinstance(t, int) or 0 <= t < B

        def is_pair(p):
            return not isinstance(p, int) or 0 <= p < PAIRS

        def pair(k):
            return body["i"] * (BODY // 2) + k // 2

        def turn(k):
            return k // 2 % 3

        def turns(k):
            return body["i"] + k // BODY + 1

        def block_loop(eng, step, first, end):
            assert BLOCKS // TURNS % 2 == 1 and BLOCKS % TURNS == 0
            body["entered"] = False
            for j in range(first, 2 * TURNS):
                step(j, j % TURNS, j // TURNS + 1)
            body["entered"] = True
            with eng.Fori(1, BLOCKS // TURNS // 2) as i:
                for r in range(2 * TURNS):
                    step(i * (2 * TURNS) + r, r % TURNS, i * 2 + (r // TURNS + 1))
            body["entered"] = True
            for j in range(BLOCKS - TURNS, end):
                step(j, j % TURNS, j // TURNS + 1)

        block = ctx.enter_context(nc.Block())

        @block.sync
        def _(sp):
            def load_x_chunk(c):
                w = B // X_CHUNKS
                sp.dma_start(X[:, c * w:(c + 1) * w, :], xd[:, c * w:(c + 1) * w, :]).then_inc(sem(f"x_loaded{c}"), 16)

            load_x_chunk(0)
            for dst, src in first_loads:
                sp.dma_start(dst, src).then_inc(sem("first_loaded"), 16)

            def attention(L):
                T0, P0 = L * B, L * PAIRS
                n_kv = (HEADS, KV1)[L]

                def known(value):
                    return value if isinstance(value, int) else sp.snap(value)

                def load_ctx(k):
                    p, b = pair(k), turn(k)
                    if is_pair(p):
                        read, column = known(p + P0 - 2), known(p * PAIR)
                        sp.wait_ge(sem("v_projected"), count(read))
                        sp.dma_start(ctxT[b][:], ctxd[:, bass.ds(column, PAIR)]).then_inc(sem(f"ctx_loaded{L}{b}"), 16)

                def load_adj(k):
                    p, b = pair(k), turn(k)
                    if is_pair(p):
                        made, row = known(p - 2), known(p * 2)
                        sp.wait_ge(sem("mask_made"), count(made))
                        sp.dma_start(adj[b][:], maskd[:, bass.ds(row, 2), :]).then_inc(sem(f"adj_loaded{b}"), 16)

                def stack_q(k):
                    p, b = pair(k), turn(k)
                    if is_pair(p):
                        read, cut = known(8 * (p + P0 - 2)), known(3 * (p + P0) + 3)
                        sp.wait_ge(sem("scoresT_ready"), count(read))
                        sp.wait_ge(sem("q_pieces"), cut)
                        for s in range(SLOTS):
                            sp.dma_start(Qs[b][s * DK:(s + 1) * DK, :, :],
                                         piece[0][:, QSLOT[s], :]).then_inc(sem(f"q_stacked{L}{b}"), 16)

                def stack_k(k):
                    p, b = pair(k), turn(k)
                    if is_pair(p):
                        cut = known(3 * (p + P0) + 3)
                        sp.wait_ge(sem("k_pieces"), cut)
                        for s in range(SLOTS):
                            sp.dma_start(Ks[b][s * DK:(s + 1) * DK, 0:n_kv, :],
                                         piece[1][0:n_kv * DK, KSLOT[s], :]).then_inc(sem(f"k_stacked{L}{b}"), 16)

                def max_rows(t, k):
                    if is_batch(t):
                        sp.wait_ge(sem("negmaxT_ready"), t + T0 + 1)
                        sp.dma_start(Qs[turn(k)][TERMS:ROWS, :, k % 2 * S:(k % 2 + 1) * S],
                                     negpT[k % 2][:]).then_inc(sem(f"max_rows{L}{k % 2}"), 16)

                def step(t, j):
                    if j % 2 == 0:
                        stack_q(j + 4)
                    else:
                        stack_k(j + 3)
                        load_ctx(j + 7)
                        if L:
                            load_adj(j + 5)
                    max_rows(t + 1, j + 1)

                return step

            step = attention(0)
            for t in range(-AHEAD, START):
                run(step, t)
                if t == -AHEAD + 1:
                    for dst, src in other_loads:
                        sp.dma_start(dst, src).then_inc(sem("weights_loaded"), 16)
                    for c in range(1, X_CHUNKS):
                        load_x_chunk(c)
            sp.wait_ge(sem("stacks_cleared"), 6)
            body_loop(sp, step, START)
            for dst, src in expert_loads:
                sp.dma_start(dst, src).then_inc(sem("experts_loaded"), 16)
            sp.wait_ge(sem("zeros_set"), 1)
            sp.dma_start(rows_d[0:DUMMIES * 128, 0:2 * D].rearrange("(n p) w -> p n w", p=128),
                         zero.unsqueeze(1).broadcast_to([128, DUMMIES, 2 * D])).then_inc(sem("rows_blank"), 16)
            sp.dma_start(rows_d[0:DUMMIES * 128, 2 * D:RW], a["tails"][0:DUMMIES * 128]).then_inc(sem("rows_blank"), 16)
            sp.dma_start(blank[:, :, 2 * D:RW], a["tails"][DUMMIES * 128:].rearrange("(e p) w -> p e w", p=128)
                         ).then_inc(sem("tails_loaded"), 16)
            body_loop(sp, attention(1))
            sp.wait_ge(sem("tails_loaded"), 16)
            sp.wait_ge(sem("ends_ready"), 1)
            for e in range(EXPERTS):
                row = sp.value_load(ends[0:1, e:e + 1], min_val=0, max_val=(EXPERTS + 1) * REGION - 128)
                sp.dma_start(rows_d[bass.ds(row, 128), :], blank[:, e, :]).then_inc(sem("rows_blank"), 16)

            def first_row(j):
                return sp.value_load(base[0:1, bass.ds(j, 1)], min_val=0, max_val=(EXPERTS + 1) * REGION - 128)

            def load_xn(j, r, row):
                sp.wait_ge(sem("b_transposed"), count(j - TURNS + 1))
                sp.dma_start(XA[r], rows_d[bass.ds(row, 128), 0:D]).then_inc(sem(f"xa_loaded{r}"), 16)

            def load_x(j, r, row):
                sp.wait_ge(sem("b_y_ready"), count(j - TURNS + 1))
                sp.wait_ge(sem("b_numbered"), count(j - TURNS + 1))
                sp.dma_start(XB[r], rows_d[bass.ds(row, 128), D:RW]).then_inc(sem(f"xb_loaded{r}"), 16)

            sp.wait_ge(sem("expert_ready"), 1)
            sp.wait_ge(sem("rows_blank"), 16 * (2 + EXPERTS))
            sp.wait_ge(sem("scattered"), 16 * B)
            rows = {}

            def step(j, r, turn):
                if body["entered"]:
                    rows[(r + 1) % TURNS], rows[(r + 2) % TURNS] = first_row(j + 1), first_row(j + 2)
                    body["entered"] = False
                if not isinstance(j, int) or j + TURNS < BLOCKS:
                    rows[r] = first_row(j + TURNS)
                    load_xn(j + TURNS, r, rows[r])
                if not isinstance(j, int) or 0 <= j + 1 < BLOCKS:
                    load_x(j + 1, (r + 1) % TURNS, rows[(r + 1) % TURNS])

            block_loop(sp, step, -TURNS, BLOCKS)

        @block.tensor
        def _(pe):
            pe.wait_ge(sem("first_loaded"), FIRST_LOADED)

            def quantize_sums():
                for i in range(2):
                    pe.wait_ge(sem("abs_summed"), count(i + 1))
                    nc.tensor.matmul(bank[i][:, 0:1], ones[:], qred[:, i:i + 1], start=True, stop=True).then_inc(sem("abs_total"), 1)
                pe.wait_ge(sem("gate_unit"), count(5))
                nc.tensor.transpose(bank[2][0:GATE, 0:EXPERTS], wgs[:, 1, :], eye[0:EXPERTS, 0:EXPERTS]).then_inc(sem("gate_T"), 1)
                pe.wait_ge(sem("quantized"), 2)
                pe.wait_ge(sem("gate_unitT"), 1)


            def attention(L):
                T0, P0 = L * B, L * PAIRS
                n_kv = (HEADS, KV1)[L]
                m = n_kv * DK
                WQ, WK, WV, WO = ((W0[:, 0, :], W0[:, 2, :], W0[:, 4, :], W0[:, 5, :]) if L == 0 else
                                  (W1Q[:], W1K[:], W1V[:], W1O[:]))

                def xn_transposes(k):
                    p = pair(k)
                    if is_pair(p):
                        pe.wait_ge(sem("xn_ready"), 2 * (p + P0) + 2)
                        pe.wait_ge(sem("v_high"), count((p + P0) - 1))
                        for b in range(2):
                            mm = nc.tensor.transpose(XNT[:, b * S:(b + 1) * S], xn[:, b, :], eye[:])
                        mm.then_inc(sem("xn_transposed"), 1)

                def project_q(k, half):
                    p = pair(k)
                    if is_pair(p) and half <= 1 - L:
                        if half == 0:
                            pe.wait_ge(sem("xnT_ready"), p + P0 + 1)
                            if L == 0:
                                pe.wait_ge(sem("k_rotated"), count(2 * p))
                            else:
                                pe.wait_ge(sem("k_full"), p + P0)
                        mm = nc.tensor.matmul(QK[:, half * PAIR:(half + 1) * PAIR], W0[:, 1, :] if half else WQ, xnT[:],
                                              start=True, stop=True)
                        if half == 1 - L:
                            mm.then_inc(sem("q_projected"), 1)

                def project_k(k, half):
                    p, b = pair(k), turn(k)
                    if is_pair(p) and half <= 1 - L:
                        if half == 0:
                            pe.wait_ge(sem(f"ctx_loaded{L}{b}"), 16 * turns(k))
                            if L == 0:
                                pe.wait_ge(sem("q_rotated"), 2 * p + 2)
                            else:
                                pe.wait_ge(sem("q_full"), p + P0 + 1)
                        mm = nc.tensor.matmul(QK[0:m, half * PAIR:(half + 1) * PAIR], W0[:, 3, :] if half else WK, ctxT[b][:],
                                              start=True, stop=True)
                        if half == 1 - L:
                            mm.then_inc(sem("k_projected"), 1)

                def project_v(k):
                    p, b = pair(k), turn(k)
                    if is_pair(p):
                        pe.wait_ge(sem("v_high"), count(p + P0))
                        if is_pair(p + 1):
                            pe.wait_ge(sem("xnT_ready"), p + P0 + 2)
                        for h in range(2):
                            o = VAL[:, h * 128:h * 128 + m]
                            mm = nc.tensor.matmul(o, ctxT[b][:, h * S:(h + 1) * S], WV, start=True, stop=(L == 0))
                            if L:
                                mm = nc.tensor.matmul(o, ones[0:1, :], rowsb[0:1, 0, 0:m], start=False, stop=True)
                        mm.then_inc(sem("v_projected"), 1)

                def scores(t, c, k):
                    if not is_batch(t):
                        return
                    pb, tb = turn(k), k % 2
                    if c == 0:
                        pe.wait_ge(sem(f"q_stacked{L}{pb}"), 16 * SLOTS * turns(k))
                        pe.wait_ge(sem(f"k_stacked{L}{pb}"), 16 * SLOTS * turns(k))
                        if L:
                            pe.wait_ge(sem("mask_made"), pair(k) + 1)
                    pe.wait_ge(sem("maxima"), count(4 * (t + T0) + c - 1))
                    o = SCORE[c % 2]
                    if L:
                        nc.tensor.matmul(o[:].rearrange("p (h k) -> p h k", h=HQ), negI[:],
                                         mask[:, k % BODY, :].unsqueeze(1).broadcast_to([128, HQ, 128]),
                                         start=True, stop=False, skip_group_check=True)
                    for i in range(HQ):
                        h = c * HQ + i
                        kv = h if L == 0 else c
                        mm = nc.tensor.matmul(o[:, i * 128:(i + 1) * 128], Qs[pb][0:TERMS, h, tb * S:(tb + 1) * S],
                                              Ks[pb][0:TERMS, kv, tb * S:(tb + 1) * S],
                                              start=(L == 0), stop=True, skip_group_check=bool(L))
                    mm.then_inc(sem("scores_ready"), 1)

                def scoresT(t, c, k):
                    if not is_batch(t):
                        return
                    pb, tb = turn(k), k % 2
                    if c == 0:
                        pe.wait_ge(sem(f"max_rows{L}{tb}"), 16 * (pair(k) + 1))
                    pe.wait_ge(sem("exp_done"), count(2 * (4 * (t + T0) + c - 1)))
                    o = SCORET[c % 2]
                    if L:
                        nc.tensor.matmul(o[:].rearrange("p (h q) -> p h q", h=HQ), mask[:, k % BODY, :],
                                         negI[:].unsqueeze(1).broadcast_to([128, HQ, 128]),
                                         start=True, stop=False, skip_group_check=True)
                        mm = nc.tensor.matmul(o[:].rearrange("p (h q) -> p h q", h=HQ), Ks[pb][0:ROWS, c, tb * S:(tb + 1) * S],
                                              Qs[pb][0:ROWS, c * HQ:(c + 1) * HQ, tb * S:(tb + 1) * S],
                                              start=False, stop=True, skip_group_check=True)
                    else:
                        for i in range(HQ):
                            h = c * HQ + i
                            mm = nc.tensor.matmul(o[:, i * 128:(i + 1) * 128], Ks[pb][0:ROWS, h, tb * S:(tb + 1) * S],
                                                  Qs[pb][0:ROWS, h, tb * S:(tb + 1) * S], start=True, stop=True)
                    mm.then_inc(sem("scoresT_ready"), 1)

                def pv(t, c, k):
                    if not is_batch(t):
                        return
                    if c == 0:
                        pe.wait_ge(sem("pv_read"), count(t + T0))
                        pe.wait_ge(sem("v_split"), (pair(k) + P0) + 1)
                    if c == 1:
                        pe.wait_ge(sem("lows_dve"), t + T0 + 1)
                    else:
                        pe.wait_ge(sem("lows_pool"), 3 * (t + T0) + (1, 1, 2, 3)[c])
                    pe.wait_ge(sem("exp_done"), 8 * (t + T0) + 2 * c + 2)
                    for i in range(HQ):
                        h = c * HQ + i
                        for n, p in enumerate((Ph, Pl)):
                            mm = nc.tensor.matmul(PVOUT[:, h * VP:(h + 1) * VP], p[:, c, i * 128:(i + 1) * 128],
                                                  Vp[:, k % BODY, h if L == 0 else c, :, :].rearrange("p c e -> p (c e)"),
                                                  start=(n == 0), stop=(n == 1))
                    mm.then_inc(sem("pv_done"), 1)

                def max_transpose(t):
                    pe.wait_ge(sem("attn_added"), count((t + T0) - 3))
                    if is_batch(t):
                        pe.wait_ge(sem("negmax_split"), 4 * (t + T0) + 4)
                        pe.wait_ge(sem("negmaxT_ready"), count(t + T0))
                        nc.tensor.transpose(MAXT, negp[:].rearrange("p c h -> p (c h)"),
                                            eyeb[:]).then_inc(sem("negmax_transposed"), 1)

                def out_transpose(t):
                    if is_batch(t):
                        if L == 0:
                            pe.wait_ge(sem("out_norm0"), 2 * t + 2)
                        else:
                            pe.wait_ge(sem("out_centred"), t + 1)
                        pe.wait_ge(sem("outT_ready"), count(t + T0))
                        nc.tensor.transpose(OUTT, (onorm if L == 0 else oln)[:], eye[:]).then_inc(sem("out_transposed"), 1)

                def out_project(t):
                    if is_batch(t):
                        if is_batch(t + 3):
                            pe.wait_ge(sem("negmaxT_ready"), t + T0 + 4)
                        pe.wait_ge(sem("outT_ready"), t + T0 + 1)
                        mm = nc.tensor.matmul(OUTP, oT[:], WO, start=True, stop=(L == 0))
                        if L:
                            mm = nc.tensor.matmul(OUTP, ones[0:1, :], rowsb[0:1, 1, :], start=False, stop=True)
                        mm.then_inc(sem("out_projected"), 1)

                def project(j, half):
                    if j % 2 == 0:
                        project_q(j + 6, half)
                    else:
                        project_k(j + 5, half)

                def step(t, j):
                    scores(t + 2, 0, j + 2)
                    pv(t - 1, 1, j - 1)
                    scoresT(t, 0, j)
                    project(j, 0)
                    scoresT(t, 1, j)
                    scores(t + 2, 1, j + 2)
                    pv(t - 1, 2, j - 1)
                    project(j, 1)
                    scoresT(t, 2, j)
                    max_transpose(t + 1)
                    scores(t + 2, 2, j + 2)
                    out_transpose(t - 2)
                    pv(t - 1, 3, j - 1)
                    scoresT(t, 3, j)
                    scores(t + 2, 3, j + 2)
                    if j % 2 == 0:
                        project_v(j + 4)
                    else:
                        xn_transposes(j + 7)
                    out_project(t - 2)
                    pv(t, 0, j)

                return step
            def ffn(early):
                def transposes(p, b):
                    if is_pair(p):
                        pe.wait_ge(sem("f_xn_ready"), 2 * p + 2)
                        pe.wait_ge(sem("f_xnT_ready"), count(p - 1))
                        for h in range(2):
                            mm = nc.tensor.transpose(bank[b][:, h * S:(h + 1) * S], fxn[:, b, h, :], eye[:])
                        mm.then_inc(sem("f_transposed"), 1)

                def up(p, b):
                    if is_pair(p):
                        pe.wait_ge(sem("f_xnT_ready"), p + 1)
                        for c in range(FC):
                            if c % 2 == 0:
                                pe.wait_ge(sem("f_relu"), count(FC * (p - 1) + c + 2))
                            mm = nc.tensor.matmul(bank[2 + c // 2][:, c % 2 * PAIR:(c % 2 + 1) * PAIR], F1[:, c * 128:(c + 1) * 128],
                                                  fxnT[:, b, :], start=True, stop=True)
                            if c % 2 == 1:
                                mm.then_inc(sem("f_up"), 1)

                def down(p, b):
                    pe.wait_ge(sem("f_relu"), FC * (p + 1))
                    for h in range(2):
                        pe.wait_ge(sem("f_added"), count(2 * p + h - 1))
                        for c in range(FC):
                            mm = nc.tensor.matmul(bank[(4, 7)[h]][:, 0:128], hT[:, b, c, h * S:(h + 1) * S], F2[:, c, :],
                                                  start=(c == 0), stop=(c == FC - 1))
                        mm.then_inc(sem("f_down"), 1)

                def step(p, b):
                    transposes(p + 2, b)
                    up(p + 1, 1 - b)
                    down(p, b)
                    run_early(early, p)

                pe.wait_ge(sem("attn_added"), B)
                transposes(0, 0)
                transposes(1, 1)
                up(0, 0)
                pair_loop(pe, step)
                pe.wait_ge(sem("f_added"), 2 * PAIRS)

            def gate():
                G = B // 4

                def transposes(g):
                    pe.wait_ge(sem("m_xn_dve"), 3 * (g + 1))
                    pe.wait_ge(sem("m_xn_act"), g + 1)
                    pe.wait_ge(sem("m_xT_ready"), count(g - 1))
                    for h in range(4):
                        mm = nc.tensor.transpose(bank[g % 2][:, h * S:(h + 1) * S], XR[:, 4 * g + h, 0:D], eye[:])
                    mm.then_inc(sem("m_transposed"), 1)

                def reduced(g):
                    pe.wait_ge(sem("m_xT_ready"), g + 1)
                    pe.wait_ge(sem("m_reduced_read"), count(g - 1))
                    nc.tensor.matmul(bank[2 + g % 2][0:GATE, :], WG[:], mxT[g % 2], start=True, stop=True
                                     ).then_inc(sem("m_reduced"), 1)

                def logits(g):
                    pe.wait_ge(sem("m_reduced_read"), g + 1)
                    pe.wait_ge(sem("logits_centred"), count(g - 1))
                    for h in range(4):
                        mm = nc.tensor.matmul(bank[4 + g % 2][:, h * EXPERTS:(h + 1) * EXPERTS],
                                              xrT[g % 2][:, h * S:(h + 1) * S], wgT[:], start=True, stop=True)
                    mm.then_inc(sem("m_logits"), 1)

                def ranks(g):
                    pe.wait_ge(sem("chosen_ready"), g + 1)
                    pe.wait_ge(sem("ranks_read"), count(g - 1))
                    o = bank[6 + g % 2][:, 0:4 * EXPERTS]
                    ch = chosen[:, 4 * g:4 * g + 4, :]
                    mm = nc.tensor.matmul(o, before[:], ch.rearrange("p t e -> p (t e)"), start=True, stop=False, skip_group_check=True)
                    for i in range(3):
                        mm = nc.tensor.matmul(o[:, (i + 1) * EXPERTS:].rearrange("p (t e) -> p t e", e=EXPERTS), onesb[:],
                                              ch[:, i:i + 1, :].broadcast_to([128, 3 - i, EXPERTS]),
                                              start=False, stop=(g == 0 and i == 2), skip_group_check=True)
                    if g:
                        pe.wait_ge(sem("summed"), g)
                        mm = nc.tensor.matmul(o.rearrange("p (t e) -> p t e", e=EXPERTS), onesb[:],
                                              sums[:, g - 1:g, :].broadcast_to([128, 4, EXPERTS]),
                                              start=False, stop=True, skip_group_check=True)
                    mm.then_inc(sem("ranked"), 1)

                for g in range(G + 4):
                    if g < G:
                        transposes(g)
                    if 1 <= g <= G:
                        reduced(g - 1)
                    if 2 <= g < G + 2:
                        logits(g - 2)
                    if g >= 4:
                        ranks(g - 4)
                pe.wait_ge(sem("summed"), G)
                pe.wait_ge(sem("ranks_read"), G - 1)
                nc.tensor.matmul(bank[6][:, 0:EXPERTS], onesb[:], sums[:, G - 1, :], start=True, stop=True).then_inc(sem("counted"), 1)

            def experts():
                def step(j, r, turn):
                    n1, n2 = (r + 1) % TURNS, (r + 2) % TURNS
                    if not isinstance(j, int) or j + 2 < BLOCKS:
                        pe.wait_ge(sem(f"xa_loaded{n2}"), 16 * (turn + (r + 2) // TURNS))
                        pe.wait_ge(sem("b_xT_ready"), count(j + 2))
                        nc.tensor.transpose(bank[0][:, 0:128], XA[n2], eye[:]).then_inc(sem("b_transposed"), 1)
                    if not isinstance(j, int) or 0 <= j + 1 < BLOCKS:
                        if isinstance(j, int) and j + 2 >= BLOCKS:
                            pe.wait_ge(sem("b_xT_ready"), j + 2)
                        pe.wait_ge(sem("b_picked"), count(j + 2))
                        for c in range(FC):
                            mm = nc.tensor.matmul(bank[1 + n1][:, c * 128:(c + 1) * 128], W1e[n1][:, c * 128:(c + 1) * 128], bxT[n1],
                                                  start=True, stop=True)
                        mm.then_inc(sem("b_up"), 1)
                    if not isinstance(j, int) or 0 <= j < BLOCKS:
                        e = pe.value_load(expert[0:1, bass.ds(j, 1)], min_val=0, max_val=EXPERTS - 1)
                        pe.wait_ge(sem("b_y_ready"), count(j + 1 - TURNS))
                        nc.tensor.matmul(bank[4 + r][:, 0:D], thrice[:], bpieces[:, bass.ds(e, 1), :].rearrange("p o n -> p (o n)"),
                                         start=True, stop=False)
                        pe.wait_ge(sem("b_gelu"), count(j + 1))
                        for c in range(FC):
                            mm = nc.tensor.matmul(bank[4 + r][:, 0:D], bhT[r][:, c * 128:(c + 1) * 128],
                                                  M2[:, bass.ds(e, 1), c:c + 1, :].rearrange("p o c n -> p (o c n)"),
                                                  start=False, stop=(c == FC - 1))
                        mm.then_inc(sem("b_down"), 1)

                pe.wait_ge(sem("biases_cut"), 1)
                block_loop(pe, step, -2, BLOCKS)

            step = attention(0)
            for t in range(-AHEAD, START):
                run(step, t)
            pe.wait_ge(sem("weights_loaded"), LOADED)
            quantize_sums()
            body_loop(pe, step, START)
            early = attention(1)
            ffn(early)
            body_loop(pe, early, EARLY - AHEAD)
            gate()
            experts()

        @block.scalar
        def _(act):
            act.wait_ge(sem("ones_set"), 1)
            nc.scalar.activation(warm[:], ones[:, 0:1], ACT.Exp).then_inc(sem("warm"), 1)

            def attention(L):
                T0, P0 = L * B, L * PAIRS
                def evac_xnT(k):
                    p = pair(k)
                    if is_pair(p):
                        act.wait_ge(sem("xn_transposed"), p + P0 + 1)
                        act.wait_ge(sem("q_projected"), count(p + P0))
                        nc.scalar.copy(xnT[:], XNT).then_inc(sem("xnT_ready"), 1)

                def whole(k, which):
                    p = pair(k)
                    if is_pair(p):
                        m = (128, KV1 * DK)[which]
                        nm = "qk"[which]
                        act.wait_ge(sem(f"{nm}_projected"), p + P0 + 1)
                        act.wait_ge(sem(f"{nm}_pieces"), count(3 * (p + P0)))
                        nc.scalar.activation(full[which][0:m, :], QK[0:m, 0:PAIR], ACT.Identity, bias=cols[0:m, which:which + 1]
                                             ).then_inc(sem(f"{nm}_full"), 1)

                def high(k, which):
                    p = pair(k)
                    if is_pair(p):
                        m = 128 if L == 0 or which == 0 else KV1 * DK
                        nm = "qk"[which]
                        act.wait_ge(sem(f"{nm}_full"), p + P0 + 1)
                        act.wait_ge(sem(f"{nm}_stacked{L}{turn(k - 2)}"), count(16 * SLOTS * turns(k - 2)))
                        nc.scalar.copy(piece[which][0:m, 0, :], full[which][0:m, :]).then_inc(sem(f"{nm}_high"), 1)

                def values(k):
                    p = pair(k)
                    if is_pair(p):
                        n_kv = (HEADS, KV1)[L]
                        src = VAL.rearrange("p (b n) -> p b n", b=2)[:, :, 0:n_kv * DK]
                        j = k % BODY
                        act.wait_ge(sem("v_projected"), p + P0 + 1)
                        act.wait_ge(sem("v_split"), count(p + P0))
                        nc.scalar.copy(vfull[:, :, 0:n_kv * DK], src).then_inc(sem("v_full"), 1)
                        act.wait_ge(sem("pv_done"), count(8 * (p + P0) - 16))
                        nc.scalar.copy(Vp[:, j:j + 2, 0:n_kv, 0, 0:DK], src.rearrange("p b (h d) -> p b h d", d=DK)
                                       ).then_inc(sem("v_high"), 1)

                def exps(t, c):
                    if is_batch(t):
                        act.wait_ge(sem("scoresT_ready"), 4 * (t + T0) + c + 1)
                        act.wait_ge(sem("pv_done"), count(4 * (t + T0) + c - 3))
                        nc.scalar.activation(P32[:, c, :], SCORET[c % 2][:], ACT.Exp, scale=SCALE).then_inc(sem("exp_done"), 1)
                        nc.scalar.activation(Ph[:, c, :], SCORET[c % 2][:], ACT.Exp, scale=SCALE).then_inc(sem("exp_done"), 1)

                def evac_max(t, k):
                    if is_batch(t):
                        act.wait_ge(sem("negmax_transposed"), t + T0 + 1)
                        if is_batch(t - 3):
                            act.wait_ge(sem("out_transposed"), (t + T0) - 2)
                        act.wait_ge(sem(f"max_rows{L}{k % 2}"), count(16 * pair(k)))
                        nc.scalar.copy(negpT[k % 2][:], MAXT[0:3 * HEADS, :]).then_inc(sem("negmaxT_ready"), 1)

                def evac_out(t):
                    if is_batch(t):
                        act.wait_ge(sem("out_transposed"), t + T0 + 1)
                        act.wait_ge(sem("out_projected"), count(t + T0))
                        if L == 0:
                            nc.scalar.copy(oT[:], OUTT).then_inc(sem("outT_ready"), 1)
                        else:
                            nc.scalar.activation(oT[:], OUTT, ACT.Identity, bias=cols[:, 3:4], scale=cols[:, 2:3]
                                                 ).then_inc(sem("outT_ready"), 1)

                def normalise(k):
                    p = pair(k)
                    if is_pair(p):
                        act.wait_ge(sem("shifted"), 2 * (p + P0) + 2)
                        act.wait_ge(sem("xn_transposed"), count(p + P0))
                        for i in range(2):
                            x = X[:, 2 * p + i, :] if isinstance(p, int) else X[:, bass.ds(p * 2 + i, 1), :].rearrange("p o d -> p (o d)")
                            nc.scalar.activation(xn[:, i, :], x, ACT.Identity, bias=shift[:, i:i + 1], scale=rstd[:, i:i + 1]
                                                 ).then_inc(sem("xn_ready"), 1)

                def step(t, j):
                    exps(t, 0)
                    if j % 2 == 0:
                        high(j + 4, 1)
                    else:
                        high(j + 5, 0)
                        normalise(j + 7)
                    exps(t, 1)
                    evac_max(t + 1, j + 1)
                    evac_out(t - 2)
                    if L:
                        if j % 2 == 0:
                            whole(j + 6, 0)
                        else:
                            whole(j + 5, 1)
                    exps(t, 2)
                    if j % 2 == 0:
                        values(j + 4)
                    exps(t, 3)
                    if j % 2 == 1:
                        evac_xnT(j + 7)

                return step

            def ffn(early):
                def evac_xnT(p, b):
                    if is_pair(p):
                        act.wait_ge(sem("f_transposed"), p + 1)
                        act.wait_ge(sem("f_up"), count(2 * (p - 1)))
                        nc.scalar.copy(fxnT[:, b, :], bank[b][:, 0:PAIR]).then_inc(sem("f_xnT_ready"), 1)

                def relus(p, b):
                    if is_pair(p):
                        for c in range(FC):
                            act.wait_ge(sem("f_up"), 2 * p + c // 2 + 1)
                            act.wait_ge(sem("f_down"), count(2 * (p - 1)))
                            nc.scalar.activation(hT[:, b, c, :], bank[2 + c // 2][:, c % 2 * PAIR:(c % 2 + 1) * PAIR], ACT.Relu,
                                                 bias=F1b[:, c:c + 1]).then_inc(sem("f_relu"), 1)

                def step(p, b):
                    evac_xnT(p + 2, b)
                    relus(p + 1, 1 - b)
                    run_early(early, p)

                evac_xnT(0, 0)
                evac_xnT(1, 1)
                relus(0, 0)
                pair_loop(act, step)

            def gate():
                G = B // 4

                def normalise(g):
                    t = 4 * g + 3
                    nc.scalar.activation(XR[:, t, 0:D], X[:, t, :], ACT.Identity, bias=mshift[:, t:t + 1], scale=mrstd[:, t:t + 1]
                                         ).then_inc(sem("m_xn_act"), 1)

                act.wait_ge(sem("m_shifted"), 1)
                normalise(0)
                for g in range(G + 4):
                    if g >= 4:
                        k = 4 * (g - 4)
                        act.wait_ge(sem("logits_centred"), g - 3)
                        nc.scalar.activation(ex[:, k:k + 4, :], lg[:, k:k + 4, :], ACT.Exp).then_inc(sem("gate_exp"), 1)
                    if g + 1 < G:
                        normalise(g + 1)
                    if g < G:
                        act.wait_ge(sem("m_transposed"), g + 1)
                        act.wait_ge(sem("m_reduced"), count(g - 1))
                        nc.scalar.copy(mxT[g % 2], bank[g % 2][:]).then_inc(sem("m_xT_ready"), 1)
                    if 1 <= g <= G:
                        act.wait_ge(sem("m_reduced"), g)
                        act.wait_ge(sem("m_logits"), count(g - 2))
                        nc.scalar.copy(xrT[(g - 1) % 2][:], bank[2 + (g - 1) % 2][0:GATE, :]).then_inc(sem("m_reduced_read"), 1)

            def experts():
                def step(j, r, turn):
                    n1, n2 = (r + 1) % TURNS, (r + 2) % TURNS
                    if not isinstance(j, int) or j + 2 < BLOCKS:
                        act.wait_ge(sem("b_transposed"), count(j + 3))
                        nc.scalar.copy(bxT[n2], bank[0][:, 0:128]).then_inc(sem("b_xT_ready"), 1)
                    if not isinstance(j, int) or 0 <= j + 1 < BLOCKS:
                        act.wait_ge(sem("b_up"), count(j + 2))
                        for c in range(FC):
                            ins = nc.scalar.activation(bhT[n1][:, c * 128:(c + 1) * 128], bank[1 + n1][:, c * 128:(c + 1) * 128],
                                                       ACT.Gelu, bias=b1e[n1][:, c:c + 1])
                        ins.then_inc(sem("b_gelu"), 1)

                nc.scalar.activation(warm[:], ones[:, 0:1], ACT.Gelu).then_inc(sem("warm"), 1)
                block_loop(act, step, -2, BLOCKS)

            step = attention(0)
            for t in range(-AHEAD, START):
                run(step, t)
            act.wait_ge(sem("weights_loaded"), LOADED)
            body_loop(act, step, START)
            early = attention(1)
            ffn(early)
            body_loop(act, early, EARLY - AHEAD)
            gate()
            experts()

        @block.gpsimd
        def _(pool):
            nc.gpsimd.memset(powers[:, 0:4], -0.5).then_inc(sem("powers_set"), 1)
            nc.gpsimd.memset(powers[:, 4:5], 0.5).then_inc(sem("powers_set"), 1)
            nc.gpsimd.memset(powers[:, 5:9], LN_EPS).then_inc(sem("powers_set"), 1)
            nc.gpsimd.memset(blank[:], 0.0).then_inc(sem("zeros_set"), 1)
            pool.wait_ge(sem("powers_set"), 3)
            pool.wait_ge(sem("zeros_set"), 1)
            pool.wait_ge(sem("tails_cleared"), 1)
            nc.gpsimd.iota(XR[:].bitcast(I32)[:, :, TOKEN_AT:TOKEN_AT + 1].rearrange("p t o -> p (t o)"), pattern=[[S, B]], base=0,
                           channel_multiplier=1).then_inc(sem("tokens_numbered"), 1)


            def rstd_of(name, index, n, mv_, rs_, depth=1):
                pool.wait_ge(sem(name + "_stats"), count(2 * n * (index + 1)))
                pool.wait_ge(sem(name), count(n * (index + 1 - depth)))
                nc.gpsimd.tensor_tensor(rs_, mv_[:, :, 1:2].rearrange("p n o -> p (n o)"), powers[:, 5:5 + n], ALU.add).then_inc(sem(name + "_rstd"), 1)
                pool.wait_ge(sem(name + "_rstd"), 2 * index + 1)
                nc.gpsimd.tensor_tensor(rs_, rs_, powers[:, 0:n], ALU.pow).then_inc(sem(name + "_rstd"), 1)

            def attention(L):
                T0, P0 = L * B, L * PAIRS
                def whole(k, which):
                    p = pair(k)
                    if is_pair(p):
                        nm = "qk"[which]
                        pool.wait_ge(sem(f"{nm}_rotated"), 2 * p + 2)
                        pool.wait_ge(sem(f"{nm}_pieces"), count(3 * (p + P0)))
                        nc.gpsimd.tensor_tensor(full[which][:], rotA[which][:], rotB[which][:], ALU.add).then_inc(sem(f"{nm}_full"), 1)

                def cut(k, which):
                    p = pair(k)
                    if is_pair(p):
                        nm = "qk"[which]
                        m = 128 if L == 0 or which == 0 else KV1 * DK
                        h, f, r, pc = (piece[which][0:m, 0, :], full[which][0:m, :], rest[which][0:m, :], piece[which])
                        pool.wait_ge(sem(f"{nm}_high"), p + P0 + 1)
                        nc.gpsimd.tensor_tensor(pc[0:m, 1, :], f, h, ALU.subtract).then_inc(sem(f"{nm}_pieces"), 1)
                        nc.gpsimd.tensor_tensor(r, f, h, ALU.subtract).then_inc(sem(f"{nm}_pieces"), 1)
                        pool.wait_ge(sem(f"{nm}_pieces"), 3 * (p + P0) + 2)
                        nc.gpsimd.tensor_tensor(pc[0:m, 2, :], r, pc[0:m, 1, :], ALU.subtract).then_inc(sem(f"{nm}_pieces"), 1)

                def low(t, c):
                    if is_batch(t):
                        pool.wait_ge(sem("exp_done"), 8 * (t + T0) + 2 * c + 2)
                        pool.wait_ge(sem("pv_done"), count(4 * (t + T0) + c - 3))
                        nc.gpsimd.tensor_tensor(Pl[:, c, :], P32[:, c, :], Ph[:, c, :], ALU.subtract).then_inc(sem("lows_pool"), 1)

                def out_rstd(t):
                    if is_batch(t):
                        pool.wait_ge(sem("out_norm1"), 4 * t + 4)
                        pool.wait_ge(sem("out_centred"), count(t))
                        nc.gpsimd.tensor_tensor(orstd[:], omv[:, 1:2], powers[:, 5:6], ALU.add).then_inc(sem("out_rstd"), 1)
                        pool.wait_ge(sem("out_rstd"), 2 * t + 1)
                        nc.gpsimd.tensor_tensor(orstd[:], orstd[:], powers[:, 0:1], ALU.pow).then_inc(sem("out_rstd"), 1)

                def shift_of(p):
                    pool.wait_ge(sem("xn_ready_rstd"), 2 * (p + P0) + 2)
                    nc.gpsimd.tensor_tensor(shift[:], mv[:, :, 0], rstd[:], ALU.mult).then_inc(sem("shifted"), 1)
                    pool.wait_ge(sem("shifted"), 2 * (p + P0) + 1)
                    nc.gpsimd.tensor_tensor(shift[:], zero[:, 0:2], shift[:], ALU.subtract).then_inc(sem("shifted"), 1)

                def step(t, j):
                    k, which = (j + 4, 1) if j % 2 == 0 else (j + 5, 0)
                    if L == 0:
                        whole(k, which)
                    else:
                        out_rstd(t - 2)
                    low(t - 1, 3)
                    low(t, 0)
                    cut(k, which)
                    if j % 2 == 0 and is_pair(pair(j + 8)):
                        rstd_of("xn_ready", pair(j + 8) + P0, 2, mv, rstd[:])
                        shift_of(pair(j + 8))
                    low(t, 2)

                return step

            step = attention(0)
            run(step, -AHEAD)
            for i in range(3):
                nc.gpsimd.memset(Qs[i][0:TERMS], 0.0).then_inc(sem("stacks_cleared"), 1)
            for t in range(-AHEAD + 1, START):
                run(step, t)
            pool.wait_ge(sem("gate_unit"), 2)
            nc.gpsimd.tensor_tensor(wgn[:, 1:2], wgn[:, 0:1], powers[0:EXPERTS, 4:5], ALU.pow).then_inc(sem("gate_norm"), 1)
            body_loop(pool, step, START)
            early = attention(1)

            def ffn_rstd(p, b):
                if is_pair(p):
                    rstd_of("f_xn_ready", p, 2, fmv[:, b], frstd[:, b], 2)

            def ffn_bias(p):
                if is_pair(p):
                    pool.wait_ge(sem("f_xn_ready"), 2 * p + 2)
                    x = X[:, 2 * p:2 * p + 2, :] if isinstance(p, int) else X[:, bass.ds(p * 2, 2), :]
                    nc.gpsimd.tensor_tensor(x, x, rowsb[:, 2:3, :].broadcast_to([128, 2, 128]), ALU.add).then_inc(sem("f_biased"), 1)

            def ffn_step(p, b):
                ffn_rstd(p + 4, b)
                ffn_bias(p + 2)
                run_early(early, p)

            pool.wait_ge(sem("weights_loaded"), LOADED)
            for p in range(4):
                ffn_rstd(p, p % 2)
            ffn_bias(0)
            ffn_bias(1)
            pair_loop(pool, ffn_step)
            body_loop(pool, early, EARLY - AHEAD)
            pool.wait_ge(sem("m_stats"), 2 * B)
            nc.gpsimd.tensor_tensor(mrstd[:], mmv[:, :, 1], powers[:, 5:6].broadcast_to([128, B]), ALU.add).then_inc(sem("m_rstd"), 1)
            pool.wait_ge(sem("m_rstd"), 1)
            nc.gpsimd.tensor_tensor(mrstd[:], mrstd[:], powers[:, 0:1].broadcast_to([128, B]), ALU.pow).then_inc(sem("m_rstd"), 1)
            pool.wait_ge(sem("tokens_numbered"), 1)
            for t in range(B):
                if t % 4 == 0:
                    pool.wait_ge(sem("slots_ready"), t // 4 + 1)
                    pool.wait_ge(sem("scored"), t // 4 + 1)
                nc.gpsimd.indirect_dma_start(out=rows_d, out_offset=bass.IndirectOffsetOnAxis(ap=sloti[:, t:t + 1], axis=0),
                                             in_=XR[:, t, :], in_offset=None).then_inc(sem("scattered"), 16)

            def step(j, r, turn):
                pool.wait_ge(sem(f"xb_loaded{r}"), 16 * turn)
                pool.wait_ge(sem(f"gone_out{r}"), count(16 * (turn - 1)))
                pool.sem_inc(sem("numbering"), 1)
                nc.gpsimd.tensor_copy(by[r].bitcast(I32)[:, D:D + 1], XB[r].bitcast(I32)[:, TOKEN_AT - D:TOKEN_AT - D + 1]
                                      ).then_inc(sem("b_numbered"), 1)
                pool.wait_ge(sem("b_numbered"), count(j + 1))
                pool.wait_ge(sem("b_y_ready"), count(j + 1))
                pool.sem_inc(sem("going_out"), 1)
                at_ = by[r].bitcast(I32)[:, D:D + 1]
                nc.gpsimd.indirect_dma_start(out=out, out_offset=bass.IndirectOffsetOnAxis(ap=at_, axis=0),
                                             in_=by[r][:, 0:D], in_offset=None).then_inc(sem(f"gone_out{r}"), 16)

            block_loop(pool, step, 0, BLOCKS)
            for r in range(TURNS):
                pool.wait_ge(sem(f"gone_out{r}"), 16 * (BLOCKS // TURNS))

        @block.vector
        def _(dve):
            nc.vector.memset(ones[:], 1.0).then_inc(sem("ones_set"), 1)
            nc.vector.memset(XR[:, :, SCORE_AT:RW], 0.0).then_inc(sem("tails_cleared"), 1)
            nc.vector.memset(onesb[:], 1.0).then_inc(sem("ones_set"), 1)
            nc.vector.memset(first[:], 0.0).then_inc(sem("ones_set"), 1)
            nc.vector.memset(negp[:], 0.0).then_inc(sem("ones_set"), 1)
            nc.vector.memset(Vp[:, :, :, 1:3, DK], 0.0).then_inc(sem("ones_set"), 1)
            nc.vector.memset(Vp[:, :, :, 0, DK], 1.0).then_inc(sem("ones_set"), 1)
            dve.wait_ge(sem("ones_set"), 6)
            nc.vector.memset(first[0:1, 2, EXPERTS:EXPERTS + 1], -128.0 * B).then_inc(sem("ones_set"), 1)
            dve.wait_ge(sem("ones_set"), 7)

            def norm_stats(name, index, n, src, st_, mv_):
                for i in range(n):
                    nc.vector.bn_stats(st_[:, i, :], src(i)).then_inc(sem(name + "_stats"), 1)
                dve.wait_ge(sem(name + "_stats"), index * 2 * n + n)
                dve.sem_inc(sem("stats_seen"), 1)
                for i in range(n):
                    nc.vector.bn_aggr(mv_[:, i, :], st_[:, i, :]).then_inc(sem(name + "_stats"), 1)

            def norm_apply(name, index, n, src, mv_, rs_, dst):
                dve.wait_ge(sem(name + "_rstd"), count(2 * (index + 1)))
                for i in range(n):
                    nc.vector.tensor_scalar(dst(i), src(i), mv_[:, i, 0:1], rs_[:, i:i + 1], ALU.subtract, ALU.mult
                                            ).then_inc(sem(name), 1)

            def attention(L):
                T0, P0 = L * B, L * PAIRS
                n_kv = (HEADS, KV1)[L]
                NORM = (2, 4)[L]

                def x_of(p):
                    if isinstance(p, int):
                        return lambda i: X[:, 2 * p + i, :]
                    return lambda i: X[:, bass.ds(p * 2 + i, 1), :].rearrange("p o d -> p (o d)")

                def x_stats(k):
                    p = pair(k)
                    if is_pair(p):
                        dve.wait_ge(sem("xn_ready"), count(2 * (p + P0)))
                        norm_stats("xn_ready", p + P0, 2, x_of(p), stats, mv)

                def rotate(k, which):
                    p = pair(k)
                    if not is_pair(p):
                        return
                    nm = "qk"[which]
                    dve.wait_ge(sem(f"{nm}_projected"), p + P0 + 1)
                    dve.wait_ge(sem(f"{nm}_full"), count(p + P0))
                    for tab, dst, off in ((cosT, rotA, 0), (sinT, rotB, PAIR)):
                        ins = nc.vector.tensor_tensor(
                            dst[which][:].rearrange("p (b s) -> p b s", b=2),
                            QK[:, off:off + PAIR].rearrange("p (b s) -> p b s", b=2),
                            tab[:].unsqueeze(1).broadcast_to([128, 2, 128]), ALU.mult)
                        ins.then_inc(sem(f"{nm}_rotated"), 1)

                def split_v(k):
                    p, j = pair(k), k % BODY
                    if not is_pair(p):
                        return
                    m = n_kv * DK
                    f, r = vfull[:, :, 0:m], vrest[:, :, 0:m]

                    def pieces(c):
                        return Vp[:, j:j + 2, 0:n_kv, c, 0:DK]

                    def heads(ap):
                        return ap.rearrange("p b (h d) -> p b h d", d=DK)

                    dve.wait_ge(sem("v_high"), p + P0 + 1)
                    nc.vector.tensor_tensor(heads(r), heads(f), pieces(0), ALU.subtract).then_inc(sem("v_rest"), 1)
                    nc.vector.tensor_tensor(pieces(1), heads(f), pieces(0), ALU.subtract).then_inc(sem("v_rest"), 1)
                    dve.wait_ge(sem("v_rest"), 2 * (p + P0) + 2)
                    nc.vector.tensor_tensor(pieces(2), heads(r), pieces(1), ALU.subtract).then_inc(sem("v_split"), 1)

                def make_mask(k):
                    p = pair(k)
                    if not is_pair(p):
                        return
                    dve.wait_ge(sem(f"adj_loaded{turn(k)}"), 16 * turns(k))
                    dve.wait_ge(sem("scoresT_ready"), count(8 * (p + P0) - 16))
                    for i in range(2):
                        ins = nc.vector.scalar_tensor_tensor(mask[:, (k + i) % BODY, :], adj[turn(k)][:, i, :], 0.0, upper[:],
                                                             ALU.is_equal, ALU.max)
                    ins.then_inc(sem("mask_made"), 1)

                def maxima(t, c, k):
                    if is_batch(t):
                        dve.wait_ge(sem("scores_ready"), 4 * (t + T0) + c + 1)
                        nc.vector.tensor_reduce(negmax[:, k % 2, c * HQ:(c + 1) * HQ], SCORE[c % 2][:].rearrange("p (h k) -> p h k", h=HQ),
                                                AX.X, ALU.max, negate=True).then_inc(sem("maxima"), 1)

                def split_max_high(t, k):
                    if is_batch(t):
                        dve.wait_ge(sem("maxima"), 4 * (t + T0) + 4)
                        dve.wait_ge(sem("negmax_transposed"), count(t + T0))
                        nc.vector.tensor_copy(negp[:, 0, :], negmax[:, k % 2, :]).then_inc(sem("negmax_split"), 1)

                def split_max_rest(t, k):
                    if is_batch(t):
                        dve.wait_ge(sem("negmax_split"), 4 * (t + T0) + 1)
                        nm = negmax[:, k % 2, :]
                        nc.vector.tensor_tensor(negrest[:], nm, negp[:, 0, :], ALU.subtract).then_inc(sem("negmax_split"), 1)
                        nc.vector.tensor_tensor(negp[:, 1, :], nm, negp[:, 0, :], ALU.subtract).then_inc(sem("negmax_split"), 1)
                        dve.wait_ge(sem("negmax_split"), 4 * (t + T0) + 3)
                        nc.vector.tensor_tensor(negp[:, 2, :], negrest[:], negp[:, 1, :], ALU.subtract).then_inc(sem("negmax_split"), 1)

                def sum_pieces(t):
                    if is_batch(t):
                        dve.wait_ge(sem("pv_done"), 4 * (t + T0) + 4)
                        nc.vector.tensor_reduce(osum[:], PVOUT[:, 0:HEADS * VP].rearrange("p (h c e) -> p h e c", c=3, e=VW),
                                                AX.X, ALU.add).then_inc(sem("pv_read"), 1)

                def denominators(t):
                    if is_batch(t):
                        dve.wait_ge(sem("pv_read"), t + T0 + 1)
                        nc.vector.reciprocal(rden[:], osum[:, :, DK:VW].rearrange("p h o -> p (h o)")).then_inc(sem(f"out_norm{L}"), 1)

                def norm_out(t):
                    if is_batch(t):
                        if L == 0:
                            dve.wait_ge(sem("out_transposed"), count(t + T0))
                        dve.wait_ge(sem(f"out_norm{L}"), NORM * t + 1)
                        nc.vector.tensor_tensor(onorm[:].rearrange("p (h d) -> p h d", d=DK), osum[:, :, 0:DK],
                                                rden[:].unsqueeze(2).broadcast_to([128, HEADS, DK]), ALU.mult).then_inc(sem(f"out_norm{L}"), 1)

                def out_stats(t):
                    if is_batch(t):
                        dve.wait_ge(sem(f"out_norm{L}"), NORM * t + 2)
                        nc.vector.bn_stats(ostat[:], onorm[:]).then_inc(sem(f"out_norm{L}"), 1)
                        dve.wait_ge(sem(f"out_norm{L}"), NORM * t + 3)
                        dve.sem_inc(sem("stats_seen"), 1)
                        nc.vector.bn_aggr(omv[:], ostat[:]).then_inc(sem(f"out_norm{L}"), 1)

                def centre_out(t):
                    if is_batch(t):
                        dve.wait_ge(sem("out_rstd"), 2 * t + 2)
                        dve.wait_ge(sem("out_transposed"), count(t + T0))
                        nc.vector.tensor_scalar(oln[:], onorm[:], omv[:, 0:1], orstd[:], ALU.subtract, ALU.mult
                                                ).then_inc(sem("out_centred"), 1)

                def low(t, c):
                    if is_batch(t):
                        dve.wait_ge(sem("exp_done"), 8 * (t + T0) + 2 * c + 2)
                        dve.wait_ge(sem("pv_done"), count(4 * (t + T0) + c - 3))
                        nc.vector.tensor_tensor(Pl[:, c, :], P32[:, c, :], Ph[:, c, :], ALU.subtract).then_inc(sem("lows_dve"), 1)

                def add_out(t):
                    if is_batch(t):
                        dve.wait_ge(sem("out_projected"), t + T0 + 1)
                        x = X[:, t, :] if isinstance(t, int) else X[:, bass.ds(t, 1), :].rearrange("p o d -> p (o d)")
                        nc.vector.tensor_tensor(x, x, OUTP, ALU.add).then_inc(sem("attn_added"), 1)

                def tile_stats(t):
                    if is_batch(t):
                        dve.wait_ge(sem("attn_added"), t + T0 + 1)
                        x = X[:, t, :] if isinstance(t, int) else X[:, bass.ds(t, 1), :].rearrange("p o d -> p (o d)")
                        st = mstats[:, t, :] if isinstance(t, int) else mstats[:, bass.ds(t, 1), :].rearrange("p o d -> p (o d)")
                        nc.vector.bn_stats(st, x).then_inc(sem("m_stats"), 1)

                def step(t, j):
                    split_max_high(t + 1, j + 1)
                    add_out(t - 3)
                    split_max_rest(t + 1, j + 1)
                    maxima(t + 2, 0, j + 2)
                    if L:
                        centre_out(t - 2)
                    if j % 2 == 0:
                        x_stats(j + 8)
                    else:
                        split_v(j + 3)
                        if L:
                            make_mask(j + 3)
                    maxima(t + 2, 1, j + 2)
                    if L == 0:
                        if j % 2 == 0:
                            rotate(j + 6, 0)
                        else:
                            rotate(j + 5, 1)
                    low(t, 1)
                    sum_pieces(t - 1)
                    maxima(t + 2, 2, j + 2)
                    denominators(t - 1)
                    maxima(t + 2, 3, j + 2)
                    norm_out(t - 1)
                    if L:
                        tile_stats(t - 3)
                    if L:
                        out_stats(t - 1)

                return step

            def ffn(early):
                def x_of(p):
                    if isinstance(p, int):
                        return lambda i: X[:, 2 * p + i, :]
                    return lambda i: X[:, bass.ds(p * 2 + i, 1), :].rearrange("p o d -> p (o d)")

                def stats_of(p, b):
                    if is_pair(p):
                        norm_stats("f_xn_ready", p, 2, x_of(p), fstats[:, b], fmv[:, b])

                def normalise(p, b):
                    if is_pair(p):
                        dve.wait_ge(sem("f_transposed"), count(p - 1))
                        norm_apply("f_xn_ready", p, 2, x_of(p), fmv[:, b], frstd[:, b], lambda i: fxn[:, b, i, :])

                def add(p):
                    dve.wait_ge(sem("f_biased"), p + 1)
                    for h in range(2):
                        dve.wait_ge(sem("f_down"), 2 * p + h + 1)
                        x = x_of(p)(h)
                        nc.vector.tensor_tensor(x, x, bank[(4, 7)[h]][:, 0:128], ALU.add).then_inc(sem("f_added"), 1)

                def step(p, b):
                    stats_of(p + 4, b)
                    normalise(p + 3, 1 - b)
                    add(p)
                    run_early(early, p)

                dve.wait_ge(sem("attn_added"), B)
                stats_of(0, 0)
                for p in range(3):
                    stats_of(p + 1, (p + 1) % 2)
                    normalise(p, p % 2)
                pair_loop(dve, step)
                dve.wait_ge(sem("f_added"), 2 * PAIRS)

            def gate():
                G = B // 4
                dve.wait_ge(sem("attn_added"), 2 * B)
                dve.wait_ge(sem("m_stats"), B)
                for t in range(B):
                    nc.vector.bn_aggr(mmv[:, t, :], mstats[:, t, :]).then_inc(sem("m_stats"), 1)
                dve.wait_ge(sem("m_stats"), 2 * B)
                dve.wait_ge(sem("m_rstd"), 2)
                nc.vector.scalar_tensor_tensor(mshift[:], mmv[:, :, 0], -1.0, mrstd[:], ALU.mult, ALU.mult).then_inc(sem("m_shifted"), 1)
                per = [128, 4, EXPERTS]
                ranks = rank[:].unsqueeze(1).broadcast_to(per)

                def choose(g):
                    tiles = slice(4 * g, 4 * g + 4)
                    src = bank[4 + g % 2][:, 0:4 * EXPERTS].rearrange("p (h e) -> p h e", h=4)
                    dve.wait_ge(sem("m_logits"), g + 1)
                    nc.vector.tensor_reduce(top[:, 0, tiles], src, AX.X, ALU.max, negate=True).then_inc(sem("topped"), 1)
                    dve.wait_ge(sem("topped"), 3 * g + 1)
                    nc.vector.tensor_tensor(lg[:, tiles, :], src, top[:, 0, tiles].unsqueeze(2).broadcast_to(per), ALU.add
                                            ).then_inc(sem("logits_centred"), 1)
                    dve.wait_ge(sem("logits_centred"), g + 1)
                    nc.vector.scalar_tensor_tensor(cand[:, tiles, :], lg[:, tiles, :], 0.0, ranks, ALU.is_ge, ALU.mult).then_inc(sem("topped"), 1)
                    dve.wait_ge(sem("topped"), 3 * g + 2)
                    nc.vector.tensor_reduce(top[:, 1, tiles], cand[:, tiles, :], AX.X, ALU.max).then_inc(sem("topped"), 1)
                    dve.wait_ge(sem("topped"), 3 * g + 3)
                    nc.vector.tensor_tensor(chosen[:, tiles, :], ranks, top[:, 1, tiles].unsqueeze(2).broadcast_to(per), ALU.is_equal
                                            ).then_inc(sem("chosen_ready"), 1)
                    dve.wait_ge(sem("chosen_ready"), g + 1)
                    with nc.allow_low_precision("counts up to B are exact"):
                        nc.vector.tensor_reduce(sums[:, g, :], chosen[:, 0:4 * g + 4, :].rearrange("p t e -> p e t"), AX.X, ALU.add
                                                ).then_inc(sem("summed"), 1)

                def place_of(g):
                    tiles = slice(4 * g, 4 * g + 4)
                    dve.wait_ge(sem("gate_exp"), g + 1)
                    nc.vector.tensor_reduce(top[:, 2, tiles], ex[:, tiles, :], AX.X, ALU.add).then_inc(sem("gate_summed"), 1)
                    dve.wait_ge(sem("ranked"), g + 1)
                    nc.vector.tensor_tensor(product[:, tiles, :], bank[6 + g % 2][:, 0:4 * EXPERTS].rearrange("p (t e) -> p t e", e=EXPERTS),
                                            chosen[:, tiles, :], ALU.mult).then_inc(sem("ranks_read"), 1)
                    dve.wait_ge(sem("gate_summed"), g + 1)
                    dve.wait_ge(sem("tokens_numbered"), 1)
                    nc.vector.reciprocal(XR[:, tiles, SCORE_AT], top[:, 2, tiles]).then_inc(sem("scored"), 1)
                    dve.wait_ge(sem("ranks_read"), g + 1)
                    nc.vector.tensor_reduce(order[:, tiles], product[:, tiles, :], AX.X, ALU.add).then_inc(sem("ordered"), 1)
                    dve.wait_ge(sem("ordered"), g + 1)
                    nc.vector.scalar_tensor_tensor(sloti[:, tiles], top[:, 1, tiles], float(REGION), order[:, tiles], ALU.mult, ALU.add
                                                   ).then_inc(sem("slots_ready"), 1)

                for g in range(G + 4):
                    if g < G:
                        for t in range(4 * g, 4 * g + 3):
                            nc.vector.tensor_scalar(XR[:, t, 0:D], X[:, t, :], mmv[:, t, 0:1], mrstd[:, t:t + 1], ALU.subtract, ALU.mult
                                                    ).then_inc(sem("m_xn_dve"), 1)
                    if 3 <= g < G + 3:
                        choose(g - 3)
                    if g >= 4:
                        place_of(g - 4)

                dve.wait_ge(sem("counted"), 1)
                c = bank[6][:, 0:EXPERTS]
                n = first[:, 1, 0:EXPERTS]
                nc.vector.tensor_scalar(n, c, 63.5, 1.0 / 128, ALU.add, ALU.mult).then_inc(sem("placing"), 1)
                nc.vector.scalar_tensor_tensor(ends[:], rank[0:1, :], float(REGION), c[0:1, :], ALU.mult, ALU.add).then_inc(sem("ends_ready"), 1)
                dve.wait_ge(sem("placing"), 1)
                nc.vector.tensor_scalar(n, n, BIG_ROUND, None, ALU.add).then_inc(sem("placing"), 1)
                dve.wait_ge(sem("placing"), 2)
                nc.vector.tensor_scalar(n, n, BIG_ROUND, None, ALU.subtract).then_inc(sem("placing"), 1)
                dve.wait_ge(sem("placing"), 3)
                nc.vector.tensor_tensor_scan(first[:, 0, 1:EXPERTS + 1], n, zero[:, 0:EXPERTS], 0.0, ALU.add, ALU.add).then_inc(sem("placing"), 1)
                dve.wait_ge(sem("placing"), 4)
                over = [1, BLOCKS, EXPERTS]
                nc.vector.tensor_tensor(past[:, 0], blk[:].unsqueeze(2).broadcast_to(over),
                                        first[0:1, 0, 1:EXPERTS + 1].unsqueeze(1).broadcast_to(over), ALU.is_ge).then_inc(sem("placing"), 1)
                nc.vector.scalar_tensor_tensor(first[0:1, 2, 0:EXPERTS], rank[0:1, :], float(REGION), zero[0:1, 0:EXPERTS],
                                               ALU.mult, ALU.add).then_inc(sem("placing"), 1)
                dve.wait_ge(sem("placing"), 6)
                nc.vector.scalar_tensor_tensor(first[0:1, 2, 0:EXPERTS], first[0:1, 0, 0:EXPERTS], -128.0, first[0:1, 2, 0:EXPERTS],
                                               ALU.mult, ALU.add).then_inc(sem("placing"), 1)
                nc.vector.tensor_reduce(place[:, 0, :], past[:, 0], AX.X, ALU.add).then_inc(sem("placing"), 1)
                dve.wait_ge(sem("placing"), 8)
                nc.vector.tensor_scalar(expert[:], place[:, 0, :], float(EXPERTS - 1), None, ALU.min).then_inc(sem("placing"), 1)
                nc.vector.tensor_tensor(steps[:], first[0:1, 2, 1:EXPERTS + 1], first[0:1, 2, 0:EXPERTS], ALU.subtract).then_inc(sem("placing"), 1)
                dve.wait_ge(sem("placing"), 10)
                nc.vector.tensor_tensor(past[:, 1], past[:, 0], steps[:].unsqueeze(1).broadcast_to(over), ALU.mult).then_inc(sem("placing"), 1)
                dve.wait_ge(sem("placing"), 11)
                nc.vector.tensor_reduce(place[:, 1, :], past[:, 1], AX.X, ALU.add).then_inc(sem("placing"), 1)
                dve.wait_ge(sem("placing"), 12)
                nc.vector.scalar_tensor_tensor(place[:, 2, :], blk[:], 128.0, place[:, 1, :], ALU.mult, ALU.add).then_inc(sem("placing"), 1)
                dve.wait_ge(sem("placing"), 13)
                nc.vector.tensor_scalar(base[:], place[:, 2, :], float(EXPERTS * REGION), None, ALU.add).then_inc(sem("expert_ready"), 1)

            def experts():
                def step(j, r, turn):
                    n2 = (r + 2) % TURNS
                    if not isinstance(j, int) or 0 <= j + 2 < BLOCKS:
                        e = dve.value_load(expert[0:1, bass.ds(j + 2, 1)], min_val=0, max_val=EXPERTS - 1)
                        nc.vector.tensor_copy(b1e[n2], M1b[:, bass.ds(e, 1), :].rearrange("p o c -> p (o c)")).then_inc(sem("b_bias"), 1)
                        nc.vector.tensor_copy(W1e[n2], M1[:, bass.ds(e, 1), :].rearrange("p o n -> p (o n)")).then_inc(sem("b_picked"), 1)
                    if not isinstance(j, int) or 0 <= j < BLOCKS:
                        dve.wait_ge(sem("b_down"), count(j + 1))
                        dve.wait_ge(sem(f"xb_loaded{r}"), 16 * turn)
                        dve.wait_ge(sem(f"gone_out{r}"), count(16 * (turn - 1)))
                        nc.vector.scalar_tensor_tensor(by[r][:, 0:D], bank[4 + r][:, 0:D], XB[r][:, SCORE_AT - D:SCORE_AT - D + 1],
                                                       XB[r][:, 0:D], ALU.mult, ALU.add).then_inc(sem("b_y_ready"), 1)

                dve.wait_ge(sem("expert_ready"), 1)
                dve.wait_ge(sem("experts_loaded"), EXPERTS_LOADED)
                nc.vector.memset(thrice[:], 0.0).then_inc(sem("bias_cut"), 1)
                nc.vector.tensor_copy(bpieces[:], M2b[:]).then_inc(sem("bias_cut"), 1)
                dve.wait_ge(sem("bias_cut"), 2)
                for k in range(3):
                    nc.vector.memset(thrice[32 * k:32 * k + 1, :], 1.0).then_inc(sem("bias_cut"), 1)
                nc.vector.tensor_tensor(brest[:], M2b[:], bpieces[:], ALU.subtract).then_inc(sem("bias_cut"), 1)
                dve.wait_ge(sem("bias_cut"), 6)
                nc.vector.tensor_copy(bpieces[32:64], brest[32:64]).then_inc(sem("bias_cut"), 1)
                nc.vector.tensor_copy(bpieces[64:96], brest[64:96]).then_inc(sem("bias_cut"), 1)
                dve.wait_ge(sem("bias_cut"), 8)
                nc.vector.tensor_tensor(brest[64:96], brest[64:96], bpieces[64:96], ALU.subtract).then_inc(sem("bias_cut"), 1)
                dve.wait_ge(sem("bias_cut"), 9)
                nc.vector.tensor_copy(bpieces[64:96], brest[64:96]).then_inc(sem("biases_cut"), 1)
                block_loop(dve, step, -2, BLOCKS)

            step = attention(0)
            dve.wait_ge(sem("x_loaded0"), 16)
            run(step, -AHEAD)
            for i in range(3):
                nc.vector.memset(Ks[i][0:TERMS], 0.0).then_inc(sem("stacks_cleared"), 1)
            dve.wait_ge(sem("first_loaded"), FIRST_LOADED)
            for t in range(-AHEAD + 1, START):
                run(step, t)
            dve.wait_ge(sem("weights_loaded"), LOADED)
            dve.wait_ge(sem("zeros_set"), 1)
            for c in range(1, X_CHUNKS):
                dve.wait_ge(sem(f"x_loaded{c}"), 16)
            FW = (F1[:], F2[:].rearrange("p c n -> p (c n)"))
            for i, w in enumerate(FW):
                nc.vector.tensor_reduce(qred[:, i:i + 1], w, AX.X, ALU.add, apply_absolute_value=True).then_inc(sem("abs_summed"), 1)
            for i, w in enumerate(FW):
                dve.wait_ge(sem("abs_total"), i + 1)
                nc.vector.tensor_scalar(qgam[:, i:i + 1], bank[i][:, 0:1], 1.0 / (FF * D), 1e-5, ALU.mult, ALU.add).then_inc(sem(f"quant{i}"), 1)
                dve.wait_ge(sem(f"quant{i}"), 1)
                nc.vector.reciprocal(qred[:, i:i + 1], qgam[:, i:i + 1]).then_inc(sem(f"quant{i}"), 1)
                dve.wait_ge(sem(f"quant{i}"), 2)
                nc.vector.tensor_scalar(w, w, qred[:, i:i + 1], 1.0, ALU.mult, ALU.min).then_inc(sem(f"quant{i}"), 1)
                dve.wait_ge(sem(f"quant{i}"), 3)
                nc.vector.tensor_scalar(w, w, -1.0, BIG_ROUND, ALU.max, ALU.add).then_inc(sem(f"quant{i}"), 1)
                dve.wait_ge(sem(f"quant{i}"), 4)
                nc.vector.tensor_scalar(w, w, BIG_ROUND, None, ALU.subtract).then_inc(sem("quantized"), 1)
            nc.vector.tensor_tensor(wgs[:, 0, :], wgr[:], wgr[:], ALU.mult).then_inc(sem("gate_unit"), 1)
            dve.wait_ge(sem("gate_unit"), 1)
            nc.vector.tensor_reduce(wgn[:, 0:1], wgs[:, 0, :], AX.X, ALU.add).then_inc(sem("gate_unit"), 1)
            dve.wait_ge(sem("gate_unit"), 2)
            dve.wait_ge(sem("gate_norm"), 1)
            nc.vector.tensor_scalar(wgn[:, 2:3], wgn[:, 1:2], 1e-4, None, ALU.max).then_inc(sem("gate_unit"), 1)
            dve.wait_ge(sem("gate_unit"), 3)
            nc.vector.reciprocal(wgn[:, 0:1], wgn[:, 2:3]).then_inc(sem("gate_unit"), 1)
            dve.wait_ge(sem("gate_unit"), 4)
            nc.vector.tensor_scalar(wgs[:, 1, :], wgr[:], wgn[:, 0:1], None, ALU.mult).then_inc(sem("gate_unit"), 1)
            dve.wait_ge(sem("gate_T"), 1)
            nc.vector.tensor_copy(wgT[:], bank[2][0:GATE, 0:EXPERTS]).then_inc(sem("gate_unitT"), 1)
            body_loop(dve, step, START)
            early = attention(1)
            ffn(early)
            body_loop(dve, early, EARLY - AHEAD)
            gate()
            experts()


def rope_tables():
    inv = (1.0 / np.power(np.float32(10000.0), np.arange(0, DK, 2, dtype=np.float32) / np.float32(DK))).astype(np.float32)
    f = np.outer(np.arange(S, dtype=np.float32), inv).astype(np.float32)
    c, s = np.cos(f).astype(np.float32), np.sin(f).astype(np.float32)
    cosT = np.zeros((DK, HEADS, S), np.float32)
    sinT = np.zeros((DK, HEADS, S), np.float32)
    for i in range(DK // 2):
        cosT[2 * i] = cosT[2 * i + 1] = c[:, i]
        sinT[2 * i] = -s[:, i]
        sinT[2 * i + 1] = s[:, i]
    return cosT.reshape(128, S), sinT.reshape(128, S)


def by_component(heads):
    return np.arange(heads * DK).reshape(heads, DK).T.reshape(-1)


def kernel(**inputs):
    import ml_dtypes
    import concourse.bacc as bacc
    from concourse.bass_utils import run_bass_kernel_spmd

    g = {k: np.asarray(v) for k, v in inputs.items()}
    order = by_component(HEADS)
    order1 = by_component(KV1)
    swap = order ^ 1
    wq, wk = g["L0_xattn_Wq"], g["L0_xattn_Wk"]
    cosT, sinT = rope_tables()
    cols = np.zeros((128, 4), np.float32)
    cols[:, 0] = g["L1_xattn_bq"][order]
    cols[0:32, 1] = g["L1_xattn_bk"][order1]
    cols[:, 2] = g["L1_xattn_ln_g"]
    cols[:, 3] = g["L1_xattn_ln_b"]
    arrays = {
        "x": g["x"], "ctxT": g["ctx_1024"].reshape(B * S, D).T, "mask": g["mask_BxSxS2_ik1"],
        "W0": np.stack([wq[order].T, wq[swap].T, wk[order].T, wk[swap].T, g["L0_xattn_Wv"].T, g["L0_xattn_Wo"].T]),
        "cosT": cosT, "sinT": sinT, "eye": np.eye(128, dtype=np.float32),
        "eyeb": np.eye(128).astype(ml_dtypes.bfloat16),
        "negI": (np.eye(128) * MASKED).astype(ml_dtypes.bfloat16),
        "upper": np.triu(np.ones((128, 128)), 1).astype(ml_dtypes.bfloat16),
        "W1Q": g["L1_xattn_Wq"][order].T, "W1K": g["L1_xattn_Wk"][order1].T, "W1V": g["L1_xattn_Wv"].T, "W1O": g["L1_xattn_Wo"].T,
        "cols": cols, "bv": g["L1_xattn_bv"], "bo": g["L1_xattn_bo"], "b2": g["L0_ffn_b2"],
        "F1": g["L0_ffn_W1"].T, "F1b": g["L0_ffn_b1"].reshape(FC, 128).T, "F2": g["L0_ffn_W2"].T,
        "WG": g["L1_ffn_wg_red"].T, "wg": g["L1_ffn_wg"],
        "rank": (EXPERTS - np.arange(EXPERTS)).astype(np.float32),
        "M1": g["L1_ffn_w1"], "M1b": g["L1_ffn_b1"].reshape(EXPERTS, FC, 128).transpose(2, 0, 1), "M2": g["L1_ffn_w2"], "M2b": g["L1_ffn_b2"],
    }
    blanks = (DUMMIES + EXPERTS) * 128
    tails = np.zeros((blanks, RW - 2 * D), np.float32)
    tails[:, TOKEN_AT - 2 * D] = (TOKENS + np.arange(blanks, dtype=np.int32)).view(np.float32)
    arrays["tails"] = tails
    arrays["before"] = np.triu(np.ones((128, 128)), 1).astype(ml_dtypes.bfloat16)
    arrays["ones"] = np.ones((ROWS - TERMS, HEADS, PAIR), ml_dtypes.bfloat16)
    arrays["blk"] = np.arange(BLOCKS, dtype=np.float32)
    nc = bacc.Bacc("TRN2", target_bir_lowering=False, num_devices=1)
    feeds, aps = {}, {}
    for name, v in arrays.items():
        v = np.ascontiguousarray(v)
        feeds[f"in_{name}"] = v
        aps[name] = nc.dram_tensor(f"in_{name}", v.shape, mybir.dt.from_np(v.dtype), kind="ExternalInput").ap()
    out = nc.dram_tensor("out_0", (TOKENS + (DUMMIES + EXPERTS) * 128, D), F32, kind="ExternalOutput").ap()
    build(nc, aps, out)
    r = run_bass_kernel_spmd(nc, [feeds], core_ids=[0])
    return r.results[0]["out_0"][0:TOKENS].reshape(B, S, D)
```
